# Optimizing a Trainium2 kernel written in Bass

```python
import numpy as np
import jax
import jax.numpy as jnp

def _softmax(x, axis=-1):
    return jax.nn.softmax(x, axis=axis)

def _gelu(x):
    return jax.nn.gelu(x, approximate=True)

def _silu(x):
    return jax.nn.silu(x)

def _sigmoid(x):
    return jax.nn.sigmoid(x)

def _layernorm(x, axis=-1, eps=1e-05):
    m = jnp.mean(x, axis=axis, keepdims=True)
    v = jnp.var(x, axis=axis, keepdims=True)
    return (x - m) / jnp.sqrt(v + eps)

def _scatter_add(tgt, idx, src, axis=0):
    return tgt.at[idx].add(src)

def _segment_sum(src, seg, n):
    return jax.ops.segment_sum(src, seg, n)
kernel_name = 'mk_vit_tower_d1_tok_img768_r4_67b490'

def setup_inputs(seed: int=0):
    np.random.seed(seed)
    _w = jnp.asarray

    def _rec_inputs():
        import jax
        import jax.numpy as jnp
        _rk = jax.random.key(seed)
        x = -0.000153849 + 1.00027 * jax.random.normal(jax.random.fold_in(_rk, 1), (64, 3, 128, 128), jnp.float32)
        return x
    x = _rec_inputs()

    def _L0_tok_setup():
        import jax, jax.numpy as jnp
        import numpy as np
        EMB = 192
        HEADS = 12
        PATCH = 16
        IN_CH = 3
        key = jax.random.key(seed)
        ks = jax.random.split(key, 11)
        x = jax.random.normal(ks[0], (8, IN_CH, 128, 128), dtype=jnp.float32)
        s_conv = 1.0 / np.sqrt(IN_CH * PATCH * PATCH)
        s_lin = 1.0 / np.sqrt(EMB)
        conv_w = jax.random.uniform(ks[1], (EMB, IN_CH, PATCH, PATCH), jnp.float32, -s_conv, s_conv)
        conv_b = jax.random.uniform(ks[2], (EMB,), jnp.float32, -s_conv, s_conv)
        wq = jax.random.uniform(ks[3], (EMB, EMB), jnp.float32, -s_lin, s_lin)
        bq = jax.random.uniform(ks[4], (EMB,), jnp.float32, -s_lin, s_lin)
        wk = jax.random.uniform(ks[5], (EMB, EMB), jnp.float32, -s_lin, s_lin)
        bk = jax.random.uniform(ks[6], (EMB,), jnp.float32, -s_lin, s_lin)
        wv = jax.random.uniform(ks[7], (EMB, EMB), jnp.float32, -s_lin, s_lin)
        bv = jax.random.uniform(ks[8], (EMB,), jnp.float32, -s_lin, s_lin)
        wo = jax.random.uniform(ks[9], (EMB, EMB), jnp.float32, -s_lin, s_lin)
        bo = jax.random.uniform(ks[10], (EMB,), jnp.float32, -s_lin, s_lin)
        return {'x': x, 'conv_w': conv_w, 'conv_b': conv_b, 'wq': wq, 'bq': bq, 'wk': wk, 'bk': bk, 'wv': wv, 'bv': bv, 'wo': wo, 'bo': bo}
    _L0_tok_all = _L0_tok_setup()
    _L0_tok_in = {k: v for k, v in _L0_tok_all.items() if k in ('conv_w', 'conv_b', 'wq', 'bq', 'wk', 'bk', 'wv', 'bv', 'wo', 'bo')}
    del _L0_tok_all

    def _L0_attn_setup():
        import jax, jax.numpy as jnp
        import numpy as np
        HID, E, S, L_CAP, EPS = (192, 384, 128, 128, 1e-05)

        def _rope_seq(x):
            n, s = (x.shape[1], x.shape[-1])
            half = s // 2
            inv_freq = jnp.power(10000.0, -jnp.arange(half, dtype=x.dtype) / half)
            sinusoid = jnp.arange(n, dtype=x.dtype)[:, None, None] * inv_freq
            sin, cos = (jnp.sin(sinusoid), jnp.cos(sinusoid))
            x1, x2 = jnp.split(x, 2, axis=-1)
            return jnp.concatenate([x1 * cos - x2 * sin, x2 * cos + x1 * sin], axis=-1)
        key = jax.random.key(seed)
        ks = jax.random.split(key, 6)
        B, L = (32, 128)
        return {'x': jax.random.normal(ks[0], (B, L, HID), dtype=jnp.float32), 'ln_gamma': jnp.ones((HID,), jnp.float32), 'ln_beta': jnp.zeros((HID,), jnp.float32), 'uv_W': jax.random.normal(ks[1], (HID, 2 * E + S), jnp.float32) * 0.02, 'uv_b': jnp.zeros((2 * E + S,), jnp.float32), 'gamma_qk': jax.random.normal(ks[2], (2, S), jnp.float32) * 0.02, 'beta_qk': jnp.zeros((2, S), jnp.float32), 'w_rel': jax.random.normal(ks[3], (2 * L_CAP - 1,), jnp.float32) * 0.02, 'o_W': jax.random.normal(ks[4], (E, HID), jnp.float32) * 0.02, 'o_b': jnp.zeros((HID,), jnp.float32)}
    _L0_attn_all = _L0_attn_setup()
    _L0_attn_in = {k: v for k, v in _L0_attn_all.items() if k in ('ln_gamma', 'ln_beta', 'uv_W', 'uv_b', 'gamma_qk', 'beta_qk', 'w_rel', 'o_W', 'o_b')}
    del _L0_attn_all

    def _L0_ffn_setup():
        import jax, jax.numpy as jnp
        import numpy as np
        B, S, D, E, K = (1, 256, 192, 8, 2)
        H = 4 * D
        key = jax.random.key(seed)
        ks = jax.random.split(key, 6)
        s = jnp.float32(0.02)
        return {'x': jax.random.normal(ks[0], (B, S, D), jnp.float32), 'Wr': jax.random.normal(ks[1], (E, D), jnp.float32) * s, 'W1': jax.random.normal(ks[2], (E, H, D), jnp.float32) * s, 'b1': jnp.zeros((E, H), jnp.float32), 'W2': jax.random.normal(ks[3], (E, D, H), jnp.float32) * s, 'b2': jnp.zeros((E, D), jnp.float32), 'sW1': jax.random.normal(ks[4], (H, D), jnp.float32) * s, 'sb1': jnp.zeros((H,), jnp.float32), 'sW2': jax.random.normal(ks[5], (D, H), jnp.float32) * s, 'sb2': jnp.zeros((D,), jnp.float32)}
    _L0_ffn_all = _L0_ffn_setup()
    _L0_ffn_in = {k: v for k, v in _L0_ffn_all.items() if k in ('Wr', 'W1', 'b1', 'W2', 'b2', 'sW1', 'sb1', 'sW2', 'sb2')}
    del _L0_ffn_all
    return {'x': x, 'L0_tok_conv_w': _L0_tok_in['conv_w'], 'L0_tok_conv_b': _L0_tok_in['conv_b'], 'L0_tok_wq': _L0_tok_in['wq'], 'L0_tok_bq': _L0_tok_in['bq'], 'L0_tok_wk': _L0_tok_in['wk'], 'L0_tok_bk': _L0_tok_in['bk'], 'L0_tok_wv': _L0_tok_in['wv'], 'L0_tok_bv': _L0_tok_in['bv'], 'L0_tok_wo': _L0_tok_in['wo'], 'L0_tok_bo': _L0_tok_in['bo'], 'L0_attn_ln_gamma': _L0_attn_in['ln_gamma'], 'L0_attn_ln_beta': _L0_attn_in['ln_beta'], 'L0_attn_uv_W': _L0_attn_in['uv_W'], 'L0_attn_uv_b': _L0_attn_in['uv_b'], 'L0_attn_gamma_qk': _L0_attn_in['gamma_qk'], 'L0_attn_beta_qk': _L0_attn_in['beta_qk'], 'L0_attn_w_rel': _L0_attn_in['w_rel'], 'L0_attn_o_W': _L0_attn_in['o_W'], 'L0_attn_o_b': _L0_attn_in['o_b'], 'L0_ffn_Wr': _L0_ffn_in['Wr'], 'L0_ffn_W1': _L0_ffn_in['W1'], 'L0_ffn_b1': _L0_ffn_in['b1'], 'L0_ffn_W2': _L0_ffn_in['W2'], 'L0_ffn_b2': _L0_ffn_in['b2'], 'L0_ffn_sW1': _L0_ffn_in['sW1'], 'L0_ffn_sb1': _L0_ffn_in['sb1'], 'L0_ffn_sW2': _L0_ffn_in['sW2'], 'L0_ffn_sb2': _L0_ffn_in['sb2']}

def reference(x, L0_tok_conv_w, L0_tok_conv_b, L0_tok_wq, L0_tok_bq, L0_tok_wk, L0_tok_bk, L0_tok_wv, L0_tok_bv, L0_tok_wo, L0_tok_bo, L0_attn_ln_gamma, L0_attn_ln_beta, L0_attn_uv_W, L0_attn_uv_b, L0_attn_gamma_qk, L0_attn_beta_qk, L0_attn_w_rel, L0_attn_o_W, L0_attn_o_b, L0_ffn_Wr, L0_ffn_W1, L0_ffn_b1, L0_ffn_W2, L0_ffn_b2, L0_ffn_sW1, L0_ffn_sb1, L0_ffn_sW2, L0_ffn_sb2):
    import jax
    import jax.numpy as jnp

    def _L0_tok_ref(x, conv_w, conv_b, wq, bq, wk, bk, wv, bv, wo, bo):
        import jax, jax.numpy as jnp
        import numpy as np
        EMB = 192
        HEADS = 12
        PATCH = 16
        IN_CH = 3
        t = jax.lax.conv_general_dilated(x, conv_w, window_strides=(PATCH, PATCH), padding='VALID', dimension_numbers=('NCHW', 'OIHW', 'NCHW')) + conv_b[None, :, None, None]
        B, C, Hp, Wp = t.shape
        N = Hp * Wp
        t = t.reshape(B, C, N).transpose(0, 2, 1)
        D = C // HEADS
        scale = D ** (-0.5)
        q = (t @ wq.T + bq).reshape(B, N, HEADS, D).transpose(0, 2, 1, 3)
        k = (t @ wk.T + bk).reshape(B, N, HEADS, D).transpose(0, 2, 1, 3)
        v = (t @ wv.T + bv).reshape(B, N, HEADS, D).transpose(0, 2, 1, 3)
        attn = jax.nn.softmax(jnp.einsum('bhnd,bhmd->bhnm', q, k) * scale, axis=-1)
        out = jnp.einsum('bhnm,bhmd->bhnd', attn, v)
        out = out.transpose(0, 2, 1, 3).reshape(B, N, C)
        out = out @ wo.T + bo
        return out

    def _L0_attn_ref(x, ln_gamma, ln_beta, uv_W, uv_b, gamma_qk, beta_qk, w_rel, o_W, o_b):
        import jax, jax.numpy as jnp
        import numpy as np
        HID, E, S, L_CAP, EPS = (192, 384, 128, 128, 1e-05)

        def _rope_seq(x):
            n, s = (x.shape[1], x.shape[-1])
            half = s // 2
            inv_freq = jnp.power(10000.0, -jnp.arange(half, dtype=x.dtype) / half)
            sinusoid = jnp.arange(n, dtype=x.dtype)[:, None, None] * inv_freq
            sin, cos = (jnp.sin(sinusoid), jnp.cos(sinusoid))
            x1, x2 = jnp.split(x, 2, axis=-1)
            return jnp.concatenate([x1 * cos - x2 * sin, x2 * cos + x1 * sin], axis=-1)
        L = x.shape[1]
        shortcut = x
        mu = jnp.mean(x, axis=-1, keepdims=True)
        var = jnp.mean(jnp.square(x - mu), axis=-1, keepdims=True)
        xn = (x - mu) * jax.lax.rsqrt(var + EPS) * ln_gamma + ln_beta
        uv = jax.nn.silu(xn @ uv_W + uv_b)
        u, v, base = jnp.split(uv, [E, 2 * E], axis=-1)
        base = base[..., None, :] * gamma_qk + beta_qk
        base = _rope_seq(base)
        q, k = (base[..., 0, :], base[..., 1, :])
        qk = jnp.einsum('bnd,bmd->bnm', q, k)
        idx = jnp.arange(L)
        bias = w_rel[idx[None, :] - idx[:, None] + L - 1]
        kernel = jnp.square(jax.nn.relu(qk / L + bias))
        out = u * jnp.einsum('bnm,bme->bne', kernel, v)
        out = out @ o_W + o_b
        return out + shortcut

    def _L0_ffn_ref(x, Wr, W1, b1, W2, b2, sW1, sb1, sW2, sb2):
        import jax, jax.numpy as jnp
        import numpy as np
        B, S, D, E, K = (1, 256, 192, 8, 2)
        H = 4 * D
        Bx, Sx, Dx = x.shape
        xf = x.reshape(-1, Dx)
        T = xf.shape[0]
        logits = xf @ Wr.T
        topv, idx = jax.lax.top_k(logits, K)
        gate_k = jax.nn.softmax(topv, axis=-1)
        gates = jnp.zeros((T, logits.shape[-1]), x.dtype).at[jnp.arange(T)[:, None], idx].add(gate_k)
        h = jax.nn.relu(jnp.einsum('td,ehd->teh', xf, W1) + b1)
        y = jnp.einsum('teh,edh->ted', h, W2) + b2
        moe = jnp.einsum('te,ted->td', gates, y)
        sh = jax.nn.relu(xf @ sW1.T + sb1) @ sW2.T + sb2
        out = moe + 0.1 * K * sh
        return out.reshape(Bx, Sx, Dx)
    h = _L0_tok_ref(x, L0_tok_conv_w, L0_tok_conv_b, L0_tok_wq, L0_tok_bq, L0_tok_wk, L0_tok_bk, L0_tok_wv, L0_tok_bv, L0_tok_wo, L0_tok_bo)
    h = h + _L0_attn_ref(_layernorm(h, axis=-1), L0_attn_ln_gamma, L0_attn_ln_beta, L0_attn_uv_W, L0_attn_uv_b, L0_attn_gamma_qk, L0_attn_beta_qk, L0_attn_w_rel, L0_attn_o_W, L0_attn_o_b)
    h = h + _L0_ffn_ref(_layernorm(h, axis=-1), L0_ffn_Wr, L0_ffn_W1, L0_ffn_b1, L0_ffn_W2, L0_ffn_b2, L0_ffn_sW1, L0_ffn_sb1, L0_ffn_sW2, L0_ffn_sb2)
    return h

_drawn_inputs = setup_inputs


def setup_inputs(seed=0):
    import zlib

    import numpy as np

    out = dict(_drawn_inputs(seed))
    spreads = {'L0_attn_ln_gamma': (1.0, 0.6),
     'L0_attn_ln_beta': (0.0, 0.8),
     'L0_attn_uv_b': (0.0, 0.8),
     'L0_attn_beta_qk': (0.0, 0.8),
     'L0_attn_o_b': (0.0, 0.8),
     'L0_ffn_b1': (0.0, 2.0),
     'L0_ffn_b2': (0.0, 0.8),
     'L0_ffn_sb1': (0.0, 2.0),
     'L0_ffn_sb2': (0.0, 2.0)}
    factors = {'L0_tok_bq': 6.261,
     'L0_tok_bk': 64.0,
     'L0_attn_uv_W': 8.0,
     'L0_attn_gamma_qk': 8.0,
     'L0_attn_w_rel': 8.0,
     'L0_attn_o_W': 8.0,
     'L0_ffn_sW1': 27.112,
     'L0_ffn_Wr': 6.321,
     'L0_ffn_W1': 8.0,
     'L0_ffn_W2': 6.506,
     'L0_ffn_sW2': 6.271}
    for name, (base, spread) in spreads.items():
        noise = np.random.default_rng([zlib.crc32(name.encode()), seed]).standard_normal(out[name].shape)
        drawn = base * np.exp(spread * noise) if base else spread * noise
        out[name] = jnp.asarray(drawn.astype(out[name].dtype))
    for name, factor in factors.items():
        out[name] = (out[name] * factor).astype(out[name].dtype)
    return out
```

```python
from contextlib import ExitStack

import concourse.bass as bass
from concourse import mybir

F32 = mybir.dt.float32
I32 = mybir.dt.int32
U32 = mybir.dt.uint32
ALU = mybir.AluOpType
ACT = mybir.ActivationFunctionType
AX = mybir.AxisListType

P = 128
B, CH, IMG, PATCH = 64, 3, 128, 16
EMB, HEADS = 192, 12
L = (IMG // PATCH) ** 2
T = B * L
HD = EMB // HEADS
PAIRS = HEADS // 2
GT = 512
G = T // GT
SUB = GT // P
NT = T // P
KP = CH * PATCH * PATCH // P
HC = EMB // 2
E_GAU, S_GAU = 384, 128
EC = E_GAU // P
NE, TOPK = 8, 2
HID = 4 * EMB
HK = HID // P
SLOTS = (T * TOPK) // P + NE - 1
ROW = EMB + 2
VH = HD + 1
EPS = 1e-5
WUV = 2 * E_GAU + 2 * S_GAU


def declare(nc):
    shapes = dict(
        patches=[G, P, KP, GT], w_conv=[P, KP, EMB], b_conv=[HC, 2], w_qkv=[HC + 1, 2, 3 * EMB],
        head_mask=[P, 2], w_o=[HC + 1, 2, EMB], w_uv=[HC + 1, 2, WUV], ln_gamma=[HC, 2], ln_beta=[HC, 2],
        qk_gain=[P, 2, 2], qk_shift=[P, 2, 2], rope=[P, 2, L], rel_bias=[P, P], w_gau=[P, EC, EMB],
        b_gau=[1, EMB], w_route=[HC, 2, NE], w1=[HC + 1, NE, 2, HID], w2=[P, NE, HK, EMB], b2=[1, NE * EMB],
        ws1=[HC + 1, 2, HID], ws2=[P, HK, EMB], bs2=[1, EMB], consts=[P, 2 * P + NE + SLOTS],
    )
    d = {k: nc.dram_tensor(k, s, F32, kind="ExternalInput").ap() for k, s in shapes.items()}
    d["pad_rows"] = nc.dram_tensor("pad_rows", [P, ROW], F32, kind="ExternalInput").ap()
    d["token_ids"] = nc.dram_tensor("token_ids", [P, NT], F32, kind="ExternalInput").ap()
    d["out"] = nc.dram_tensor("out", [T + P, EMB], F32, kind="ExternalOutput").ap()
    d["x3t"] = nc.dram_tensor("x3t", [G, HC, 2, GT], F32, kind="Internal").ap()
    d["slot_rows"] = nc.dram_tensor("slot_rows", [(SLOTS + 1) * P, ROW], F32, kind="Internal").ap()
    return d


def least(eng, sem, n):
    if not isinstance(n, int) or n > 0:
        eng.wait_ge(sem, n)


def apart(eng, passed):
    eng.sem_inc(passed, 1)


def build_program(nc, d):
    with ExitStack() as whole:
        def keep(name, shape, dt=F32):
            return whole.enter_context(nc.sbuf_tensor(name, shape, dt))

        psum = whole.enter_context(nc.psum_tensor("psum", [P, 8, 512], F32))
        h2_all = keep("h2_all", [P, NT, EMB])
        x3_all = keep("x3_all", [P, NT, ROW])
        top_all = keep("top_all", [P, NT, TOPK])
        idx_all = keep("idx_all", [P, NT, TOPK])
        consts = keep("consts_sb", [P, 2 * P + NE + SLOTS])
        ident = consts[:, 0:P]
        with ExitStack() as scope:
            front_and_back(nc, d, scope, psum, h2_all, x3_all, top_all, idx_all, consts, ident)
        with ExitStack() as scope:
            experts(nc, d, scope, psum, h2_all, x3_all, top_all, idx_all, consts, ident)


def front_and_back(nc, d, scope, psum, h2_all, x3_all, top_all, idx_all, consts, ident):
    def sb(name, shape, dt=F32):
        return scope.enter_context(nc.sbuf_tensor(name, shape, dt))

    def sem(name):
        return scope.enter_context(nc.semaphore(name))

    w_conv = sb("w_conv_sb", [P, KP, EMB])
    b_conv = sb("b_conv_sb", [HC, 2])
    w_qkv = sb("w_qkv_sb", [HC + 1, 2, 3 * EMB])
    head_mask = sb("head_mask_sb", [P, 2])
    w_o = sb("w_o_sb", [HC + 1, 2, EMB])
    w_uv = sb("w_uv_sb", [HC + 1, 2, WUV])
    gamma = sb("gamma_sb", [HC, 2])
    beta = sb("beta_sb", [HC, 2])
    qk_gain = sb("qk_gain_sb", [P, 2, 2])
    qk_shift = sb("qk_shift_sb", [P, 2, 2])
    rope = sb("rope_sb", [P, 2, L])
    rel_bias = sb("rel_bias_sb", [P, P])
    w_gau = sb("w_gau_sb", [P, EC, EMB])
    b_gau = sb("b_gau_sb", [P, EMB])
    w_route = sb("w_route_sb", [HC, 2, NE])
    rope_tab = sb("rope_tab", [P, 3, 2, L])
    minus_half = sb("minus_half", [P, SUB])
    eps = sb("eps", [P, SUB])
    one = sb("one", [P, SUB])
    minus_one = sb("minus_one", [P, SUB])
    patches = sb("patches_sb", [P, KP, GT])
    tok_t = sb("tok_t", [HC + 1, 2, GT])
    q_a = sb("q_a", [P, GT // L, 2, L])
    q_b = sb("q_b", [P, GT // L, 2, L])
    k_a = sb("k_a", [P, 4, GT])
    k_b = sb("k_b", [P, 2, GT])
    v_ones = sb("v_ones", [P, SUB, PAIRS, 2, 2 * VH])
    row_max = sb("row_max", [P, 2, 2, PAIRS])
    probs = sb("probs", [P, 2, PAIRS, 2, L])
    probs_t = sb("probs_t", [P, 2, PAIRS, P])
    inv_sum = sb("inv_sum", [P, 2, PAIRS, 2])
    att = sb("att", [P, 2, 2, PAIRS, HD])
    att_t = sb("att_t", [HC + 1, 2, 2, P])
    h1 = sb("h1", [P, SUB, EMB])
    stats1 = sb("stats1", [P, SUB, 6])
    mean_var1 = sb("mean_var1", [P, SUB, 2])
    coef = sb("coef", [P, 8, SUB])
    h1_plus = sb("h1_plus", [P, SUB, EMB])
    xn = sb("xn", [P, SUB, EMB])
    xn_t = sb("xn_t", [HC + 1, 2, GT])
    tanh = sb("tanh", [P, 3, 512])
    u_t = sb("u_t", [P, EC, GT])
    base = sb("base", [P, 2, GT])
    rope_1 = sb("rope_1", [P, 2, GT])
    rope_2 = sb("rope_2", [P, 2, GT])
    qk_t = sb("qk_t", [P, 2, GT])
    v_nat = sb("v_nat", [P, SUB, E_GAU])
    biased = sb("biased", [P, SUB, P])
    kern = sb("kern", [P, SUB, P])
    gated = sb("gated", [P, EC, GT])
    h2 = sb("h2", [P, SUB, EMB])
    stats2 = sb("stats2", [P, SUB, 6])
    mean_var2 = sb("mean_var2", [P, SUB, 2])
    coef2 = sb("coef2", [P, 2, SUB])
    x3 = sb("x3", [P, SUB, EMB])
    x3_t = sb("x3_t", [HC, 2, GT])
    logits = sb("logits", [P, SUB, NE])
    best = sb("best", [P, SUB, 8])
    best_at = sb("best_at", [P, SUB, 8], U32)

    weights_in = sem("weights_in")
    patches_in = sem("patches_in")
    pads_in = sem("pads_in")
    conv_done, qk_done, v_done = sem("conv_done"), sem("qk_done"), sem("v_done")
    scores_done, probs_turned, pv_done = sem("scores_done"), sem("probs_turned"), sem("pv_done")
    att_turned, proj_done = sem("att_turned"), sem("proj_done")
    xn_turned, uv_done, gqk_done, kv_done = sem("xn_turned"), sem("uv_done"), sem("gqk_done"), sem("kv_done")
    gau_done, x3_turned, route_done, fold_done = sem("gau_done"), sem("x3_turned"), sem("route_done"), sem("fold_done")
    const_ready, fold_ready = sem("const_ready"), sem("fold_ready")
    tok_ready = sem("tok_ready")
    qk_by_act, qk_by_dve = sem("qk_by_act"), sem("qk_by_dve")
    v_by_act, v_by_dve = sem("v_by_act"), sem("v_by_dve")
    max_ready, shifted, exp_done = sem("max_ready"), sem("shifted"), sem("exp_done")
    probs_t_act, probs_t_dve = sem("probs_t_act"), sem("probs_t_dve")
    inv_ready, att_ready, att_t_ready, h1_ready = sem("inv_ready"), sem("att_ready"), sem("att_t_ready"), sem("h1_ready")
    stat_step, var1_ready, coef_step, coef1_ready = sem("stat_step"), sem("var1_ready"), sem("coef_step"), sem("coef1_ready")
    xn_ready, h1_plus_act, h1_plus_ready = sem("xn_ready"), sem("h1_plus_act"), sem("h1_plus_ready")
    xn_t_ready, tanh_ready, silu_ready = sem("xn_t_ready"), sem("tanh_ready"), sem("silu_ready")
    rope_1_ready, rope_2_half, rope_2_ready, rope_ready = sem("rope_1_ready"), sem("rope_2_half"), sem("rope_2_ready"), sem("rope_ready")
    biased_ready, kern_ready, gated_ready = sem("biased_ready"), sem("kern_ready"), sem("gated_ready")
    h2_ready, var2_ready, coef2_ready, x3_ready, x3_t_ready = sem("h2_ready"), sem("var2_ready"), sem("coef2_ready"), sem("x3_ready"), sem("x3_t_ready")
    logits_read, best_step, routed = sem("logits_read"), sem("best_step"), sem("routed")
    dve_passed = sem("dve_passed")
    h2_kept, x3_kept, x3_t_kept = sem("h2_kept"), sem("x3_kept"), sem("x3_t_kept")

    weights = [
        (w_conv, d["w_conv"]), (b_conv, d["b_conv"]), (w_qkv, d["w_qkv"]), (head_mask, d["head_mask"]),
        (w_o, d["w_o"]), (w_uv, d["w_uv"]), (gamma, d["ln_gamma"]), (beta, d["ln_beta"]),
        (qk_gain, d["qk_gain"]), (qk_shift, d["qk_shift"]), (rope, d["rope"]), (rel_bias, d["rel_bias"]),
        (w_gau, d["w_gau"]), (w_route, d["w_route"]), (consts, d["consts"]),
    ]
    N_WEIGHTS = len(weights) + 1
    ALL_WEIGHTS = 16 * N_WEIGHTS
    N_FOLDS = 13
    N_CONST = 13

    def peeled(eng, first, both, last):
        first(0)
        with eng.Fori(1, G - 1) as g:
            both(g, True)
        both(G - 1, False)
        last(G - 1)

    def images(t):
        return t.rearrange("p (i n) -> p i n", n=L)

    def by_image(t):
        return t[:].rearrange("p q (i n) -> p q i n", n=L)

    def of_base(t):
        return t.rearrange("p (i n) -> p i n", n=L).unsqueeze(1).broadcast_to([P, 2, GT // L, L])

    def table(i):
        return rope_tab[:, i, :, :].unsqueeze(2).broadcast_to([P, 2, GT // L, L])

    def v_dest(half, i):
        t = v_ones[64 * i:64 * i + 64, 2 * half:2 * half + 2, :, i, :]
        return t.rearrange("p s a (h e) -> p (s a) h e", e=VH)[:, :, :, 0:HD]

    def v_src(half, i):
        t = psum[64 * i:64 * i + 64, half, 0:2 * EMB]
        return t.rearrange("p (a h e) -> p a h e", h=2, e=HD)

    def score_banks(s):
        return 2 * (s % 2)

    block = scope.enter_context(nc.Block())

    @block.sync
    def _(sp):
        sp.dma_start(patches[:], d["patches"][0]).then_inc(patches_in, 16)
        for tile, src in weights:
            sp.dma_start(tile[:], src).then_inc(weights_in, 16)
        sp.dma_start(b_gau[:], d["b_gau"].broadcast_to([P, EMB])).then_inc(weights_in, 16)
        sp.dma_start(d["slot_rows"].rearrange("(s p) w -> s p w", p=P),
                     d["pad_rows"].unsqueeze(0).broadcast_to([SLOTS + 1, P, ROW])).then_inc(pads_in, 16)
        sp.dma_start(x3_all[:, :, EMB + 1:EMB + 2], d["token_ids"].unsqueeze(2),
                     allow_slow_non_contiguous=True).then_inc(pads_in, 16)

        def load_patches(g):
            sp.wait_ge(conv_done, 2 * g)
            sp.dma_start(patches[:], d["patches"][bass.ds(g, 1)].rearrange("a p c t -> p (a c) t")).then_inc(patches_in, 16)

        def store(g):
            sp.wait_ge(h2_ready, 2 * g + 2)
            sp.dma_start(h2_all[:, bass.ds(SUB * g, SUB), :], h2[:]).then_inc(h2_kept, 16)
            sp.wait_ge(x3_ready, SUB * g + SUB)
            sp.dma_start(x3_all[:, bass.ds(SUB * g, SUB), 0:EMB], x3[:]).then_inc(x3_kept, 16)
            sp.wait_ge(x3_t_ready, 2 * g + 2)
            sp.dma_start(d["x3t"][bass.ds(g, 1)].rearrange("a p c t -> p (a c) t"), x3_t[:]).then_inc(x3_t_kept, 16)

        def both(g, more):
            if more:
                load_patches(g + 1)
            store(g - 1)

        peeled(sp, lambda g: load_patches(1), both, store)
        sp.wait_ge(pads_in, 32)
        sp.wait_ge(h2_kept, 16 * G)
        sp.wait_ge(x3_kept, 16 * G)
        sp.wait_ge(x3_t_kept, 16 * G)

    @block.gpsimd
    def _(pool):
        cleared = [q_b[:], k_a[:], k_b[:], v_ones[:]]
        ones = [tok_t[HC:HC + 1, 0, :], xn_t[HC:HC + 1, 0, :], att_t[HC:HC + 1, :, 0, :]]
        ones += [v_ones[64 * i:64 * i + 64, :, :, i, HD::VH] for i in range(2)]
        for n, tile in enumerate(cleared + ones):
            pool.memset(tile, 0.0 if n < len(cleared) else 1.0).then_inc(const_ready, 1)
            pool.wait_ge(const_ready, n + 1)
        for n, (tile, value) in enumerate(((minus_half, -0.5), (eps, EPS), (one, 1.0), (minus_one, -1.0))):
            pool.memset(tile[:], value).then_inc(const_ready, 1)
            pool.wait_ge(const_ready, len(cleared + ones) + n + 1)

        def coef1(g):
            pool.wait_ge(var1_ready, g + 1)
            if not isinstance(g, int) or g > 0:
                pool.wait_ge(xn_ready, SUB * g)
                pool.wait_ge(h1_plus_act, SUB * g)
            n = 7 * g

            def step(ins):
                nonlocal n
                n = n + 1
                ins.then_inc(coef_step, 1)
                pool.wait_ge(coef_step, n)

            mean, var = mean_var1[:, :, 0], mean_var1[:, :, 1]
            step(pool.tensor_tensor(coef[:, 1, :], coef[:, 0, :], minus_half[:], ALU.pow))
            step(pool.tensor_tensor(coef[:, 2, :], coef[:, 1, :], coef[:, 1, :], ALU.mult))
            step(pool.tensor_tensor(coef[:, 2, :], coef[:, 2, :], var, ALU.mult))
            step(pool.tensor_tensor(coef[:, 2, :], coef[:, 2, :], eps[:], ALU.add))
            step(pool.tensor_tensor(coef[:, 3, :], coef[:, 2, :], minus_half[:], ALU.pow))
            step(pool.tensor_tensor(coef[:, 4, :], mean, coef[:, 1, :], ALU.mult))
            step(pool.tensor_tensor(coef[:, 5, :], coef[:, 4, :], minus_one[:], ALU.mult))
            pool.tensor_tensor(coef[:, 6, :], coef[:, 1, :], one[:], ALU.add).then_inc(coef1_ready, 1)
            pool.tensor_tensor(coef[:, 7, :], coef[:, 1, :], coef[:, 3, :], ALU.mult).then_inc(coef1_ready, 1)

        def add_b_gau(g):
            pool.wait_ge(h1_plus_act, SUB * g + SUB)
            pool.tensor_tensor(h1_plus[:], h1_plus[:], b_gau[:].unsqueeze(1).broadcast_to([P, SUB, EMB]), ALU.add)\
                .then_inc(h1_plus_ready, 1)

        def rope_second(g):
            pool.wait_ge(silu_ready, 9 * g + 2)
            least(pool, rope_ready, g)
            pool.tensor_tensor(by_image(rope_2), of_base(base[:, 1, :]), table(1), ALU.mult).then_inc(rope_2_half, 1)
            pool.wait_ge(rope_2_half, g + 1)
            pool.tensor_tensor(by_image(rope_2), by_image(rope_2), table(2), ALU.add).then_inc(rope_2_ready, 1)

        def coef2_of(g):
            pool.wait_ge(var2_ready, g + 1)
            least(pool, x3_ready, SUB * g)
            pool.tensor_tensor(coef2[:, 1, :], coef2[:, 0, :], minus_half[:], ALU.pow).then_inc(coef2_ready, 1)

        def front(g):
            coef1(g)
            add_b_gau(g)

        def both(g, more):
            rope_second(g - 1)
            coef1(g)
            coef2_of(g - 1)
            add_b_gau(g)

        def back(g):
            rope_second(g)
            coef2_of(g)

        pool.wait_ge(weights_in, ALL_WEIGHTS)
        pool.wait_ge(fold_ready, N_FOLDS)
        peeled(pool, front, both, back)

    @block.scalar
    def _(act):
        def conv_out(g, j):
            act.wait_ge(conv_done, 2 * g + j + 1)
            least(act, v_done, 2 * g)
            act.activation(tok_t[0:HC, j, :], psum[0:HC, j, :], ACT.Identity, bias=b_conv[:, j:j + 1]).then_inc(tok_ready, 1)

        def qk_out(g):
            least(act, scores_done, SUB * g)
            act.wait_ge(qk_done, 3 * g + 1)
            for h in range(2):
                act.activation(q_a[:, :, h, :], images(psum[:, 2, :]), ACT.Copy, scale=head_mask[:, h:h + 1]).then_inc(qk_by_act, 1)
            act.wait_ge(qk_done, 3 * g + 2)
            for a in range(2):
                act.activation(k_b[32 * a:32 * a + 32, a, :], psum[64 + 32 * a:96 + 32 * a, 3, :], ACT.Copy).then_inc(qk_by_act, 1)
            act.wait_ge(qk_done, 3 * g + 3)
            act.activation(k_a[0:32, 0, :], psum[0:32, 4, :], ACT.Copy).then_inc(qk_by_act, 1)

        def v_out(g):
            least(act, pv_done, SUB * g)
            for half in range(2):
                act.wait_ge(v_done, 2 * g + half + 1)
                act.activation(v_dest(half, 0), v_src(half, 0), ACT.Copy).then_inc(v_by_act, 1)

        def exp(g, s):
            act.wait_ge(shifted, SUB * g + s + 1)
            x = probs[:, s % 2, :, :, :]
            act.activation(x, x, ACT.Exp).then_inc(exp_done, 1)

        def probs_t_out(g, s):
            act.wait_ge(probs_turned, SUB * g + s + 1)
            least(act, pv_done, SUB * g + s - 1)
            act.activation(probs_t[:, s % 2, 0:3, :], psum[:, score_banks(s), 0:384], ACT.Copy).then_inc(probs_t_act, 1)

        def att_t_out(g, s):
            act.wait_ge(att_turned, SUB * g + s + 1)
            least(act, proj_done, SUB * g + s - 1)
            act.activation(att_t[0:HC, s % 2, :, :].rearrange("p h (i q) -> p i h q", i=2),
                           psum[0:HC, 5, 0:2 * P].rearrange("p (i h q) -> p i h q", i=2, h=2), ACT.Copy)\
               .then_inc(att_t_ready, 1)

        def h1_out(g, s):
            act.wait_ge(proj_done, SUB * g + s + 1)
            least(act, xn_ready, SUB * g)
            least(act, h1_plus_act, SUB * g)
            act.activation(h1[:, s, :], psum[:, 5, 2 * P:2 * P + EMB], ACT.Copy).then_inc(h1_ready, 1)

        def residual(g):
            act.wait_ge(coef1_ready, 2 * g + 2)
            least(act, h2_ready, 2 * g)
            for s in range(SUB):
                act.activation(h1_plus[:, s, :], h1[:, s, :], ACT.Identity, scale=coef[:, 6, s:s + 1],
                               bias=coef[:, 5, s:s + 1]).then_inc(h1_plus_act, 1)

        def xn_t_out(g, j):
            act.wait_ge(xn_turned, 2 * g + j + 1)
            least(act, uv_done, 9 * g)
            act.activation(xn_t[0:HC, j, :], psum[0:HC, 6 + j, :], ACT.Copy).then_inc(xn_t_ready, 1)

        def tanh_of(g, k):
            bank, cols = (6 + k % 2, 512) if k < 5 else (6 + k % 2, E_GAU)
            act.wait_ge(uv_done, 9 * g + k + 1)
            if k >= 3:
                act.wait_ge(silu_ready, 9 * g + k - 2)
            act.activation(tanh[:, k % 3, 0:cols], psum[:, bank, 0:cols], ACT.Tanh, scale=0.5).then_inc(tanh_ready, 1)

        def x3_t_out(g, j):
            act.wait_ge(x3_turned, 2 * g + j + 1)
            least(act, route_done, g)
            least(act, x3_t_kept, 16 * g)
            act.activation(x3_t[:, j, :], psum[0:HC, 7 - j, :], ACT.Copy).then_inc(x3_t_ready, 1)

        def front(g):
            qk_out(g)
            v_out(g)
            exp(g, 0)
            exp(g, 1)
            probs_t_out(g, 0)
            probs_t_out(g, 1)
            exp(g, 2)
            att_t_out(g, 0)
            h1_out(g, 0)
            exp(g, 3)
            att_t_out(g, 1)
            probs_t_out(g, 2)
            h1_out(g, 1)
            probs_t_out(g, 3)
            att_t_out(g, 2)
            conv_out(g + 1, 0)
            h1_out(g, 2)
            att_t_out(g, 3)
            conv_out(g + 1, 1)
            h1_out(g, 3)
            residual(g)

        def both(g, more):
            b = g - 1
            qk_out(g)
            xn_t_out(b, 0)
            xn_t_out(b, 1)
            v_out(g)
            tanh_of(b, 0)
            tanh_of(b, 1)
            exp(g, 0)
            tanh_of(b, 2)
            exp(g, 1)
            tanh_of(b, 3)
            probs_t_out(g, 0)
            probs_t_out(g, 1)
            tanh_of(b, 4)
            exp(g, 2)
            att_t_out(g, 0)
            tanh_of(b, 5)
            h1_out(g, 0)
            exp(g, 3)
            att_t_out(g, 1)
            tanh_of(b, 6)
            h1_out(g, 1)
            probs_t_out(g, 2)
            tanh_of(b, 7)
            probs_t_out(g, 3)
            tanh_of(b, 8)
            att_t_out(g, 2)
            h1_out(g, 2)
            att_t_out(g, 3)
            h1_out(g, 3)
            if more:
                conv_out(g + 1, 0)
            residual(g)
            if more:
                conv_out(g + 1, 1)
            x3_t_out(b, 0)
            x3_t_out(b, 1)

        def back(g):
            xn_t_out(g, 0)
            xn_t_out(g, 1)
            for k in range(9):
                tanh_of(g, k)
            x3_t_out(g, 0)
            x3_t_out(g, 1)

        act.wait_ge(weights_in, ALL_WEIGHTS)
        act.wait_ge(const_ready, N_CONST)
        conv_out(0, 0)
        conv_out(0, 1)
        peeled(act, front, both, back)

    @block.tensor
    def _(pe):
        def mm(out, lhs, rhs, start, stop):
            return pe.matmul(out, lhs, rhs, start=start, stop=stop)

        def conv(g, j):
            pe.wait_ge(patches_in, 16 * (g + 1))
            least(pe, probs_t_act, SUB * g - 1)
            least(pe, probs_t_dve, SUB * g - 1)
            for c in range(KP):
                m = mm(psum[0:HC, j, :], w_conv[:, c, HC * j:HC * j + HC], patches[:, c, :], c == 0, c == KP - 1)
            m.then_inc(conv_done, 1)

        def two(out, lhs, rhs):
            mm(out, lhs(HC + 1, 0), rhs(HC + 1, 0), True, False)
            return mm(out, lhs(HC, 1), rhs(HC, 1), False, True)

        def qk(g, m):
            pe.wait_ge(tok_ready, 2 * g + 2)
            if m < 2:
                least(pe, probs_t_act, SUB * g)
                least(pe, probs_t_dve, SUB * g)
            else:
                least(pe, att_ready, 2 * SUB * g)
            two(psum[:, 2 + m, :], lambda k, j: w_qkv[0:k, j, P * m:P * m + P],
                lambda k, j: tok_t[0:k, j, :]).then_inc(qk_done, 1)

        def v(g, half):
            for s in range(2):
                m = two(psum[:, half, EMB * s:EMB * s + EMB],
                        lambda k, j: tok_t[0:k, j, P * (2 * half + s):P * (2 * half + s) + P],
                        lambda k, j: w_qkv[0:k, j, 2 * EMB:3 * EMB])
            m.then_inc(v_done, 1)

        def scores(g, s):
            pe.wait_ge(qk_by_act, 5 * g + 5)
            pe.wait_ge(qk_by_dve, 5 * g + 5)
            if s == 0:
                pe.wait_ge(v_by_act, 2 * g + 2)
                pe.wait_ge(v_by_dve, 2 * g + 2)
            if s >= 2:
                pe.wait_ge(probs_t_act, SUB * g + s - 1)
                pe.wait_ge(probs_t_dve, SUB * g + s - 1)
            for i in range(2):
                t = slice(P * s + L * i, P * s + L * i + L)
                out = psum[:, score_banks(s) + i, :]
                mm(out[:, 0:4 * L], q_a[:, 2 * s + i].rearrange("p h q -> p (h q)"), k_a[:, :, t], True, True)
                m = mm(out[:, 4 * L:6 * L], q_b[:, 2 * s + i].rearrange("p h q -> p (h q)"), k_b[:, :, t], True, True)
            m.then_inc(scores_done, 1)

        def turn_probs(g, s):
            pe.wait_ge(exp_done, SUB * g + s + 1)
            for a in range(PAIRS):
                out = psum[:, score_banks(s) + a // 3, P * (a % 3):P * (a % 3) + P]
                m = pe.transpose(out, probs[:, s % 2, a].rearrange("p i k -> p (i k)"), ident)
            m.then_inc(probs_turned, 1)

        def pv(g, s):
            pe.wait_ge(probs_t_act, SUB * g + s + 1)
            pe.wait_ge(probs_t_dve, SUB * g + s + 1)
            if s > 0:
                pe.wait_ge(att_ready, 2 * (SUB * g + s))
            for a in range(PAIRS):
                m = mm(psum[:, 4, 4 * VH * a:4 * VH * a + 4 * VH], probs_t[:, s % 2, a, :],
                       v_ones[:, s, a, :, :].rearrange("p i e -> p (i e)"), True, True)
            m.then_inc(pv_done, 1)

        def turn_att(g, s):
            pe.wait_ge(att_ready, 2 * (SUB * g + s + 1))
            least(pe, h1_ready, SUB * g + s)
            for i in range(2):
                m = pe.transpose(psum[0:HC, 5, P * i:P * i + P], att[:, s % 2, i, :, :].rearrange("p a e -> p (a e)"), ident)
            m.then_inc(att_turned, 1)

        def proj(g, s):
            pe.wait_ge(att_t_ready, SUB * g + s + 1)
            two(psum[:, 5, 2 * P:2 * P + EMB], lambda k, j: att_t[0:k, s % 2, j, :], lambda k, j: w_o[0:k, j, :]).then_inc(proj_done, 1)

        def turn_xn(g, j):
            pe.wait_ge(xn_ready, SUB * g + SUB)
            if j == 0:
                least(pe, x3_t_ready, 2 * g)
            else:
                least(pe, logits_read, g)
            for s in range(SUB):
                m = pe.transpose(psum[0:HC, 6 + j, P * s:P * s + P], xn[:, s, HC * j:HC * j + HC], ident)
            m.then_inc(xn_turned, 1)

        def uv(g, k):
            pe.wait_ge(xn_t_ready, 2 * g + 2)
            if k == 7:
                pe.wait_ge(biased_ready, g + 1)
            elif k >= 2:
                pe.wait_ge(silu_ready, 9 * g + k - 1)
            if k < 5:
                col = 2 * E_GAU + P * k if k < 2 else P * (k - 2)
                m = two(psum[:, 6 + k % 2, :], lambda r, j: w_uv[0:r, j, col:col + P], lambda r, j: xn_t[0:r, j, :])
            else:
                t = P * (k - 5)
                m = two(psum[:, 6 + k % 2, 0:E_GAU], lambda r, j: xn_t[0:r, j, t:t + P], lambda r, j: w_uv[0:r, j, E_GAU:2 * E_GAU])
            m.then_inc(uv_done, 1)

        def gqk(g):
            pe.wait_ge(rope_ready, g + 1)
            pe.wait_ge(silu_ready, 9 * g + 6)
            for s in range(SUB):
                t = slice(P * s, P * s + P)
                m = mm(psum[:, 7, t], qk_t[:, 1, t], qk_t[:, 0, t], True, True)
            m.then_inc(gqk_done, 1)

        def kv(g, c):
            pe.wait_ge(kern_ready, g + 1)
            pe.wait_ge(silu_ready, 9 * g + 9)
            if c == 2:
                pe.wait_ge(gated_ready, EC * g + 1)
            for s in range(SUB):
                t = slice(P * s, P * s + P)
                m = mm(psum[:, 6 + c % 2, t], v_nat[:, s, P * c:P * c + P], kern[:, s, :], True, True)
            m.then_inc(kv_done, 1)

        def gau(g, half):
            pe.wait_ge(gated_ready, EC * g + EC)
            for s in (2 * half, 2 * half + 1):
                for c in range(EC):
                    m = mm(psum[:, 7 - half, EMB * (s % 2):EMB * (s % 2) + EMB], gated[:, c, P * s:P * s + P],
                           w_gau[:, c, :], c == 0, c == EC - 1)
            m.then_inc(gau_done, 1)

        def turn_x3(g, j):
            pe.wait_ge(x3_ready, SUB * g + SUB)
            pe.wait_ge(h2_ready, 2 * g + 2)
            for s in range(SUB):
                m = pe.transpose(psum[0:HC, 7 - j, P * s:P * s + P], x3[:, s, HC * j:HC * j + HC], ident)
            m.then_inc(x3_turned, 1)

        def route(g):
            pe.wait_ge(x3_t_ready, 2 * g + 2)
            for s in range(SUB):
                for j in range(2):
                    m = mm(psum[:, 7, NE * s:NE * s + NE], x3_t[:, j, P * s:P * s + P], w_route[:, j, :], j == 0, j == 1)
            m.then_inc(route_done, 1)

        def front(g):
            v(g, 0)
            v(g, 1)
            scores(g, 0)
            scores(g, 1)
            turn_probs(g, 0)
            turn_probs(g, 1)
            pv(g, 0)
            scores(g, 2)
            pv(g, 1)
            turn_att(g, 0)
            scores(g, 3)
            proj(g, 0)
            turn_att(g, 1)
            turn_probs(g, 2)
            proj(g, 1)
            pv(g, 2)
            turn_probs(g, 3)
            turn_att(g, 2)
            conv(g + 1, 0)
            pv(g, 3)
            proj(g, 2)
            turn_att(g, 3)
            conv(g + 1, 1)
            proj(g, 3)
            for m in range(3):
                qk(g + 1, m)

        def both(g, more):
            b = g - 1
            turn_xn(b, 0)
            turn_xn(b, 1)
            v(g, 0)
            v(g, 1)
            uv(b, 0)
            scores(g, 0)
            uv(b, 1)
            scores(g, 1)
            uv(b, 2)
            turn_probs(g, 0)
            uv(b, 3)
            turn_probs(g, 1)
            pv(g, 0)
            uv(b, 4)
            scores(g, 2)
            pv(g, 1)
            turn_att(g, 0)
            uv(b, 5)
            scores(g, 3)
            proj(g, 0)
            turn_att(g, 1)
            gqk(b)
            uv(b, 6)
            proj(g, 1)
            turn_probs(g, 2)
            uv(b, 7)
            pv(g, 2)
            turn_probs(g, 3)
            uv(b, 8)
            turn_att(g, 2)
            kv(b, 0)
            pv(g, 3)
            proj(g, 2)
            kv(b, 1)
            turn_att(g, 3)
            kv(b, 2)
            proj(g, 3)
            if more:
                conv(g + 1, 0)
            gau(b, 0)
            gau(b, 1)
            if more:
                conv(g + 1, 1)
            turn_x3(b, 0)
            turn_x3(b, 1)
            if more:
                qk(g + 1, 0)
                qk(g + 1, 1)
            route(b)
            if more:
                qk(g + 1, 2)

        def back(g):
            turn_xn(g, 0)
            turn_xn(g, 1)
            for k in range(6):
                uv(g, k)
            gqk(g)
            for k in range(6, 9):
                uv(g, k)
            for c in range(EC):
                kv(g, c)
            gau(g, 0)
            gau(g, 1)
            turn_x3(g, 0)
            turn_x3(g, 1)
            route(g)

        pe.wait_ge(weights_in, ALL_WEIGHTS)
        pe.wait_ge(const_ready, N_CONST)
        for n in range(2):
            for j in range(2):
                m = mm(psum[0:1, 6 + n, :], beta[:, j:j + 1], w_uv[0:HC, j, 512 * n:512 * n + 512], j == 0, j == 1)
        m.then_inc(fold_done, 1)
        conv(0, 0)
        conv(0, 1)
        for m in range(3):
            qk(0, m)
        pe.wait_ge(fold_ready, N_FOLDS)
        peeled(pe, front, both, back)

    @block.vector
    def _(dve):
        def fold(ins, n):
            ins.then_inc(fold_ready, 1)
            dve.wait_ge(fold_ready, n)

        def prepare():
            dve.wait_ge(fold_done, 1)
            fold(dve.tensor_tensor(w_uv[HC:HC + 1, 0, :].rearrange("p (a b) -> p a b", a=2), psum[0:1, 6:8, :],
                                   w_uv[HC:HC + 1, 0, :].rearrange("p (a b) -> p a b", a=2), ALU.add), 1)
            fold(dve.tensor_scalar(w_uv[0:HC, 0, :], w_uv[0:HC, 0, :], gamma[:, 0:1], None, ALU.mult), 2)
            fold(dve.tensor_scalar(w_uv[0:HC, 1, :], w_uv[0:HC, 1, :], gamma[:, 1:2], None, ALU.mult), 3)
            for q in range(2):
                fold(dve.tensor_scalar(rope_tab[:, 0, q, :], rope[:, 0, :], qk_gain[:, q, 0:1], 0.5, ALU.mult, ALU.mult), 5 * q + 4)
                fold(dve.tensor_scalar(rope_tab[:, 1, q, :], rope[:, 1, :], qk_gain[:, q, 1:2], 0.5, ALU.mult, ALU.mult), 5 * q + 5)
                fold(dve.tensor_scalar(rope_tab[:, 2, q, :], rope[:, 0, :], qk_shift[:, q, 0:1], None, ALU.mult), 5 * q + 6)
                fold(dve.tensor_scalar(biased[:, q, 0:L], rope[:, 1, :], qk_shift[:, q, 1:2], None, ALU.mult), 5 * q + 7)
                fold(dve.tensor_tensor(rope_tab[:, 2, q, :], rope_tab[:, 2, q, :], biased[:, q, 0:L], ALU.add), 5 * q + 8)

        def qk_out(g):
            least(dve, scores_done, SUB * g)
            dve.wait_ge(qk_done, 3 * g + 2)
            for h in range(2):
                dve.tensor_scalar(q_b[0:64, :, h, :], images(psum[0:64, 3, :]), head_mask[0:64, h:h + 1], None, ALU.mult).then_inc(qk_by_dve, 1)
            dve.wait_ge(qk_done, 3 * g + 3)
            for a in range(1, 4):
                dve.tensor_copy(k_a[32 * a:32 * a + 32, a, :], psum[32 * a:32 * a + 32, 4, :]).then_inc(qk_by_dve, 1)

        def v_out(g):
            least(dve, pv_done, SUB * g)
            for half in range(2):
                dve.wait_ge(v_done, 2 * g + half + 1)
                dve.tensor_copy(v_dest(half, 1), v_src(half, 1)).then_inc(v_by_dve, 1)

        def shift(g, s):
            dve.wait_ge(scores_done, SUB * g + s + 1)
            x = psum[:, score_banks(s):score_banks(s) + 2, 0:PAIRS * L].rearrange("p i (a k) -> p i a k", k=L)
            top = row_max[:, s % 2, :, :]
            dve.tensor_reduce(top, x, AX.X, ALU.max).then_inc(max_ready, 1)
            dve.wait_ge(max_ready, SUB * g + s + 1)
            least(dve, probs_turned, SUB * g + s - 1)
            dve.tensor_tensor(probs[:, s % 2].rearrange("p a i k -> p i a k"), x, top.unsqueeze(3).broadcast_to([P, 2, PAIRS, L]), ALU.subtract)\
                .then_inc(shifted, 1)

        def probs_t_out(g, s):
            dve.wait_ge(probs_turned, SUB * g + s + 1)
            least(dve, pv_done, SUB * g + s - 1)
            dve.tensor_copy(probs_t[:, s % 2, 3:6, :].rearrange("p a q -> p (a q)"), psum[:, score_banks(s) + 1, 0:384]).then_inc(probs_t_dve, 1)

        def normalise(g, s):
            dve.wait_ge(pv_done, SUB * g + s + 1)
            least(dve, att_turned, SUB * g + s - 1)
            o = psum[:, 4, 0:PAIRS * 4 * VH].rearrange("p (a i e) -> p a i e", i=2, e=2 * VH)
            for h in range(2):
                r = slice(64 * h, 64 * h + 64)
                dve.reciprocal(inv_sum[r, s % 2, :, :], o[r, :, :, VH * h + HD]).then_inc(inv_ready, 1)
            dve.wait_ge(inv_ready, 2 * (SUB * g + s + 1))
            for h in range(2):
                r = slice(64 * h, 64 * h + 64)
                dve.tensor_tensor(att[r, s % 2, :, :, :].rearrange("p i a e -> p a i e"), o[r, :, :, VH * h:VH * h + HD],
                                  inv_sum[r, s % 2, :, :].unsqueeze(3).broadcast_to([64, PAIRS, 2, HD]), ALU.mult)\
                   .then_inc(att_ready, 1)

        def moments1(g, s):
            dve.wait_ge(h1_ready, SUB * g + s + 1)
            if s == 0 and (not isinstance(g, int) or g > 0):
                dve.wait_ge(coef1_ready, 2 * g)
            dve.bn_stats(stats1[:, s, :], h1[:, s, :]).then_inc(stat_step, 1)

        def moments1_end(g, stat_base):
            dve.wait_ge(stat_step, stat_base + 4)
            apart(dve, dve_passed)
            for s in range(SUB):
                ins = dve.bn_aggr(mean_var1[:, s, :], stats1[:, s, :]).then_inc(stat_step, 1)
            dve.wait_ge(stat_step, stat_base + 8)
            dve.tensor_scalar(coef[:, 0, :], mean_var1[:, :, 1], EPS, None, ALU.add).then_inc(var1_ready, 1)

        def xn_out(g):
            dve.wait_ge(coef1_ready, 2 * g + 2)
            least(dve, xn_turned, 2 * g)
            for s in range(SUB):
                dve.tensor_scalar(xn[:, s, :], h1[:, s, :], mean_var1[:, s, 0:1], coef[:, 7, s:s + 1],
                                  ALU.subtract, ALU.mult).then_inc(xn_ready, 1)

        def silu(g, k):
            bank, cols = (6 + k % 2, 512) if k < 5 else (6 + k % 2, E_GAU)
            dve.wait_ge(tanh_ready, 9 * g + k + 1)
            if k == 1:
                least(dve, rope_2_half, g)
            if k == 5:
                least(dve, kv_done, EC * g)
            dest = base[:, k, :] if k < 2 else u_t[:, k - 2, :] if k < 5 else v_nat[:, k - 5, :]
            dve.scalar_tensor_tensor(dest, tanh[:, k % 3, 0:cols], 1.0, psum[:, bank, 0:cols], ALU.add, ALU.mult)\
               .then_inc(silu_ready, 1)

        def rope_first(g):
            dve.wait_ge(silu_ready, 9 * g + 1)
            dve.tensor_tensor(by_image(rope_1), of_base(base[:, 0, :]), table(0), ALU.mult).then_inc(rope_1_ready, 1)

        def rope_out(g):
            dve.wait_ge(rope_1_ready, g + 1)
            dve.wait_ge(rope_2_ready, g + 1)
            least(dve, gqk_done, g)
            dve.tensor_tensor(qk_t[:], rope_1[:], rope_2[:], ALU.add).then_inc(rope_ready, 1)

        def kern_out(g):
            dve.wait_ge(gqk_done, g + 1)
            least(dve, kv_done, EC * g)
            dve.scalar_tensor_tensor(biased[:], psum[:, 7, :].rearrange("p (s n) -> p s n", n=P), 1.0 / L,
                                     rel_bias[:].unsqueeze(1).broadcast_to([P, SUB, P]), ALU.mult, ALU.add).then_inc(biased_ready, 1)
            dve.wait_ge(biased_ready, g + 1)
            dve.scalar_tensor_tensor(kern[:], biased[:], 0.0, biased[:], ALU.max, ALU.mult).then_inc(kern_ready, 1)

        def gate_out(g, c):
            dve.wait_ge(kv_done, EC * g + c + 1)
            least(dve, gau_done, 2 * g)
            dve.scalar_tensor_tensor(gated[:, c, :], u_t[:, c, :], 0.25, psum[:, 6 + c % 2, :], ALU.mult, ALU.mult)\
               .then_inc(gated_ready, 1)

        def h2_out(g, half):
            dve.wait_ge(gau_done, 2 * g + half + 1)
            dve.wait_ge(h1_plus_ready, g + 1)
            least(dve, h2_kept, 16 * g)
            s = slice(2 * half, 2 * half + 2)
            dve.tensor_tensor(h2[:, s, :], psum[:, 7 - half, 0:2 * EMB].rearrange("p (s e) -> p s e", e=EMB),
                              h1_plus[:, s, :], ALU.add).then_inc(h2_ready, 1)

        def moments2(g, stat_base):
            dve.wait_ge(h2_ready, 2 * g + 2)
            least(dve, coef2_ready, g)
            for s in range(SUB):
                dve.bn_stats(stats2[:, s, :], h2[:, s, :]).then_inc(stat_step, 1)
            dve.wait_ge(stat_step, stat_base + 4)
            apart(dve, dve_passed)
            for s in range(SUB):
                dve.bn_aggr(mean_var2[:, s, :], stats2[:, s, :]).then_inc(stat_step, 1)
            dve.wait_ge(stat_step, stat_base + 8)
            dve.tensor_scalar(coef2[:, 0, :], mean_var2[:, :, 1], EPS, None, ALU.add).then_inc(var2_ready, 1)

        def x3_out(g):
            dve.wait_ge(coef2_ready, g + 1)
            least(dve, x3_kept, 16 * g)
            least(dve, x3_turned, 2 * g)
            for s in range(SUB):
                dve.tensor_scalar(x3[:, s, :], h2[:, s, :], mean_var2[:, s, 0:1], coef2[:, 1, s:s + 1],
                                  ALU.subtract, ALU.mult).then_inc(x3_ready, 1)

        def choose(g):
            n = 9 * g
            dve.wait_ge(route_done, g + 1)
            dve.tensor_copy(logits[:], psum[:, 7, 0:SUB * NE].rearrange("p (s e) -> p s e", e=NE)).then_inc(logits_read, 1)
            dve.wait_ge(logits_read, g + 1)
            apart(dve, dve_passed)
            for s in range(SUB):
                dve.max(best[:, s, :], logits[:, s, :]).then_inc(best_step, 1)
            dve.wait_ge(best_step, 8 * g + 4)
            apart(dve, dve_passed)
            for s in range(SUB):
                dve.max_index(best_at[:, s, :], best[:, s, :], logits[:, s, :]).then_inc(best_step, 1)
            dve.wait_ge(best_step, 8 * g + 8)
            dve.tensor_copy(top_all[:, bass.ds(SUB * g, SUB), :], best[:, :, 0:TOPK]).then_inc(routed, 1)
            dve.tensor_copy(idx_all[:, bass.ds(SUB * g, SUB), :], best_at[:, :, 0:TOPK]).then_inc(routed, 1)

        def front(g):
            qk_out(g)
            v_out(g)
            shift(g, 0)
            shift(g, 1)
            probs_t_out(g, 0)
            probs_t_out(g, 1)
            normalise(g, 0)
            shift(g, 2)
            normalise(g, 1)
            shift(g, 3)
            probs_t_out(g, 2)
            normalise(g, 2)
            probs_t_out(g, 3)
            normalise(g, 3)
            for s in range(SUB):
                moments1(g, s)
            moments1_end(g, 0)
            xn_out(g)

        def both(g, more):
            b = g - 1
            qk_out(g)
            v_out(g)
            silu(b, 0)
            shift(g, 0)
            silu(b, 1)
            rope_first(b)
            shift(g, 1)
            silu(b, 2)
            probs_t_out(g, 0)
            silu(b, 3)
            rope_out(b)
            probs_t_out(g, 1)
            normalise(g, 0)
            silu(b, 4)
            shift(g, 2)
            normalise(g, 1)
            silu(b, 5)
            shift(g, 3)
            kern_out(b)
            silu(b, 6)
            probs_t_out(g, 2)
            silu(b, 7)
            probs_t_out(g, 3)
            normalise(g, 2)
            silu(b, 8)
            gate_out(b, 0)
            normalise(g, 3)
            gate_out(b, 1)
            gate_out(b, 2)
            for s in range(SUB):
                moments1(g, s)
            moments1_end(g, 16 * g - 8)
            h2_out(b, 0)
            h2_out(b, 1)
            moments2(b, 16 * g)
            xn_out(g)
            x3_out(b)
            choose(b)

        def back(g):
            for k in range(3):
                silu(g, k)
            rope_first(g)
            for k in range(3, 6):
                silu(g, k)
            rope_out(g)
            kern_out(g)
            for k in range(6, 9):
                silu(g, k)
            for c in range(EC):
                gate_out(g, c)
            h2_out(g, 0)
            h2_out(g, 1)
            moments2(g, 16 * g + 8)
            x3_out(g)
            choose(g)

        dve.wait_ge(weights_in, ALL_WEIGHTS)
        dve.wait_ge(const_ready, N_CONST)
        prepare()
        peeled(dve, front, both, back)
        dve.wait_ge(routed, 2 * G)


def experts(nc, d, scope, psum, h2_all, x3_all, top_all, idx_all, consts, ident):
    def sb(name, shape, dt=F32):
        return scope.enter_context(nc.sbuf_tensor(name, shape, dt))

    def sem(name):
        return scope.enter_context(nc.semaphore(name))

    tri = consts[:, P:2 * P]
    experts_iota = consts[:, 2 * P:2 * P + NE]
    slot_starts = consts[:, 2 * P + NE:2 * P + NE + SLOTS]
    w1 = sb("w1_sb", [HC + 1, NE, 2, HID])
    w2 = sb("w2_sb", [P, NE, HK, EMB])
    b2 = sb("b2_sb", [P, NE, EMB])
    ws1 = sb("ws1_sb", [HC + 1, 2, HID])
    ws2 = sb("ws2_sb", [P, HK, EMB])
    bs2 = sb("bs2_sb", [P, EMB])
    x3_t = sb("x3_t_in", [HC + 1, 2, GT])
    hs_t = sb("hs_t", [P, HK, GT])
    ys = sb("ys", [P, 2, EMB])
    ones = sb("ones", [P, P])
    chosen = sb("chosen", [P, TOPK, NT, NE])
    mask = sb("mask", [P, NT, NE])
    running = sb("running", [P, 2, NT, NE])
    place = sb("place", [P, NT, NE])
    product = sb("product", [P, NT, NE])
    rows_f = sb("rows_f", [P, TOPK, NT])
    rows = sb("rows", [P, TOPK, NT], U32)
    gap = sb("gap", [P, NT])
    gate = sb("gate", [P, 3, NT])
    padded_i = sb("padded_i", [P, NE], I32)
    padded = sb("padded", [P, NE])
    ends = sb("ends", [P, 2, NE])
    starts = sb("starts", [P, NE])
    past = sb("past", [1, SLOTS, NE])
    slot_expert_f = sb("slot_expert_f", [1, SLOTS])
    slot_expert = sb("slot_expert", [1, SLOTS], I32)
    meta = sb("meta", [P, SLOTS + 1, 2])
    x_slot = sb("x_slot", [P, 2, ROW])
    x_slot_t = sb("x_slot_t", [HC + 1, 2, 2, P])
    h_slot = sb("h_slot", [P, 2, HID])
    h_slot_t = sb("h_slot_t", [P, 2, HK, P])
    y_plain = sb("y_plain", [P, 2, EMB])
    y_gated = sb("y_gated", [P, 2, EMB])
    tokens = sb("tokens", [P, 2], U32)

    x3t_in, shared_in, experts_in = sem("x3t_in"), sem("shared_in"), sem("experts_in")
    hs_done, hs_by_act, hs_by_dve = sem("hs_done"), sem("hs_by_act"), sem("hs_by_dve")
    ys_done, ys_step, shared_ready, out_stored = sem("ys_done"), sem("ys_step"), sem("shared_ready"), sem("out_stored")
    ones_ready, mask_ready, ranks_done, route_step = sem("ones_ready"), sem("mask_ready"), sem("ranks_done"), sem("route_step")
    gates_ready = sem("gates_ready")
    gap_ready, gap_exp, table_ready = sem("gap_ready"), sem("gap_exp"), sem("table_ready")
    rows_ready, gate_set, dispatched = sem("rows_ready"), sem("gate_set"), sem("dispatched")
    meta_ready = sem("meta_ready")
    x_slot_in = [sem("x_slot_in0"), sem("x_slot_in1")]
    x_turned, x_t_ready = sem("x_turned"), sem("x_t_ready")
    h_done, h_by_act, h_by_dve = sem("h_done"), sem("h_by_act"), sem("h_by_dve")
    h_turned, h_t_by_act, h_t_by_dve = sem("h_turned"), sem("h_t_by_act"), sem("h_t_by_dve")
    y_done, y_plain_ready, y_ready = sem("y_done"), sem("y_plain_ready"), sem("y_ready")
    tokens_ready, added, pool_passed = sem("tokens_ready"), sem("added"), sem("pool_passed")
    HALF = HID // 2

    def groups(eng, body):
        body(0)
        with eng.Fori(1, G) as g:
            body(g)

    def slots(eng, step):
        step(1, 1, 0)
        step(2, 0, 1)
        with eng.Fori(1, (SLOTS - 1) // 2) as i:
            step(2 * i + 1, 1, i)
            step(2 * i + 2, 0, i + 1)

    block = scope.enter_context(nc.Block())

    @block.sync
    def _(sp):
        sp.dma_start(x3_t[0:HC], d["x3t"][0]).then_inc(x3t_in, 16)
        sp.dma_start(ws1[:], d["ws1"]).then_inc(shared_in, 16)
        sp.dma_start(ws2[:], d["ws2"]).then_inc(shared_in, 16)
        sp.dma_start(bs2[:], d["bs2"].broadcast_to([P, EMB])).then_inc(shared_in, 16)
        sp.dma_start(w1[:], d["w1"]).then_inc(experts_in, 16)
        sp.dma_start(w2[:], d["w2"]).then_inc(experts_in, 16)
        sp.dma_start(b2[:].rearrange("p e n -> p (e n)"), d["b2"].broadcast_to([P, NE * EMB])).then_inc(experts_in, 16)
        with sp.Fori(1, G) as g:
            sp.wait_ge(hs_done, HK * g)
            sp.dma_start(x3_t[0:HC], d["x3t"][bass.ds(g, 1)].rearrange("a p c t -> p (a c) t")).then_inc(x3t_in, 16)
            sp.wait_ge(shared_ready, SUB * g)
            sp.dma_start(d["out"][bass.ds(GT * (g - 1), GT), :].rearrange("(s p) e -> p s e", p=P),
                         h2_all[:, bass.ds(SUB * (g - 1), SUB), :]).then_inc(out_stored, 16)
        sp.wait_ge(shared_ready, SUB * G)
        sp.dma_start(d["out"][GT * (G - 1):GT * G, :].rearrange("(s p) e -> p s e", p=P),
                     h2_all[:, SUB * (G - 1):SUB * G, :]).then_inc(out_stored, 16)
        sp.wait_ge(dispatched, 16 * TOPK * NT)

        def load(s, par):
            sp.dma_start(x_slot[:, par, :], d["slot_rows"][bass.ds(P * s, P), :]).then_inc(x_slot_in[par], 16)

        load(0, 0)
        load(1, 1)
        with sp.Fori(0, (SLOTS - 1) // 2) as i:
            sp.wait_ge(x_turned, 2 * i + 1)
            sp.wait_ge(meta_ready, 2 * i + 1)
            load(2 * i + 2, 0)
            sp.wait_ge(x_turned, 2 * i + 2)
            sp.wait_ge(meta_ready, 2 * i + 2)
            load(2 * i + 3, 1)
        sp.wait_ge(out_stored, 16 * G)

    @block.gpsimd
    def _(pool):
        for n, tile in enumerate((ones[:], x3_t[HC:HC + 1, 0, :], x_slot_t[HC:HC + 1, :, 0, :])):
            pool.memset(tile, 1.0).then_inc(ones_ready, 1)
            pool.wait_ge(ones_ready, n + 1)
        pool.wait_ge(rows_ready, 1)
        for k in range(TOPK):
            if k > 0:
                pool.wait_ge(dispatched, 16 * NT)
            pool.wait_ge(gates_ready, 1)
            pool.tensor_copy(x3_all[:, :, EMB], gate[:, k, :]).then_inc(gate_set, 1)
            pool.wait_ge(gate_set, k + 1)
            for t in range(NT):
                pool.indirect_dma_start(out=d["slot_rows"], out_offset=bass.IndirectOffsetOnAxis(ap=rows[:, k, t:t + 1], axis=0),
                                        in_=x3_all[:, t, :], in_offset=None).then_inc(dispatched, 16)
        pool.wait_ge(out_stored, 16 * G)

        def take_meta(s, par, half):
            pool.wait_ge(x_slot_in[par], 16 * (half + 1))
            apart(pool, pool_passed)
            pool.tensor_copy(meta[:, bass.ds(s, 1), :].rearrange("p a w -> p (a w)"), x_slot[:, par, EMB:ROW]).then_inc(meta_ready, 1)

        def add_rows(s, par, half):
            take_meta(s + 1, 1 - par, half + par)
            pool.wait_ge(meta_ready, s + 1)
            least(pool, added, 16 * (s - 1))
            apart(pool, pool_passed)
            pool.tensor_copy(tokens[:, par:par + 1], meta[:, bass.ds(s, 1), 1]).then_inc(tokens_ready, 1)
            pool.wait_ge(tokens_ready, s + 1)
            pool.wait_ge(y_ready, s + 1)
            least(pool, added, 16 * s)
            apart(pool, pool_passed)
            pool.indirect_dma_start(out=d["out"], out_offset=bass.IndirectOffsetOnAxis(ap=tokens[:, par:par + 1], axis=0),
                                    in_=y_gated[:, par, :], in_offset=None, compute_op=ALU.add).then_inc(added, 16)

        take_meta(0, 0, 0)
        add_rows(0, 0, 0)
        slots(pool, add_rows)
        pool.wait_ge(added, 16 * SLOTS)

    @block.scalar
    def _(act):
        def hs_out(g):
            least(act, ys_done, SUB * g)
            for c in range(0, HK, 2):
                act.wait_ge(hs_done, HK * g + c + 1)
                act.activation(hs_t[:, c, :], psum[:, c % 3, :], ACT.Relu).then_inc(hs_by_act, 1)

        act.wait_ge(gap_ready, 1)
        act.activation(gate[:, 2, :], gap[:], ACT.Exp).then_inc(gap_exp, 1)
        groups(act, hs_out)

        def x_t_out(s, par):
            act.wait_ge(x_turned, s + 1)
            least(act, h_done, s - 1)
            act.activation(x_slot_t[0:HC, par, :, :].rearrange("p j t -> p (j t)"), psum[0:HC, 0, 0:2 * P], ACT.Copy).then_inc(x_t_ready, 1)

        def h_out(s, par):
            act.wait_ge(h_done, s + 1)
            least(act, h_turned, s - 1)
            act.activation(h_slot[:, par, 0:HALF], psum[:, 1, 0:HALF], ACT.Relu).then_inc(h_by_act, 1)

        def h_t_out(s, par):
            act.wait_ge(h_turned, s + 1)
            least(act, y_done, s - 1)
            act.activation(h_slot_t[:, par, 0:3, :].rearrange("p c t -> p (c t)"), psum[:, 3, 0:HALF], ACT.Copy).then_inc(h_t_by_act, 1)

        def y_out(s, par):
            act.wait_ge(y_plain_ready, s + 1)
            act.wait_ge(meta_ready, s + 1)
            least(act, added, 16 * (s - 1))
            act.activation(y_gated[:, par, :], y_plain[:, par, :], ACT.Copy, scale=meta[:, bass.ds(s, 1), 0]).then_inc(y_ready, 1)

        def step(s, par, half):
            h_out(s, par)
            x_t_out(s + 1, 1 - par)
            y_out(s - 1, 1 - par)
            h_t_out(s, par)

        act.wait_ge(ones_ready, 3)
        x_t_out(0, 0)
        h_out(0, 0)
        x_t_out(1, 1)
        h_t_out(0, 0)
        slots(act, step)
        y_out(SLOTS - 1, 0)

    @block.tensor
    def _(pe):
        def two(out, lhs, rhs):
            pe.matmul(out, lhs(HC + 1, 0), rhs(HC + 1, 0), start=True, stop=False)
            return pe.matmul(out, lhs(HC, 1), rhs(HC, 1), start=False, stop=True)

        def hs(g):
            pe.wait_ge(x3t_in, 16 * (g + 1))
            for c in range(HK):
                if c in (0, 2):
                    least(pe, hs_by_dve, 3 * g - (c == 0))
                elif c == 1:
                    least(pe, hs_by_act, 3 * g)
                else:
                    pe.wait_ge(hs_by_dve if c == 4 else hs_by_act, 3 * g + (2 if c == 5 else 1))
                two(psum[:, c % 3, :], lambda k, j: ws1[0:k, j, P * c:P * c + P], lambda k, j: x3_t[0:k, j, :]).then_inc(hs_done, 1)

        def ys_of(g):
            pe.wait_ge(hs_by_act, 3 * g + 3)
            pe.wait_ge(hs_by_dve, 3 * g + 3)
            for s in range(SUB):
                least(pe, shared_ready, SUB * g + s - 1)
                for c in range(HK):
                    m = pe.matmul(psum[:, 3 + s % 2, 0:EMB], hs_t[:, c, P * s:P * s + P], ws2[:, c, :],
                                  start=(c == 0), stop=(c == HK - 1))
                m.then_inc(ys_done, 1)

        def shared(g):
            hs(g)
            ys_of(g)

        pe.wait_ge(shared_in, 48)
        pe.wait_ge(ones_ready, 2)
        hs(0)
        pe.wait_ge(mask_ready, 1)
        flat = mask[:].rearrange("p t e -> p (t e)")
        pe.matmul(psum[:, 6, 0:NT * NE], tri, flat, start=True, stop=True)
        pe.matmul(psum[:, 7, 0:NT * NE], ones[:], flat, start=True, stop=True).then_inc(ranks_done, 1)
        ys_of(0)
        with pe.Fori(1, G) as g:
            shared(g)

        def expert(s):
            return pe.value_load(slot_expert[0:1, bass.ds(s, 1)], min_val=0, max_val=NE - 1)

        def turn_x(s, par, half):
            pe.wait_ge(x_slot_in[par], 16 * (half + 1))
            least(pe, x_t_ready, s)
            for j in range(2):
                m = pe.transpose(psum[0:HC, 0, P * j:P * j + P], x_slot[:, par, HC * j:HC * j + HC], ident)
            m.then_inc(x_turned, 1)

        def h(s, par, e):
            pe.wait_ge(x_t_ready, s + 1)
            least(pe, h_by_act, s)
            least(pe, h_by_dve, s)
            for k, j in ((HC + 1, 0), (HC, 1)):
                for n in range(2):
                    m = pe.matmul(psum[:, 1 + n, 0:HALF], x_slot_t[0:k, par, j, :],
                                  w1[0:k, bass.ds(e, 1), j, HALF * n:HALF * n + HALF].rearrange("p a n -> p (a n)"),
                                  start=(j == 0), stop=(j == 1))
            m.then_inc(h_done, 1)

        def turn_h(s, par):
            pe.wait_ge(h_by_act, s + 1)
            pe.wait_ge(h_by_dve, s + 1)
            least(pe, h_t_by_act, s)
            least(pe, h_t_by_dve, s)
            for c in range(HK):
                m = pe.transpose(psum[:, 3 + c // 3, P * (c % 3):P * (c % 3) + P], h_slot[:, par, P * c:P * c + P], ident)
            m.then_inc(h_turned, 1)

        def y(s, par, e):
            pe.wait_ge(h_t_by_act, s + 1)
            pe.wait_ge(h_t_by_dve, s + 1)
            least(pe, y_plain_ready, s - 1)
            for c in range(HK):
                m = pe.matmul(psum[:, 5 + par, 0:EMB], h_slot_t[:, par, c, :],
                              w2[:, bass.ds(e, 1), c, :].rearrange("p a n -> p (a n)"), start=(c == 0), stop=(c == HK - 1))
            m.then_inc(y_done, 1)

        def step(s, par, half):
            before, now = expert(s - 1), expert(s)
            h(s, par, now)
            turn_x(s + 1, 1 - par, half + par)
            y(s - 1, 1 - par, before)
            turn_h(s, par)

        pe.wait_ge(experts_in, 48)
        pe.wait_ge(ones_ready, 3)
        pe.wait_ge(table_ready, 1)
        turn_x(0, 0, 0)
        h(0, 0, expert(0))
        turn_x(1, 1, 0)
        turn_h(0, 0)
        slots(pe, step)
        y(SLOTS - 1, 0, expert(SLOTS - 1))

    @block.vector
    def _(dve):
        steps = [0]

        def link(ins):
            steps[0] += 1
            ins.then_inc(route_step, 1)
            dve.wait_ge(route_step, steps[0])

        def by_token(x):
            return x.unsqueeze(1).broadcast_to([P, NT, NE])

        dve.tensor_tensor(gap[:], top_all[:, :, 1], top_all[:, :, 0], ALU.subtract).then_inc(gap_ready, 1)
        for k in range(TOPK):
            link(dve.tensor_tensor(chosen[:, k], by_token(experts_iota), idx_all[:, :, k].unsqueeze(2).broadcast_to([P, NT, NE]),
                                   ALU.is_equal))
        dve.tensor_tensor(mask[:], chosen[:, 0], chosen[:, 1], ALU.add).then_inc(mask_ready, 1)
        dve.wait_ge(gap_exp, 1)
        link(dve.tensor_scalar(gap[:], gate[:, 2, :], 1.0, None, ALU.add))
        link(dve.reciprocal(gate[:, 0, :], gap[:]))
        dve.tensor_tensor(gate[:, 1, :], gate[:, 2, :], gate[:, 0, :], ALU.mult).then_inc(gates_ready, 1)

        def hs_out(g):
            least(dve, ys_done, SUB * g)
            for c in range(1, HK, 2):
                dve.wait_ge(hs_done, HK * g + c + 1)
                dve.tensor_scalar(hs_t[:, c, :], psum[:, c % 3, :], 0.0, None, ALU.max).then_inc(hs_by_dve, 1)

        def ys_out(g):
            for s in range(SUB):
                dve.wait_ge(ys_done, SUB * g + s + 1)
                dve.tensor_tensor(ys[:, s % 2, :], psum[:, 3 + s % 2, 0:EMB], bs2[:], ALU.add).then_inc(ys_step, 1)
                dve.wait_ge(ys_step, SUB * g + s + 1)
                row = h2_all[:, bass.ds(SUB * g + s, 1), :].rearrange("p a e -> p (a e)")
                dve.scalar_tensor_tensor(row, ys[:, s % 2, :], 0.1 * TOPK, row, ALU.mult, ALU.add).then_inc(shared_ready, 1)

        dve.wait_ge(shared_in, 48)
        hs_out(0)
        dve.wait_ge(ranks_done, 1)
        ranks = psum[:, 6, 0:NT * NE].rearrange("p (t e) -> p t e", e=NE)
        totals = psum[:, 7, 0:NT * NE].rearrange("p (t e) -> p t e", e=NE)
        link(dve.tensor_copy(running[:, 0], totals))
        at = 0
        for hop in (1, 2, 4, 8, 16):
            link(dve.tensor_tensor(running[:, 1 - at, hop:], running[:, at, hop:], running[:, at, :NT - hop], ALU.add))
            link(dve.tensor_copy(running[:, 1 - at, :hop], running[:, at, :hop]))
            at = 1 - at
        link(dve.tensor_scalar(padded_i[:], running[:, at, NT - 1, :], float(P - 1), None, ALU.add))
        link(dve.tensor_single_scalar(padded_i[:], padded_i[:], -P, ALU.bitwise_and))
        link(dve.tensor_copy(padded[:], padded_i[:]))
        link(dve.tensor_copy(ends[:, 0], padded[:]))
        top = 0
        for hop in (1, 2, 4):
            link(dve.tensor_tensor(ends[:, 1 - top, hop:], ends[:, top, hop:], ends[:, top, :NE - hop], ALU.add))
            link(dve.tensor_copy(ends[:, 1 - top, :hop], ends[:, top, :hop]))
            top = 1 - top
        link(dve.tensor_tensor(starts[:], ends[:, top], padded[:], ALU.subtract))
        link(dve.tensor_tensor(place[:], running[:, at], totals, ALU.subtract))
        link(dve.tensor_tensor(place[:], place[:], ranks, ALU.add))
        link(dve.tensor_tensor(place[:], place[:], by_token(starts[:]), ALU.add))
        for k in range(TOPK):
            link(dve.tensor_tensor(product[:], chosen[:, k], place[:], ALU.mult))
            link(dve.tensor_reduce(rows_f[:, k, :], product[:], AX.X, ALU.add))
        dve.tensor_copy(rows[:], rows_f[:]).then_inc(rows_ready, 1)
        link(dve.tensor_tensor(past[:], slot_starts[0:1].unsqueeze(2).broadcast_to([1, SLOTS, NE]),
                               ends[0:1, top].unsqueeze(1).broadcast_to([1, SLOTS, NE]), ALU.is_ge))
        link(dve.tensor_reduce(slot_expert_f[:], past[:], AX.X, ALU.add))
        dve.tensor_scalar(slot_expert[:], slot_expert_f[:], float(NE - 1), None, ALU.min).then_inc(table_ready, 1)
        ys_out(0)
        with dve.Fori(1, G) as g:
            hs_out(g)
            ys_out(g)

        def h_out(s, par):
            dve.wait_ge(h_done, s + 1)
            least(dve, h_turned, s - 1)
            dve.tensor_scalar(h_slot[:, par, HALF:], psum[:, 2, 0:HALF], 0.0, None, ALU.max).then_inc(h_by_dve, 1)

        def h_t_out(s, par):
            dve.wait_ge(h_turned, s + 1)
            least(dve, y_done, s - 1)
            dve.tensor_copy(h_slot_t[:, par, 3:6, :].rearrange("p c t -> p (c t)"), psum[:, 4, 0:HALF]).then_inc(h_t_by_dve, 1)

        def y_out(s, par):
            e = dve.value_load(slot_expert[0:1, bass.ds(s, 1)], min_val=0, max_val=NE - 1)
            dve.wait_ge(y_done, s + 1)
            least(dve, y_ready, s - 1)
            dve.tensor_tensor(y_plain[:, par, :], psum[:, 5 + par, 0:EMB],
                              b2[:, bass.ds(e, 1), :].rearrange("p a n -> p (a n)"), ALU.add).then_inc(y_plain_ready, 1)

        def step(s, par, half):
            h_out(s, par)
            y_out(s - 1, 1 - par)
            h_t_out(s, par)

        dve.wait_ge(table_ready, 1)
        dve.wait_ge(experts_in, 48)
        h_out(0, 0)
        h_t_out(0, 0)
        slots(dve, step)
        y_out(SLOTS - 1, 0)


def lay_out(x):
    import numpy as np
    a = {k: np.asarray(v) for k, v in x.items()}

    def halves(w, bias=None):
        n = w.shape[1]
        t = np.zeros((HC + 1, 2, n), w.dtype)
        t[:HC] = w.reshape(2, HC, n).transpose(1, 0, 2)
        if bias is not None:
            t[HC, 0] = bias
        return t

    side = IMG // PATCH
    patches = a["x"].reshape(G, B // G, CH, side, PATCH, side, PATCH).transpose(0, 2, 4, 6, 1, 3, 5)
    patches = patches.reshape(G, KP, P, GT).transpose(0, 2, 1, 3)
    w_conv = a["L0_tok_conv_w"].reshape(EMB, KP, P).transpose(2, 1, 0)
    wq, wk, wv, wo = (a[f"L0_tok_w{c}"].T for c in "qkvo")
    bq, bk, bv, bo = (a[f"L0_tok_b{c}"] for c in "qkvo")
    w_qkv = halves(np.concatenate([wq, wk[:, P:], wk[:, :P], wv], 1), np.concatenate([bq, bk[P:], bk[:P], bv]))
    w_o = halves(wo.reshape(PAIRS, 2, HD, EMB).transpose(1, 0, 2, 3).reshape(EMB, EMB), bo)
    uv, uvb = a["L0_attn_uv_W"], a["L0_attn_uv_b"]
    swap = (np.arange(S_GAU) + S_GAU // 2) % S_GAU
    base_cols = 2 * E_GAU + swap
    w_uv = halves(np.concatenate([uv, uv[:, base_cols]], 1), np.concatenate([uvb, uvb[base_cols]]))
    gq, bqk = a["L0_attn_gamma_qk"], a["L0_attn_beta_qk"]
    pair_up = lambda v: np.stack([v.T, v[:, swap].T], 2)
    half = S_GAU // 2
    inv_freq = np.power(np.float32(10000.0), -np.arange(half, dtype=np.float32) / half).astype(np.float32)
    angle = (np.arange(L, dtype=np.float32)[None, :] * inv_freq[:, None]).astype(np.float32)
    cos, sin = np.cos(angle), np.sin(angle)
    rope = np.stack([np.concatenate([cos, cos]), np.concatenate([-sin, sin])], 1)
    m, n = np.meshgrid(np.arange(P), np.arange(P), indexing="ij")
    inside = (m // L) == (n // L)
    rel = a["L0_attn_w_rel"][np.where(inside, m - n + L - 1, 0)]
    rel_bias = np.where(inside, rel, np.float32(-1e30))
    head_mask = np.zeros((P, 2), np.float32)
    for h in range(2):
        head_mask[(np.arange(P) // HD) % 2 == h, h] = HD ** -0.5
    consts = np.concatenate([
        np.eye(P), np.triu(np.ones((P, P)), 1), np.tile(np.arange(NE), (P, 1)), np.tile(P * np.arange(SLOTS), (P, 1)),
    ], 1)
    pad_rows = np.zeros((P, ROW), np.float32)
    pad_rows[:, EMB + 1] = T + np.arange(P)
    token_ids = (np.arange(NT)[None, :] * P + np.arange(P)[:, None]).astype(np.float32)
    w1 = np.stack([halves(a["L0_ffn_W1"][e].T, a["L0_ffn_b1"][e]) for e in range(NE)], 1)
    w2 = a["L0_ffn_W2"].transpose(0, 2, 1).reshape(NE, HK, P, EMB).transpose(2, 0, 1, 3)
    w = dict(
        patches=patches, w_conv=w_conv, b_conv=a["L0_tok_conv_b"].reshape(2, HC).T, w_qkv=w_qkv, head_mask=head_mask,
        w_o=w_o, w_uv=w_uv, ln_gamma=a["L0_attn_ln_gamma"].reshape(2, HC).T, ln_beta=a["L0_attn_ln_beta"].reshape(2, HC).T,
        qk_gain=pair_up(gq), qk_shift=pair_up(bqk), rope=rope, rel_bias=rel_bias,
        w_gau=a["L0_attn_o_W"].reshape(EC, P, EMB).transpose(1, 0, 2), b_gau=a["L0_attn_o_b"][None],
        w_route=a["L0_ffn_Wr"].T.reshape(2, HC, NE).transpose(1, 0, 2), w1=w1, w2=w2, b2=a["L0_ffn_b2"].reshape(1, -1),
        ws1=halves(a["L0_ffn_sW1"].T, a["L0_ffn_sb1"]), ws2=a["L0_ffn_sW2"].T.reshape(HK, P, EMB).transpose(1, 0, 2),
        bs2=a["L0_ffn_sb2"][None], consts=consts.astype(np.float32), pad_rows=pad_rows, token_ids=token_ids,
    )
    return {k: np.ascontiguousarray(v) for k, v in w.items()}


def kernel(**inputs):
    import concourse.bacc as bacc
    from concourse.bass_utils import run_bass_kernel_spmd

    nc = bacc.Bacc("TRN2", target_bir_lowering=False, num_devices=1)
    build_program(nc, declare(nc))
    result = run_bass_kernel_spmd(nc, [lay_out(inputs)], core_ids=[0])
    return result.results[0]["out"][:T].reshape(B, L, EMB)
```

```python
from contextlib import ExitStack

import concourse.bass as bass
from concourse import mybir

F32 = mybir.dt.float32
F32R = mybir.dt.float32r
I32 = mybir.dt.int32
U32 = mybir.dt.uint32
ALU = mybir.AluOpType
ACT = mybir.ActivationFunctionType
AX = mybir.AxisListType

P = 128
B, CH, IMG, PATCH = 64, 3, 128, 16
EMB, HEADS = 192, 12
L = (IMG // PATCH) ** 2
T = B * L
HD = EMB // HEADS
PAIRS = HEADS // 2
GT = 512
G = T // GT
SUB = GT // P
NT = T // P
KP = CH * PATCH * PATCH // P
HC = EMB // 2
TAIL = EMB - P
REST = 97
E_GAU, S_GAU = 384, 128
EC = E_GAU // P
NE, TOPK = 8, 2
HID = 4 * EMB
HK = HID // P
SLOTS = (T * TOPK) // P + NE - 1
ROW = EMB + 2
VH = HD + 1
EPS = 1e-5
FAR = 3e38
WUV = 2 * E_GAU + 2 * S_GAU
HT, HS = GT // 2, SUB // 2


def declare(nc):
    shapes = dict(
        patches=[G, P, KP, GT], w_conv=[P, KP, EMB], b_conv=[P, 2], w_qkv=[P, 3, 3 * EMB],
        head_mask=[P, 2], w_o=[HC + 1, 2, EMB], w_uv=[P, 3, WUV], ln_gamma=[P, 3], ln_beta=[P, 2, REST],
        qk_gain=[P, 2, 2], qk_shift=[P, 2, 2], rope=[P, 2, L], rel_bias=[P, P], w_gau=[P, EC, EMB],
        b_gau=[1, EMB], w_route=[P, 2, NE], w1=[NE, P, 3, HID], w2=[P, NE, HK, EMB], b2=[1, NE * EMB],
        ws1=[P, 3, HID], ws2=[P, HK, EMB], bs2=[1, EMB], consts=[P, 2 * P + NE + SLOTS],
    )
    d = {k: nc.dram_tensor(k, s, F32, kind="ExternalInput").ap() for k, s in shapes.items()}
    d["pad_rows"] = nc.dram_tensor("pad_rows", [P, ROW], F32, kind="ExternalInput").ap()
    d["token_ids"] = nc.dram_tensor("token_ids", [P, NT], F32, kind="ExternalInput").ap()
    d["out"] = nc.dram_tensor("out", [T + P, EMB], F32, kind="ExternalOutput").ap()
    d["x3t"] = nc.dram_tensor("x3t", [G, P, 2, GT], F32, kind="Internal").ap()
    d["h2"] = nc.dram_tensor("h2_of_groups", [G, P, SUB, EMB], F32, kind="Internal").ap()
    d["slot_rows"] = nc.dram_tensor("slot_rows", [(SLOTS + 1) * P, ROW], F32, kind="Internal").ap()
    return d


def least(eng, sem, n):
    if not isinstance(n, int) or n > 0:
        eng.wait_ge(sem, n)


def apart(eng, passed):
    eng.sem_inc(passed, 1)


class Packed:

    def __init__(self, sb, name, cols):
        self.hi = sb(name + "_hi", [P, cols], F32R)
        self.lo = sb(name + "_lo", [P, cols], F32R)
        self.both = sb(name + "_both", [P, cols], F32R)
        self.rest = sb(name + "_rest", [REST, cols], F32R)

    def weights(self, cols):
        return [t[:, cols] for t in (self.hi, self.lo, self.hi, self.both, self.rest)]

    def activations(self, cols):
        return [t[:, cols] for t in (self.hi, self.hi, self.lo, self.both, self.rest)]


def product(pe, out, stationary, moving):
    for i in range(5):
        m = pe.matmul(out, stationary[i], moving[i], start=(i == 0), stop=(i == 4))
    return m


def round_weights(act, w, raw, done):
    act.activation(w.hi[:], raw[0], ACT.Copy).then_inc(done, 1)
    act.activation(w.both[:], raw[1], ACT.Copy).then_inc(done, 1)
    act.activation(w.rest[:], raw[2][0:REST], ACT.Copy).then_inc(done, 1)


def rest_of_weights(dve, w, raw, done):
    dve.tensor_tensor(w.lo[:], raw[0], w.hi[:].bitcast(F32), ALU.subtract).then_inc(done, 1)
    dve.tensor_tensor(w.rest[0:TAIL], raw[2][0:TAIL], w.rest[0:TAIL].bitcast(F32), ALU.subtract).then_inc(done, 1)
    dve.tensor_tensor(w.rest[REST - 1:REST], raw[2][REST - 1:REST], w.rest[REST - 1:REST].bitcast(F32), ALU.subtract).then_inc(done, 1)


def build_program(nc, d):
    with ExitStack() as whole:
        def keep(name, shape, dt=F32):
            return whole.enter_context(nc.sbuf_tensor(name, shape, dt))

        psum = whole.enter_context(nc.psum_tensor("psum", [P, 8, 512], F32))
        w2 = keep("w2_sb", [P, NE, HK, EMB])
        x3_all = w2[:].rearrange("p e c n -> p (e c n)")[:, 0:NT * ROW].rearrange("p (t w) -> p t w", w=ROW)
        logits_all = keep("logits_all", [P, NT, NE])
        consts = keep("consts_sb", [P, 2 * P + NE + SLOTS])
        ident = consts[:, 0:P]
        with ExitStack() as scope:
            front_and_back(nc, d, scope, psum, x3_all, logits_all, consts, ident)
        with ExitStack() as scope:
            experts(nc, d, scope, psum, w2, x3_all, logits_all, consts, ident)


def front_and_back(nc, d, scope, psum, x3_all, logits_all, consts, ident):
    def sb(name, shape, dt=F32):
        return scope.enter_context(nc.sbuf_tensor(name, shape, dt))

    def sem(name):
        return scope.enter_context(nc.semaphore(name))

    w_conv = sb("w_conv_sb", [P, KP, EMB])
    b_conv = sb("b_conv_sb", [P, 2])
    w_qkv = Packed(sb, "w_qkv", 3 * EMB)
    head_mask = sb("head_mask_sb", [P, 2])
    w_o = sb("w_o_sb", [HC + 1, 2, EMB])
    w_uv = Packed(sb, "w_uv", WUV)
    gamma = sb("gamma_sb", [P, 3])
    beta = sb("beta_sb", [P, 2, REST])
    qk_gain = sb("qk_gain_sb", [P, 2, 2])
    qk_shift = sb("qk_shift_sb", [P, 2, 2])
    rope = sb("rope_sb", [P, 2, L])
    rel_bias = sb("rel_bias_sb", [P, P])
    w_gau = sb("w_gau_sb", [P, EC, EMB])
    b_gau = sb("b_gau_sb", [P, EMB])
    w_route = sb("w_route_sb", [P, 2, NE])
    rope_tab = sb("rope_tab", [P, 3, 2, L])
    minus_half = sb("minus_half", [P, SUB])
    eps = sb("eps", [P, SUB])
    one = sb("one", [P, SUB])
    minus_one = sb("minus_one", [P, SUB])
    patches = sb("patches_sb", [P, KP, GT])
    tok = Packed(sb, "tok", GT)
    q_a = sb("q_a", [P, GT // L, 2, L])
    q_b = sb("q_b", [P, GT // L, 2, L])
    k_a = sb("k_a", [P, 4, GT])
    k_b = sb("k_b", [P, 2, GT])
    v_ones = sb("v_ones", [P, SUB, PAIRS, 2, 2 * VH])
    row_max = sb("row_max", [P, 2, 2, PAIRS])
    probs = sb("probs", [P, 2, PAIRS, 2, L])
    probs_t = sb("probs_t", [P, 2, PAIRS, P])
    inv_sum = sb("inv_sum", [P, 2, PAIRS, 2])
    att = sb("att", [P, 2, 2, PAIRS, HD])
    att_t = sb("att_t", [HC + 1, 2, 2, P])
    h1 = sb("h1", [P, SUB, EMB])
    stats1 = sb("stats1", [P, SUB, 6])
    mean_var1 = sb("mean_var1", [P, SUB, 2])
    coef = sb("coef", [P, 8, SUB])
    h1_plus = sb("h1_plus", [P, SUB, EMB])
    xn = sb("xn", [P, SUB, EMB])
    xn_t = Packed(sb, "xn_t", GT)
    tanh = sb("tanh", [P, 3, 512])
    u_t = sb("u_t", [P, EC, GT])
    base = sb("base", [P, 2, GT])
    rope_1 = sb("rope_1", [P, 2, GT])
    rope_2 = sb("rope_2", [P, 2, GT])
    qk_t = sb("qk_t", [P, 2, GT])
    v_nat = sb("v_nat", [P, SUB, E_GAU])
    biased = sb("biased", [P, SUB, P])
    gated = sb("gated", [P, EC, GT])
    h2 = sb("h2", [P, SUB, EMB])
    stats2 = sb("stats2", [P, SUB, 6])
    mean_var2 = sb("mean_var2", [P, SUB, 2])
    coef2 = sb("coef2", [P, 3, SUB])
    x3 = sb("x3", [P, SUB, EMB])
    x3_t = sb("x3_t", [P, 2, GT])

    weights_in, patch_weights_in = sem("weights_in"), sem("patch_weights_in")
    patches_in = sem("patches_in")
    pads_in = sem("pads_in")
    conv_done, qk_done, v_done = sem("conv_done"), sem("qk_done"), sem("v_done")
    scores_done, probs_turned, pv_done = sem("scores_done"), sem("probs_turned"), sem("pv_done")
    att_turned, proj_done = sem("att_turned"), sem("proj_done")
    xn_turned, uv_done, gqk_done, kv_done = sem("xn_turned"), sem("uv_done"), sem("gqk_done"), sem("kv_done")
    gau_done, x3_turned, route_done, fold_done = sem("gau_done"), sem("x3_turned"), sem("route_done"), sem("fold_done")
    const_ready, fold_ready = sem("const_ready"), sem("fold_ready")
    tok_hi, tok_lo, xn_hi, xn_lo = sem("tok_hi"), sem("tok_lo"), sem("xn_hi"), sem("xn_lo")
    qkv_hi, qkv_lo, uv_hi, uv_lo = sem("qkv_hi"), sem("qkv_lo"), sem("uv_hi"), sem("uv_lo")
    rows_set, rows_copied = sem("rows_set"), sem("rows_copied")
    qk_by_act, qk_by_dve = sem("qk_by_act"), sem("qk_by_dve")
    v_ready = sem("v_ready")
    max_ready, shifted, exp_done = sem("max_ready"), sem("shifted"), sem("exp_done")
    probs_t_act, probs_t_dve = sem("probs_t_act"), sem("probs_t_dve")
    inv_ready, att_ready, att_t_ready, h1_ready = sem("inv_ready"), sem("att_ready"), sem("att_t_ready"), sem("h1_ready")
    stat_step, var1_ready, coef_step, coef1_ready = sem("stat_step"), sem("var1_ready"), sem("coef_step"), sem("coef1_ready")
    xn_ready, h1_plus_act, h1_plus_ready = sem("xn_ready"), sem("h1_plus_act"), sem("h1_plus_ready")
    tanh_ready, silu_ready = sem("tanh_ready"), sem("silu_ready")
    rope_1_ready, rope_2_half, rope_2_ready, rope_ready = sem("rope_1_ready"), sem("rope_2_half"), sem("rope_2_ready"), sem("rope_ready")
    biased_ready, kern_ready, gated_ready = sem("biased_ready"), sem("kern_ready"), sem("gated_ready")
    h2_ready, var2_ready, coef2_ready, x3_ready, x3_t_ready = sem("h2_ready"), sem("var2_ready"), sem("coef2_ready"), sem("x3_ready"), sem("x3_t_ready")
    logits_read, coef2_step = sem("logits_read"), sem("coef2_step")
    dve_passed, pe_passed = sem("dve_passed"), sem("pe_passed")
    h2_kept, x3_kept, x3_t_kept = sem("h2_kept"), sem("x3_kept"), sem("x3_t_kept")

    qkv_raw = [v_nat[:].rearrange("p s e -> p (s e)")[:, 3 * EMB * i:3 * EMB * i + 3 * EMB] for i in range(2)]
    qkv_raw.append(u_t[:].rearrange("p c t -> p (c t)")[:, 0:3 * EMB])
    uv_raw = [t[:].rearrange("p q t -> p (q t)") for t in (base, rope_1, rope_2)]

    patch_weights = [(w_conv, d["w_conv"]), (b_conv, d["b_conv"])]
    weights = [(t, d["w_qkv"][:, i]) for i, t in enumerate(qkv_raw)] + [(t, d["w_uv"][:, i]) for i, t in enumerate(uv_raw)]
    weights += [
        (head_mask, d["head_mask"]),
        (w_o, d["w_o"]), (gamma, d["ln_gamma"]), (beta, d["ln_beta"]),
        (qk_gain, d["qk_gain"]), (qk_shift, d["qk_shift"]), (rope, d["rope"]), (rel_bias, d["rel_bias"]),
        (w_gau, d["w_gau"]), (w_route, d["w_route"]), (consts, d["consts"]),
    ]
    N_WEIGHTS = len(weights) + 1
    ALL_WEIGHTS = 16 * N_WEIGHTS
    N_FOLDS = 13
    N_CONST = 11

    def peeled(eng, first, both, last):
        first(0)
        with eng.Fori(1, G - 1) as g:
            both(g, True)
        both(G - 1, False)
        last(G - 1)

    def cut(j):
        return slice(P, EMB) if j else slice(0, P)

    def images(t):
        return t.rearrange("p (i n) -> p i n", n=L)

    def by_image(t):
        return t[:].rearrange("p q (i n) -> p q i n", n=L)

    def of_base(t):
        return t.rearrange("p (i n) -> p i n", n=L).unsqueeze(1).broadcast_to([P, 2, GT // L, L])

    def table(i):
        return rope_tab[:, i, :, :].unsqueeze(2).broadcast_to([P, 2, GT // L, L])

    def v_dest(half, i):
        t = v_ones[64 * i:64 * i + 64, 2 * half:2 * half + 2, :, i, :]
        return t.rearrange("p s a (h e) -> p (s a) h e", e=VH)[:, :, :, 0:HD]

    def v_src(half, i):
        t = psum[64 * i:64 * i + 64, half, 0:2 * EMB]
        return t.rearrange("p (a h e) -> p a h e", h=2, e=HD)

    def score_banks(s):
        return 2 - 2 * (s % 2)

    block = scope.enter_context(nc.Block())

    @block.sync
    def _(sp):
        sp.dma_start(patches[:], d["patches"][0]).then_inc(patches_in, 16)
        for tile, src in patch_weights:
            sp.dma_start(tile[:], src).then_inc(patch_weights_in, 16)
        for tile, src in weights:
            sp.dma_start(tile[:], src).then_inc(weights_in, 16)
        sp.dma_start(b_gau[:], d["b_gau"].broadcast_to([P, EMB])).then_inc(weights_in, 16)
        sp.dma_start(d["slot_rows"].rearrange("(s p) w -> s p w", p=P),
                     d["pad_rows"].unsqueeze(0).broadcast_to([SLOTS + 1, P, ROW])).then_inc(pads_in, 16)
        sp.dma_start(x3_all[:, :, EMB + 1:EMB + 2], d["token_ids"].unsqueeze(2),
                     allow_slow_non_contiguous=True).then_inc(pads_in, 16)

        def load_patches(g):
            sp.wait_ge(conv_done, 2 * g)
            sp.dma_start(patches[:], d["patches"][bass.ds(g, 1)].rearrange("a p c t -> p (a c) t")).then_inc(patches_in, 16)

        def store(g):
            sp.wait_ge(h2_ready, 2 * g + 2)
            sp.dma_start(d["h2"][bass.ds(g, 1)].rearrange("a p s e -> p (a s) e"), h2[:]).then_inc(h2_kept, 16)
            sp.wait_ge(x3_ready, SUB * g + SUB)
            sp.dma_start(x3_all[:, bass.ds(SUB * g, SUB), 0:EMB], x3[:]).then_inc(x3_kept, 16)
            sp.wait_ge(x3_t_ready, 2 * g + 2)
            for j, n in ((0, P), (1, TAIL)):
                sp.dma_start(d["x3t"][bass.ds(g, 1), 0:n, j, :].rearrange("a p t -> p (a t)"), x3_t[0:n, j, :]).then_inc(x3_t_kept, 16)

        def both(g, more):
            if more:
                load_patches(g + 1)
            store(g - 1)

        peeled(sp, lambda g: load_patches(1), both, store)
        sp.wait_ge(pads_in, 32)
        sp.wait_ge(h2_kept, 16 * G)
        sp.wait_ge(x3_kept, 16 * G)
        sp.wait_ge(x3_t_kept, 32 * G)

    @block.gpsimd
    def _(pool):
        cleared = [q_b[:], k_a[:], k_b[:], v_ones[:]]
        ones = [att_t[HC:HC + 1, :, 0, :]]
        ones += [v_ones[64 * i:64 * i + 64, :, :, i, HD::VH] for i in range(2)]
        for n, tile in enumerate(cleared + ones):
            pool.memset(tile, 0.0 if n < len(cleared) else 1.0).then_inc(const_ready, 1)
            pool.wait_ge(const_ready, n + 1)
        for n, (tile, value) in enumerate(((minus_half, -0.5), (eps, EPS), (one, 1.0), (minus_one, -1.0))):
            pool.memset(tile[:], value).then_inc(const_ready, 1)
            pool.wait_ge(const_ready, len(cleared + ones) + n + 1)

        for n, (rows, value) in enumerate(((slice(TAIL, REST), 0.0), (slice(TAIL, TAIL + 1), 1.0), (slice(REST - 1, REST), 1.0))):
            pool.memset(biased[rows], value).then_inc(rows_set, 1)
            pool.wait_ge(rows_set, n + 1)

        def coef1(g):
            pool.wait_ge(var1_ready, g + 1)
            if not isinstance(g, int) or g > 0:
                pool.wait_ge(xn_ready, SUB * g)
                pool.wait_ge(h1_plus_act, SUB * g)
            n = 7 * g

            def step(ins):
                nonlocal n
                n = n + 1
                ins.then_inc(coef_step, 1)
                pool.wait_ge(coef_step, n)

            mean, var = mean_var1[:, :, 0], mean_var1[:, :, 1]
            step(pool.tensor_tensor(coef[:, 1, :], coef[:, 0, :], minus_half[:], ALU.pow))
            step(pool.tensor_tensor(coef[:, 2, :], coef[:, 1, :], coef[:, 1, :], ALU.mult))
            step(pool.tensor_tensor(coef[:, 2, :], coef[:, 2, :], var, ALU.mult))
            step(pool.tensor_tensor(coef[:, 2, :], coef[:, 2, :], eps[:], ALU.add))
            step(pool.tensor_tensor(coef[:, 3, :], coef[:, 2, :], minus_half[:], ALU.pow))
            step(pool.tensor_tensor(coef[:, 4, :], mean, coef[:, 1, :], ALU.mult))
            step(pool.tensor_tensor(coef[:, 5, :], coef[:, 4, :], minus_one[:], ALU.mult))
            pool.tensor_tensor(coef[:, 6, :], coef[:, 1, :], one[:], ALU.add).then_inc(coef1_ready, 1)
            pool.tensor_tensor(coef[:, 7, :], coef[:, 1, :], coef[:, 3, :], ALU.mult).then_inc(coef1_ready, 1)

        def add_b_gau(g):
            pool.wait_ge(h1_plus_act, SUB * g + SUB)
            pool.tensor_tensor(h1_plus[:], h1_plus[:], b_gau[:].unsqueeze(1).broadcast_to([P, SUB, EMB]), ALU.add)\
                .then_inc(h1_plus_ready, 1)

        def rope_second(g):
            pool.wait_ge(fold_ready, N_FOLDS)
            pool.wait_ge(silu_ready, 9 * g + 2)
            least(pool, rope_ready, g)
            pool.tensor_tensor(by_image(rope_2), of_base(base[:, 1, :]), table(1), ALU.mult).then_inc(rope_2_half, 1)
            pool.wait_ge(rope_2_half, g + 1)
            pool.tensor_tensor(by_image(rope_2), by_image(rope_2), table(2), ALU.add).then_inc(rope_2_ready, 1)

        def coef2_of(g):
            pool.wait_ge(var2_ready, g + 1)
            least(pool, x3_ready, SUB * g)
            pool.tensor_tensor(coef2[:, 1, :], coef2[:, 0, :], minus_half[:], ALU.pow).then_inc(coef2_step, 1)
            pool.wait_ge(coef2_step, 2 * g + 1)
            pool.tensor_tensor(coef2[:, 2, :], coef2[:, 1, :], mean_var2[:, :, 0], ALU.mult).then_inc(coef2_step, 1)
            pool.wait_ge(coef2_step, 2 * g + 2)
            pool.tensor_tensor(coef2[:, 2, :], coef2[:, 2, :], minus_one[:], ALU.mult).then_inc(coef2_ready, 1)

        def both(g, more):
            add_b_gau(g - 1)
            coef1(g)
            coef2_of(g - 1)
            rope_second(g)

        def front(g):
            coef1(g)
            rope_second(g)

        def back(g):
            add_b_gau(g)
            coef2_of(g)

        pool.wait_ge(weights_in, ALL_WEIGHTS)
        peeled(pool, front, both, back)

    @block.scalar
    def _(act):
        def conv_out(g, j):
            act.wait_ge(conv_done, 2 * g + j + 1)
            least(act, v_done, 2 * g)
            for part in ([tok.hi[:]] if j == 0 else [tok.both[0:TAIL], tok.rest[0:TAIL]]):
                n = part.shape[0]
                act.activation(part, psum[0:n, j, :], ACT.Identity, bias=b_conv[0:n, j:j + 1]).then_inc(tok_hi, 1)

        def q_a_out(g):
            least(act, scores_done, SUB * g)
            act.wait_ge(qk_done, 3 * g + 1)
            for h in range(2):
                act.activation(q_a[:, :, h, :], images(psum[:, 2, :]), ACT.Copy, scale=head_mask[:, h:h + 1]).then_inc(qk_by_act, 1)

        def k_out(g):
            act.wait_ge(qk_done, 3 * g + 2)
            for a in range(2):
                act.activation(k_b[32 * a:32 * a + 32, a, :], psum[64 + 32 * a:96 + 32 * a, 3, :], ACT.Copy).then_inc(qk_by_act, 1)
            act.wait_ge(qk_done, 3 * g + 3)
            for a in range(2):
                act.activation(k_a[32 * a:32 * a + 32, a, :], psum[32 * a:32 * a + 32, 4, :], ACT.Copy).then_inc(qk_by_act, 1)

        def v_out(g, half):
            least(act, pv_done, SUB * g)
            act.wait_ge(v_done, 2 * g + half + 1)
            for i in range(2):
                act.activation(v_dest(half, i), v_src(half, i), ACT.Copy).then_inc(v_ready, 1)

        def exp(g, s):
            act.wait_ge(shifted, SUB * g + s + 1)
            x = probs[:, s % 2, :, :, :]
            act.activation(x, x, ACT.Exp).then_inc(exp_done, 1)

        def probs_t_out(g, s):
            act.wait_ge(probs_turned, SUB * g + s + 1)
            least(act, pv_done, SUB * g + s - 1)
            act.activation(probs_t[:, s % 2, 0:3, :], psum[:, score_banks(s), 0:384], ACT.Copy).then_inc(probs_t_act, 1)

        def att_t_out(g, s):
            act.wait_ge(att_turned, SUB * g + s + 1)
            least(act, proj_done, SUB * g + s - 1)
            act.activation(att_t[0:HC, s % 2, :, :].rearrange("p h (i q) -> p i h q", i=2),
                           psum[0:HC, 5, 0:2 * P].rearrange("p (i h q) -> p i h q", i=2, h=2), ACT.Copy)\
               .then_inc(att_t_ready, 1)

        def h1_out(g, s):
            act.wait_ge(proj_done, SUB * g + s + 1)
            least(act, xn_ready, SUB * g)
            least(act, h1_plus_act, SUB * g)
            act.activation(h1[:, s, :], psum[:, 5, 2 * P:2 * P + EMB], ACT.Copy).then_inc(h1_ready, 1)

        def residual(g):
            act.wait_ge(coef1_ready, 2 * g + 2)
            least(act, h2_ready, 2 * g)
            for s in range(SUB):
                act.activation(h1_plus[:, s, :], h1[:, s, :], ACT.Identity, scale=coef[:, 6, s:s + 1],
                               bias=coef[:, 5, s:s + 1]).then_inc(h1_plus_act, 1)

        def xn_t_out(g, j):
            act.wait_ge(xn_turned, 2 * g + j + 1)
            least(act, uv_done, 9 * g)
            for part in ([xn_t.hi[:]] if j == 0 else [xn_t.both[0:TAIL], xn_t.rest[0:TAIL]]):
                act.activation(part, psum[0:part.shape[0], 6 + j, :], ACT.Copy).then_inc(xn_hi, 1)

        def tanh_of(g, k):
            bank, cols = (6 + k % 2, 512) if k < 5 else (6 + k % 2, E_GAU)
            act.wait_ge(uv_done, 9 * g + k + 1)
            if k >= 3:
                act.wait_ge(silu_ready, 9 * g + k - 2)
            act.activation(tanh[:, k % 3, 0:cols], psum[:, bank, 0:cols], ACT.Tanh, scale=0.5).then_inc(tanh_ready, 1)

        def x3_t_out(g, j):
            act.wait_ge(x3_turned, 2 * g + j + 1)
            least(act, route_done, 2 * g)
            least(act, x3_t_kept, 32 * g)
            n = TAIL if j else P
            act.activation(x3_t[0:n, j, :], psum[0:n, 5, :], ACT.Copy).then_inc(x3_t_ready, 1)

        def x3_out(g):
            act.wait_ge(coef2_ready, g + 1)
            least(act, x3_kept, 16 * g)
            least(act, x3_turned, 2 * g)
            for s in range(SUB):
                act.activation(x3[:, s, :], h2[:, s, :], ACT.Identity, scale=coef2[:, 1, s:s + 1],
                               bias=coef2[:, 2, s:s + 1]).then_inc(x3_ready, 1)

        def front(g):
            exp(g, 2)
            att_t_out(g, 0)
            h1_out(g, 0)
            exp(g, 3)
            att_t_out(g, 1)
            probs_t_out(g, 2)
            h1_out(g, 1)
            probs_t_out(g, 3)
            act.wait_ge(fold_ready, 3)
            round_weights(act, w_uv, uv_raw, uv_hi)
            att_t_out(g, 2)
            h1_out(g, 2)
            conv_out(g + 1, 0)
            att_t_out(g, 3)
            h1_out(g, 3)
            conv_out(g + 1, 1)
            q_a_out(g + 1)
            xn_t_out(g, 0)
            xn_t_out(g, 1)
            k_out(g + 1)
            v_out(g + 1, 0)
            v_out(g + 1, 1)
            tanh_of(g, 0)
            exp(g + 1, 0)
            tanh_of(g, 1)
            exp(g + 1, 1)
            tanh_of(g, 2)
            probs_t_out(g + 1, 0)
            tanh_of(g, 3)
            probs_t_out(g + 1, 1)
            tanh_of(g, 4)

        def both(g, more):
            b = g - 1
            residual(b)
            exp(g, 2)
            att_t_out(g, 0)
            tanh_of(b, 5)
            h1_out(g, 0)
            att_t_out(g, 1)
            exp(g, 3)
            tanh_of(b, 6)
            h1_out(g, 1)
            probs_t_out(g, 2)
            tanh_of(b, 7)
            probs_t_out(g, 3)
            tanh_of(b, 8)
            att_t_out(g, 2)
            h1_out(g, 2)
            att_t_out(g, 3)
            if more:
                conv_out(g + 1, 0)
            h1_out(g, 3)
            if more:
                conv_out(g + 1, 1)
            xn_t_out(g, 0)
            xn_t_out(g, 1)
            if more:
                q_a_out(g + 1)
                k_out(g + 1)
                v_out(g + 1, 0)
                v_out(g + 1, 1)
            tanh_of(g, 0)
            x3_out(b)
            if more:
                exp(g + 1, 0)
            tanh_of(g, 1)
            x3_t_out(b, 0)
            if more:
                exp(g + 1, 1)
            tanh_of(g, 2)
            x3_t_out(b, 1)
            if more:
                probs_t_out(g + 1, 0)
            tanh_of(g, 3)
            if more:
                probs_t_out(g + 1, 1)
            tanh_of(g, 4)

        def back(g):
            residual(g)
            for k in range(5, 9):
                tanh_of(g, k)
            x3_out(g)
            x3_t_out(g, 0)
            x3_t_out(g, 1)

        act.wait_ge(patch_weights_in, 32)
        act.wait_ge(weights_in, ALL_WEIGHTS)
        act.wait_ge(const_ready, N_CONST)
        round_weights(act, w_qkv, qkv_raw, qkv_hi)
        act.wait_ge(rows_set, 3)
        for t in (tok, xn_t):
            act.activation(t.rest[TAIL:REST], biased[TAIL:REST].rearrange("p s n -> p (s n)"), ACT.Copy).then_inc(rows_copied, 1)
        conv_out(0, 0)
        conv_out(0, 1)
        q_a_out(0)
        k_out(0)
        v_out(0, 0)
        v_out(0, 1)
        exp(0, 0)
        exp(0, 1)
        probs_t_out(0, 0)
        probs_t_out(0, 1)
        peeled(act, front, both, back)

    @block.tensor
    def _(pe):
        def mm(out, lhs, rhs, start, stop):
            return pe.matmul(out, lhs, rhs, start=start, stop=stop)

        def conv(g, j, chunks=(0, KP)):
            if chunks[0] == 0:
                pe.wait_ge(patches_in, 16 * (g + 1))
                least(pe, probs_t_act, SUB * g)
                least(pe, probs_t_dve, SUB * g)
            for c in range(*chunks):
                m = mm(psum[0:(TAIL if j else P), j, :], w_conv[:, c, cut(j)], patches[:, c, :], c == 0, c == KP - 1)
            if chunks[1] == KP:
                m.then_inc(conv_done, 1)

        def two(out, lhs, rhs):
            mm(out, lhs(HC + 1, 0), rhs(HC + 1, 0), True, False)
            return mm(out, lhs(HC, 1), rhs(HC, 1), False, True)

        def qk(g, m):
            pe.wait_ge(tok_hi, 3 * g + 3)
            pe.wait_ge(tok_lo, 2 * g + 2)
            if m < 2:
                least(pe, probs_t_act, SUB * g - 1)
                least(pe, probs_t_dve, SUB * g - 1)
            else:
                least(pe, att_ready, 2 * SUB * g)
            product(pe, psum[:, 2 + m, :], w_qkv.weights(slice(P * m, P * m + P)), tok.activations(slice(0, GT))).then_inc(qk_done, 1)

        def v(g, half):
            for s in range(2):
                t = P * (2 * half + s)
                m = product(pe, psum[:, half, EMB * s:EMB * s + EMB], tok.activations(slice(t, t + P)),
                            w_qkv.weights(slice(2 * EMB, 3 * EMB)))
            m.then_inc(v_done, 1)

        def scores(g, s):
            pe.wait_ge(qk_by_act, 6 * g + 6)
            pe.wait_ge(qk_by_dve, 4 * g + 4)
            if s == 1:
                pe.wait_ge(v_ready, 4 * g + 4)
            if s >= 2:
                pe.wait_ge(probs_t_act, SUB * g + s - 1)
                pe.wait_ge(probs_t_dve, SUB * g + s - 1)
            for i in range(2):
                t = slice(P * s + L * i, P * s + L * i + L)
                out = psum[:, score_banks(s) + i, :]
                mm(out[:, 0:4 * L], q_a[:, 2 * s + i].rearrange("p h q -> p (h q)"), k_a[:, :, t], True, True)
                m = mm(out[:, 4 * L:6 * L], q_b[:, 2 * s + i].rearrange("p h q -> p (h q)"), k_b[:, :, t], True, True)
            m.then_inc(scores_done, 1)

        def turn_probs(g, s):
            pe.wait_ge(exp_done, SUB * g + s + 1)
            for a in range(PAIRS):
                out = psum[:, score_banks(s) + a // 3, P * (a % 3):P * (a % 3) + P]
                m = pe.transpose(out, probs[:, s % 2, a].rearrange("p i k -> p (i k)"), ident)
            m.then_inc(probs_turned, 1)

        def pv(g, s):
            pe.wait_ge(probs_t_act, SUB * g + s + 1)
            pe.wait_ge(probs_t_dve, SUB * g + s + 1)
            if s > 0:
                pe.wait_ge(att_ready, 2 * (SUB * g + s))
            for a in range(PAIRS):
                m = mm(psum[:, 4, 4 * VH * a:4 * VH * a + 4 * VH], probs_t[:, s % 2, a, :],
                       v_ones[:, s, a, :, :].rearrange("p i e -> p (i e)"), True, True)
            m.then_inc(pv_done, 1)

        def turn_att(g, s):
            pe.wait_ge(att_ready, 2 * (SUB * g + s + 1))
            least(pe, h1_ready, SUB * g + s)
            if s == 0:
                least(pe, logits_read, g - 1)
            for i in range(2):
                m = pe.transpose(psum[0:HC, 5, P * i:P * i + P], att[:, s % 2, i, :, :].rearrange("p a e -> p (a e)"), ident)
            m.then_inc(att_turned, 1)

        def proj(g, s):
            pe.wait_ge(att_t_ready, SUB * g + s + 1)
            two(psum[:, 5, 2 * P:2 * P + EMB], lambda k, j: att_t[0:k, s % 2, j, :], lambda k, j: w_o[0:k, j, :]).then_inc(proj_done, 1)

        def turn_xn(g, j):
            pe.wait_ge(xn_ready, SUB * g + SUB)
            if j == 0:
                least(pe, gated_ready, EC * g)
            else:
                least(pe, h2_ready, 2 * g - 1)
            if j:
                apart(pe, pe_passed)
            for s in range(SUB):
                m = pe.transpose(psum[0:(TAIL if j else P), 6 + j, P * s:P * s + P], xn[:, s, cut(j)], ident)
            m.then_inc(xn_turned, 1)

        def uv(g, k):
            pe.wait_ge(xn_hi, 3 * g + 3)
            pe.wait_ge(xn_lo, 2 * g + 2)
            if k < 2:
                least(pe, h2_ready, 2 * g)
            if k == 7:
                pe.wait_ge(biased_ready, g + 1)
            elif k >= 2:
                pe.wait_ge(silu_ready, 9 * g + k - 1)
            if k < 5:
                col = 2 * E_GAU + P * k if k < 2 else P * (k - 2)
                m = product(pe, psum[:, 6 + k % 2, :], w_uv.weights(slice(col, col + P)), xn_t.activations(slice(0, GT)))
            else:
                t = P * (k - 5)
                m = product(pe, psum[:, 6 + k % 2, 0:E_GAU], xn_t.activations(slice(t, t + P)), w_uv.weights(slice(E_GAU, 2 * E_GAU)))
            m.then_inc(uv_done, 1)

        def gqk(g):
            pe.wait_ge(rope_ready, g + 1)
            pe.wait_ge(silu_ready, 9 * g + 6)
            for s in range(SUB):
                t = slice(P * s, P * s + P)
                m = mm(psum[:, 7, t], qk_t[:, 1, t], qk_t[:, 0, t], True, True)
            m.then_inc(gqk_done, 1)

        def kv(g, c):
            pe.wait_ge(kern_ready, g + 1)
            pe.wait_ge(silu_ready, 9 * g + 9)
            if c == 2:
                pe.wait_ge(gated_ready, EC * g + 1)
            for s in range(SUB):
                t = slice(P * s, P * s + P)
                m = mm(psum[:, 6 + c % 2, t], v_nat[:, s, P * c:P * c + P], biased[:, s, :], True, True)
            m.then_inc(kv_done, 1)

        def gau(g, half, xn_count):
            pe.wait_ge(gated_ready, EC * g + EC)
            least(pe, xn_hi, xn_count[0])
            least(pe, xn_lo, xn_count[1])
            for s in (2 * half, 2 * half + 1):
                for c in range(EC):
                    m = mm(psum[:, 7 - half, EMB * (s % 2):EMB * (s % 2) + EMB], gated[:, c, P * s:P * s + P],
                           w_gau[:, c, :], c == 0, c == EC - 1)
            m.then_inc(gau_done, 1)

        def turn_x3(g, j, h1_count):
            pe.wait_ge(x3_ready, SUB * g + SUB)
            if j == 0:
                pe.wait_ge(h1_ready, h1_count)
            else:
                pe.wait_ge(x3_t_ready, 2 * g + 1)
            if j:
                apart(pe, pe_passed)
            for s in range(SUB):
                t = slice(P * s, P * s + P)
                m = pe.transpose(psum[0:(TAIL if j else P), 5, t], x3[:, s, cut(j)], ident)
            m.then_inc(x3_turned, 1)

        def route(g, subtiles):
            pe.wait_ge(x3_t_ready, 2 * g + 2)
            for s in subtiles:
                for j in range(2):
                    k = TAIL if j else P
                    m = mm(psum[:, 5, NE * s:NE * s + NE], x3_t[0:k, j, P * s:P * s + P], w_route[0:k, j, :], j == 0, j == 1)
            m.then_inc(route_done, 1)

        def front(g):
            turn_att(g, 0)
            scores(g, 3)
            proj(g, 0)
            turn_att(g, 1)
            turn_probs(g, 2)
            proj(g, 1)
            pv(g, 2)
            turn_probs(g, 3)
            turn_att(g, 2)
            conv(g + 1, 0, (0, 3))
            pv(g, 3)
            proj(g, 2)
            conv(g + 1, 0, (3, 6))
            turn_att(g, 3)
            conv(g + 1, 1, (0, 2))
            proj(g, 3)
            conv(g + 1, 1, (2, 6))
            qk(g + 1, 0)
            qk(g + 1, 1)
            turn_xn(g, 0)
            turn_xn(g, 1)
            qk(g + 1, 2)
            v(g + 1, 0)
            v(g + 1, 1)
            pe.wait_ge(uv_hi, 3)
            pe.wait_ge(uv_lo, 3)
            uv(g, 0)
            scores(g + 1, 0)
            uv(g, 1)
            scores(g + 1, 1)
            uv(g, 2)
            turn_probs(g + 1, 0)
            uv(g, 3)
            turn_probs(g + 1, 1)
            pv(g + 1, 0)
            uv(g, 4)
            scores(g + 1, 2)
            pv(g + 1, 1)

        def both(g, more):
            b = g - 1
            turn_att(g, 0)
            uv(b, 5)
            scores(g, 3)
            proj(g, 0)
            gqk(b)
            turn_att(g, 1)
            uv(b, 6)
            proj(g, 1)
            turn_probs(g, 2)
            uv(b, 7)
            pv(g, 2)
            turn_probs(g, 3)
            uv(b, 8)
            turn_att(g, 2)
            if more:
                conv(g + 1, 0, (0, 2))
            kv(b, 0)
            pv(g, 3)
            proj(g, 2)
            if more:
                conv(g + 1, 0, (2, 4))
            kv(b, 1)
            turn_att(g, 3)
            kv(b, 2)
            if more:
                conv(g + 1, 0, (4, 6))
            proj(g, 3)
            if more:
                conv(g + 1, 1)
            gau(b, 0, (0, 0))
            if more:
                qk(g + 1, 0)
                qk(g + 1, 1)
            turn_xn(g, 0)
            turn_xn(g, 1)
            if more:
                qk(g + 1, 2)
            if more:
                v(g + 1, 0)
            gau(b, 1, (3 * g + 1, 2 * g + 1))
            if more:
                v(g + 1, 1)
            uv(g, 0)
            if more:
                scores(g + 1, 0)
            uv(g, 1)
            if more:
                scores(g + 1, 1)
            turn_x3(b, 0, SUB * g + SUB)
            uv(g, 2)
            if more:
                turn_probs(g + 1, 0)
            turn_x3(b, 1, 0)
            uv(g, 3)
            if more:
                turn_probs(g + 1, 1)
            uv(g, 4)
            if more:
                pv(g + 1, 0)
            route(b, (0, 1))
            if more:
                scores(g + 1, 2)
            route(b, (2, 3))
            if more:
                pv(g + 1, 1)

        def back(g):
            uv(g, 5)
            gqk(g)
            for k in range(6, 9):
                uv(g, k)
            for c in range(EC):
                kv(g, c)
            gau(g, 0, (0, 0))
            gau(g, 1, (0, 0))
            turn_x3(g, 0, SUB * g + SUB)
            turn_x3(g, 1, 0)
            route(g, (0, 1))
            route(g, (2, 3))

        pe.wait_ge(patch_weights_in, 32)
        conv(0, 0)
        conv(0, 1)
        pe.wait_ge(weights_in, ALL_WEIGHTS)
        pe.wait_ge(const_ready, N_CONST)
        for n in range(2):
            for j in range(2):
                k = TAIL if j else P
                m = mm(psum[0:REST, 6 + n, :], beta[0:k, j, :], uv_raw[j][0:k, 512 * n:512 * n + 512], j == 0, j == 1)
        m.then_inc(fold_done, 1)
        pe.wait_ge(qkv_hi, 3)
        pe.wait_ge(qkv_lo, 3)
        pe.wait_ge(rows_copied, 2)
        for m in range(3):
            qk(0, m)
        v(0, 0)
        v(0, 1)
        scores(0, 0)
        scores(0, 1)
        turn_probs(0, 0)
        turn_probs(0, 1)
        pv(0, 0)
        scores(0, 2)
        pv(0, 1)
        peeled(pe, front, both, back)

    @block.vector
    def _(dve):
        def fold(ins, n):
            ins.then_inc(fold_ready, 1)
            dve.wait_ge(fold_ready, n)

        def prepare():
            dve.wait_ge(rows_copied, 2)
            dve.wait_ge(fold_done, 1)
            fold(dve.tensor_scalar(uv_raw[0], uv_raw[0], gamma[:, 0:1], None, ALU.mult), 1)
            fold(dve.tensor_scalar(uv_raw[1], uv_raw[1], gamma[:, 1:2], None, ALU.mult), 2)
            raw = uv_raw[2][0:REST].rearrange("p (a b) -> p a b", a=2)
            fold(dve.scalar_tensor_tensor(raw, raw, gamma[0:REST, 2:3], psum[0:REST, 6:8, :], ALU.mult, ALU.add), 3)
            for q in range(2):
                fold(dve.tensor_scalar(rope_tab[:, 0, q, :], rope[:, 0, :], qk_gain[:, q, 0:1], 0.5, ALU.mult, ALU.mult), 5 * q + 4)
                fold(dve.tensor_scalar(rope_tab[:, 1, q, :], rope[:, 1, :], qk_gain[:, q, 1:2], 0.5, ALU.mult, ALU.mult), 5 * q + 5)
                fold(dve.tensor_scalar(rope_tab[:, 2, q, :], rope[:, 0, :], qk_shift[:, q, 0:1], None, ALU.mult), 5 * q + 6)
                fold(dve.tensor_scalar(biased[:, q, 0:L], rope[:, 1, :], qk_shift[:, q, 1:2], None, ALU.mult), 5 * q + 7)
                fold(dve.tensor_tensor(rope_tab[:, 2, q, :], rope_tab[:, 2, q, :], biased[:, q, 0:L], ALU.add), 5 * q + 8)
            dve.wait_ge(uv_hi, 3)
            rest_of_weights(dve, w_uv, uv_raw, uv_lo)

        def tok_lo_out(g, j):
            dve.wait_ge(tok_hi, 3 * g + (3 if j else 1))
            least(dve, v_done, 2 * g)
            hi, lo = (tok.both[0:TAIL], tok.both[TAIL:P]) if j else (tok.hi[:], tok.lo[:])
            n = hi.shape[0]
            dve.scalar_tensor_tensor(lo, psum[0:n, j, :], b_conv[0:n, j:j + 1], hi.bitcast(F32), ALU.add, ALU.subtract).then_inc(tok_lo, 1)

        def xn_lo_out(g, j):
            dve.wait_ge(xn_hi, 3 * g + (3 if j else 1))
            least(dve, uv_done, 9 * g)
            hi, lo = (xn_t.both[0:TAIL], xn_t.both[TAIL:P]) if j else (xn_t.hi[:], xn_t.lo[:])
            dve.tensor_tensor(lo, psum[0:hi.shape[0], 6 + j, :], hi.bitcast(F32), ALU.subtract).then_inc(xn_lo, 1)

        def qk_out(g):
            least(dve, scores_done, SUB * g)
            dve.wait_ge(qk_done, 3 * g + 2)
            for h in range(2):
                dve.tensor_scalar(q_b[0:64, :, h, :], images(psum[0:64, 3, :]), head_mask[0:64, h:h + 1], None, ALU.mult).then_inc(qk_by_dve, 1)
            dve.wait_ge(qk_done, 3 * g + 3)
            for a in range(2, 4):
                dve.tensor_copy(k_a[32 * a:32 * a + 32, a, :], psum[32 * a:32 * a + 32, 4, :]).then_inc(qk_by_dve, 1)

        def shift(g, s):
            dve.wait_ge(scores_done, SUB * g + s + 1)
            x = psum[:, score_banks(s):score_banks(s) + 2, 0:PAIRS * L].rearrange("p i (a k) -> p i a k", k=L)
            top = row_max[:, s % 2, :, :]
            dve.tensor_reduce(top, x, AX.X, ALU.max).then_inc(max_ready, 1)
            dve.wait_ge(max_ready, SUB * g + s + 1)
            least(dve, probs_turned, SUB * g + s - 1)
            dve.tensor_tensor(probs[:, s % 2].rearrange("p a i k -> p i a k"), x, top.unsqueeze(3).broadcast_to([P, 2, PAIRS, L]), ALU.subtract)\
                .then_inc(shifted, 1)

        def probs_t_out(g, s):
            dve.wait_ge(probs_turned, SUB * g + s + 1)
            least(dve, pv_done, SUB * g + s - 1)
            dve.tensor_copy(probs_t[:, s % 2, 3:6, :].rearrange("p a q -> p (a q)"), psum[:, score_banks(s) + 1, 0:384]).then_inc(probs_t_dve, 1)

        def normalise(g, s):
            dve.wait_ge(pv_done, SUB * g + s + 1)
            least(dve, att_turned, SUB * g + s - 1)
            o = psum[:, 4, 0:PAIRS * 4 * VH].rearrange("p (a i e) -> p a i e", i=2, e=2 * VH)
            for h in range(2):
                r = slice(64 * h, 64 * h + 64)
                dve.reciprocal(inv_sum[r, s % 2, :, :], o[r, :, :, VH * h + HD]).then_inc(inv_ready, 1)
            dve.wait_ge(inv_ready, 2 * (SUB * g + s + 1))
            for h in range(2):
                r = slice(64 * h, 64 * h + 64)
                dve.tensor_tensor(att[r, s % 2, :, :, :].rearrange("p i a e -> p a i e"), o[r, :, :, VH * h:VH * h + HD],
                                  inv_sum[r, s % 2, :, :].unsqueeze(3).broadcast_to([64, PAIRS, 2, HD]), ALU.mult)\
                   .then_inc(att_ready, 1)

        def moments1(g, s):
            dve.wait_ge(h1_ready, SUB * g + s + 1)
            if s == 0 and (not isinstance(g, int) or g > 0):
                dve.wait_ge(coef1_ready, 2 * g)
            dve.bn_stats(stats1[:, s, :], h1[:, s, :]).then_inc(stat_step, 1)

        def moments1_end(g, stat_base):
            dve.wait_ge(stat_step, stat_base + 4)
            apart(dve, dve_passed)
            for s in range(SUB):
                ins = dve.bn_aggr(mean_var1[:, s, :], stats1[:, s, :]).then_inc(stat_step, 1)
            dve.wait_ge(stat_step, stat_base + 8)
            dve.tensor_scalar(coef[:, 0, :], mean_var1[:, :, 1], EPS, None, ALU.add).then_inc(var1_ready, 1)

        def xn_out(g):
            dve.wait_ge(coef1_ready, 2 * g + 2)
            least(dve, xn_turned, 2 * g)
            for s in range(SUB):
                dve.tensor_scalar(xn[:, s, :], h1[:, s, :], mean_var1[:, s, 0:1], coef[:, 7, s:s + 1],
                                  ALU.subtract, ALU.mult).then_inc(xn_ready, 1)

        def silu(g, k):
            bank, cols = (6 + k % 2, 512) if k < 5 else (6 + k % 2, E_GAU)
            dve.wait_ge(tanh_ready, 9 * g + k + 1)
            if k == 1:
                least(dve, rope_2_half, g)
            if k == 5:
                least(dve, kv_done, EC * g)
            dest = base[:, k, :] if k < 2 else u_t[:, k - 2, :] if k < 5 else v_nat[:, k - 5, :]
            dve.scalar_tensor_tensor(dest, tanh[:, k % 3, 0:cols], 1.0, psum[:, bank, 0:cols], ALU.add, ALU.mult)\
               .then_inc(silu_ready, 1)

        def rope_first(g):
            dve.wait_ge(silu_ready, 9 * g + 1)
            dve.tensor_tensor(by_image(rope_1), of_base(base[:, 0, :]), table(0), ALU.mult).then_inc(rope_1_ready, 1)

        def rope_out(g):
            dve.wait_ge(rope_1_ready, g + 1)
            dve.wait_ge(rope_2_ready, g + 1)
            least(dve, gqk_done, g)
            dve.tensor_tensor(qk_t[:], rope_1[:], rope_2[:], ALU.add).then_inc(rope_ready, 1)

        def kern_out(g):
            dve.wait_ge(gqk_done, g + 1)
            least(dve, kv_done, EC * g)
            dve.scalar_tensor_tensor(biased[:], psum[:, 7, :].rearrange("p (s n) -> p s n", n=P), 1.0 / L,
                                     rel_bias[:].unsqueeze(1).broadcast_to([P, SUB, P]), ALU.mult, ALU.add).then_inc(biased_ready, 1)
            dve.wait_ge(biased_ready, g + 1)
            dve.scalar_tensor_tensor(biased[:], biased[:], 0.0, biased[:], ALU.max, ALU.mult).then_inc(kern_ready, 1)

        def gate_out(g, c):
            dve.wait_ge(kv_done, EC * g + c + 1)
            least(dve, gau_done, 2 * g)
            dve.scalar_tensor_tensor(gated[:, c, :], u_t[:, c, :], 0.25, psum[:, 6 + c % 2, :], ALU.mult, ALU.mult)\
               .then_inc(gated_ready, 1)

        def h2_out(g, half):
            dve.wait_ge(gau_done, 2 * g + half + 1)
            dve.wait_ge(h1_plus_ready, g + 1)
            least(dve, h2_kept, 16 * g)
            s = slice(2 * half, 2 * half + 2)
            dve.tensor_tensor(h2[:, s, :], psum[:, 7 - half, 0:2 * EMB].rearrange("p (s e) -> p s e", e=EMB),
                              h1_plus[:, s, :], ALU.add).then_inc(h2_ready, 1)

        def moments2(g, stat_base):
            dve.wait_ge(h2_ready, 2 * g + 2)
            least(dve, coef2_ready, g)
            for s in range(SUB):
                dve.bn_stats(stats2[:, s, :], h2[:, s, :]).then_inc(stat_step, 1)
            dve.wait_ge(stat_step, stat_base + 4)
            apart(dve, dve_passed)
            for s in range(SUB):
                dve.bn_aggr(mean_var2[:, s, :], stats2[:, s, :]).then_inc(stat_step, 1)
            dve.wait_ge(stat_step, stat_base + 8)
            dve.tensor_scalar(coef2[:, 0, :], mean_var2[:, :, 1], EPS, None, ALU.add).then_inc(var2_ready, 1)

        def logits_out(g):
            dve.wait_ge(route_done, 2 * g + 2)
            dve.tensor_copy(logits_all[:, bass.ds(SUB * g, SUB), :], psum[:, 5, 0:SUB * NE].rearrange("p (s e) -> p s e", e=NE)).then_inc(logits_read, 1)

        def front(g):
            normalise(g, 1)
            shift(g, 3)
            probs_t_out(g, 2)
            normalise(g, 2)
            probs_t_out(g, 3)
            prepare()
            normalise(g, 3)
            for s in range(SUB):
                moments1(g, s)
            moments1_end(g, 0)
            tok_lo_out(g + 1, 0)
            xn_out(g)
            tok_lo_out(g + 1, 1)
            xn_lo_out(g, 0)
            xn_lo_out(g, 1)
            qk_out(g + 1)
            silu(g, 0)
            shift(g + 1, 0)
            silu(g, 1)
            shift(g + 1, 1)
            silu(g, 2)
            probs_t_out(g + 1, 0)
            silu(g, 3)
            probs_t_out(g + 1, 1)
            normalise(g + 1, 0)
            rope_first(g)
            silu(g, 4)
            shift(g + 1, 2)

        def both(g, more):
            b = g - 1
            normalise(g, 1)
            rope_out(b)
            silu(b, 5)
            shift(g, 3)
            kern_out(b)
            silu(b, 6)
            probs_t_out(g, 2)
            silu(b, 7)
            normalise(g, 2)
            probs_t_out(g, 3)
            silu(b, 8)
            gate_out(b, 0)
            normalise(g, 3)
            gate_out(b, 1)
            gate_out(b, 2)
            for s in range(SUB):
                moments1(g, s)
            moments1_end(g, 16 * g - 8)
            if more:
                tok_lo_out(g + 1, 0)
            if more:
                tok_lo_out(g + 1, 1)
            xn_out(g)
            h2_out(b, 0)
            xn_lo_out(g, 0)
            xn_lo_out(g, 1)
            if more:
                qk_out(g + 1)
            h2_out(b, 1)
            moments2(b, 16 * g)
            silu(g, 0)
            if more:
                shift(g + 1, 0)
            silu(g, 1)
            if more:
                shift(g + 1, 1)
            silu(g, 2)
            if more:
                probs_t_out(g + 1, 0)
            silu(g, 3)
            if more:
                probs_t_out(g + 1, 1)
                normalise(g + 1, 0)
            rope_first(g)
            silu(g, 4)
            logits_out(b)
            if more:
                shift(g + 1, 2)

        def back(g):
            rope_out(g)
            silu(g, 5)
            kern_out(g)
            for k in range(6, 9):
                silu(g, k)
            for c in range(EC):
                gate_out(g, c)
            h2_out(g, 0)
            h2_out(g, 1)
            moments2(g, 16 * g + 8)
            logits_out(g)

        dve.wait_ge(patch_weights_in, 32)
        dve.wait_ge(weights_in, ALL_WEIGHTS)
        dve.wait_ge(const_ready, N_CONST)
        dve.wait_ge(qkv_hi, 3)
        rest_of_weights(dve, w_qkv, qkv_raw, qkv_lo)
        tok_lo_out(0, 0)
        tok_lo_out(0, 1)
        qk_out(0)
        shift(0, 0)
        shift(0, 1)
        probs_t_out(0, 0)
        probs_t_out(0, 1)
        normalise(0, 0)
        shift(0, 2)
        peeled(dve, front, both, back)
        dve.wait_ge(logits_read, G)


def experts(nc, d, scope, psum, w2, x3_all, logits_all, consts, ident):
    def sb(name, shape, dt=F32):
        return scope.enter_context(nc.sbuf_tensor(name, shape, dt))

    def sem(name):
        return scope.enter_context(nc.semaphore(name))

    tri = consts[:, P:2 * P]
    experts_iota = consts[:, 2 * P:2 * P + NE]
    slot_starts = consts[:, 2 * P + NE:2 * P + NE + SLOTS]
    w1 = Packed(sb, "w1", NE * HID)
    b2 = sb("b2_sb", [P, NE, EMB])
    ws1 = Packed(sb, "ws1", HID)
    ws2_hi = sb("ws2_hi", [P, HK, EMB], F32R)
    ws2_lo = sb("ws2_lo", [P, HK, EMB], F32R)
    h_slot_t = sb("h_slot_t", [P, 2, HK, P])
    y_slot = sb("y_slot", [P, 2, 2, EMB])
    w2_flat = w2[:].rearrange("p e c n -> p (e c n)")
    ws1_raw = [w2_flat[:, NT * ROW + HID * i:NT * ROW + HID * i + HID] for i in range(3)]
    h_slot_t_flat = h_slot_t[:].rearrange("p q c t -> p (q c t)")
    ws2_raw = h_slot_t_flat[:, 0:HK * EMB].rearrange("p (c n) -> p c n", n=EMB)
    w1_raw = [h_slot_t_flat[:, 0:HID], h_slot_t_flat[:, HID:2 * HID], y_slot[:].rearrange("p q k e -> p (q k e)")]
    bs2 = sb("bs2_sb", [P, EMB])
    x3_in = sb("x3_in", [P, 2, HT])
    x3_t = Packed(sb, "x3_t", HT)
    hs_hi = sb("hs_hi", [P, HK, HT], F32R)
    hs_lo = sb("hs_lo", [P, HK, HT], F32R)
    ones = sb("ones", [P, P])
    chosen = sb("chosen", [P, TOPK, NT, NE])
    mask = sb("mask", [P, NT, NE])
    running = sb("running", [P, 2, NT, NE])
    place = sb("place", [P, NT, NE])
    rows_f = sb("rows_f", [P, TOPK, NT])
    rows = sb("rows", [P, TOPK, NT], U32)
    top = sb("top", [P, TOPK, NT])
    at_expert = sb("at_expert", [P, NT])
    gap = sb("gap", [P, NT])
    gate = sb("gate", [P, 3, NT])
    padded_i = sb("padded_i", [P, NE], I32)
    padded = sb("padded", [P, NE])
    ends = sb("ends", [P, 2, NE])
    starts = sb("starts", [P, NE])
    past = sb("past", [1, (SLOTS + 1) // 2, NE])
    slot_expert_f = sb("slot_expert_f", [1, SLOTS])
    slot_expert = sb("slot_expert", [1, SLOTS], I32)
    meta = sb("meta", [P, SLOTS + 1, 2])
    x_slot = sb("x_slot", [P, 2, ROW])
    h_slot = sb("h_slot", [P, 2, HID])
    h2_in = h_slot[:, 0, 0:HS * EMB].rearrange("p (s e) -> p s e", e=EMB)
    out_rows = h_slot[:, 1, 0:HS * EMB].rearrange("p (s e) -> p s e", e=EMB)
    tokens = sb("tokens", [P, 2], U32)

    x3t_in, shared_in, b2_in, w2_in, h2_loaded = sem("x3t_in"), sem("shared_in"), sem("b2_in"), sem("w2_in"), sem("h2_loaded")
    shared_hi, shared_lo, rows_copied, bias_scaled = sem("shared_hi"), sem("shared_lo"), sem("rows_copied"), sem("bias_scaled")
    x_hi, x_lo, hs_done, hs_hi_ready, hs_lo_ready = sem("x_hi"), sem("x_lo"), sem("hs_done"), sem("hs_hi_ready"), sem("hs_lo_ready")
    ys_done, h2_plus, shared_ready, out_stored = sem("ys_done"), sem("h2_plus"), sem("shared_ready"), sem("out_stored")
    ones_ready, mask_ready, ranks_done, route_step = sem("ones_ready"), sem("mask_ready"), sem("ranks_done"), sem("route_step")
    gates_ready = sem("gates_ready")
    gap_ready, gap_exp, table_ready = sem("gap_ready"), sem("gap_exp"), sem("table_ready")
    rows_ready, gate_set, dispatched = sem("rows_ready"), sem("gate_set"), sem("dispatched")
    meta_ready = sem("meta_ready")
    x_slot_in = [sem("x_slot_in0"), sem("x_slot_in1")]
    x_turned, x_t_hi, x_t_lo = sem("x_turned"), sem("x_t_hi"), sem("x_t_lo")
    w1_raw_in, w1_hi, w1_lo = sem("w1_raw_in"), sem("w1_hi"), sem("w1_lo")
    h_done, h_by_act, h_by_dve = sem("h_done"), sem("h_by_act"), sem("h_by_dve")
    h_turned, h_t_by_act, h_t_by_dve = sem("h_turned"), sem("h_t_by_act"), sem("h_t_by_dve")
    y_done, y_plain_ready, y_ready = sem("y_done"), sem("y_plain_ready"), sem("y_ready")
    tokens_ready, added, pool_passed = sem("tokens_ready"), sem("added"), sem("pool_passed")
    HALF = HID // 2
    SHARED_LOADS = 16 * 5
    HALVES = 2 * G

    def expert_part(tile, e):
        return tile[:, HID * e:HID * e + HID] if isinstance(e, int) else tile[:, bass.ds(HID * e, HID)]

    def groups(eng, body):
        body(0, True)
        with eng.Fori(1, G - 1) as g:
            body(g, True)
        body(G - 1, False)

    def slots(eng, step):
        assert (SLOTS - 3) % 4 == 0
        step(1, 1, 0)
        step(2, 0, 1)
        with eng.Fori(0, (SLOTS - 3) // 4) as i:
            step(4 * i + 3, 1, 2 * i + 1)
            step(4 * i + 4, 0, 2 * i + 2)
            step(4 * i + 5, 1, 2 * i + 2)
            step(4 * i + 6, 0, 2 * i + 3)

    block = scope.enter_context(nc.Block())

    @block.sync
    def _(sp):
        def load_x3(g, half):
            t = slice(HT * half, HT * half + HT)
            for j, n in ((0, P), (1, TAIL)):
                sp.dma_start(x3_in[0:n, j, :], d["x3t"][bass.ds(g, 1), 0:n, j, t].rearrange("a p t -> p (a t)")).then_inc(x3t_in, 16)

        def load_h2(g, half):
            sp.dma_start(h2_in, d["h2"][bass.ds(g, 1), :, HS * half:HS * half + HS, :].rearrange("a p s e -> p (a s) e")).then_inc(h2_loaded, 16)

        def load_w1(e):
            for i, t in enumerate(w1_raw):
                sp.dma_start(t, d["w1"][bass.ds(e, 1), :, i, :].rearrange("a p n -> p (a n)")).then_inc(w1_raw_in, 16)

        load_x3(0, 0)
        for i, t in enumerate(ws1_raw):
            sp.dma_start(t, d["ws1"][:, i]).then_inc(shared_in, 16)
        sp.dma_start(ws2_raw, d["ws2"]).then_inc(shared_in, 16)
        sp.dma_start(bs2[:], d["bs2"].broadcast_to([P, EMB])).then_inc(shared_in, 16)
        load_h2(0, 0)
        sp.dma_start(b2[:].rearrange("p e n -> p (e n)"), d["b2"].broadcast_to([P, NE * EMB])).then_inc(b2_in, 16)

        def half_group(g, half, more):
            h = 2 * g + half
            after = (g, 1) if half == 0 else (g + 1, 0)
            if more:
                sp.wait_ge(x_hi, 3 * h + 3)
                sp.wait_ge(x_lo, 2 * h + 2)
                load_x3(*after)
            if half == 0 and isinstance(g, int) and g == 0:
                sp.wait_ge(shared_hi, 4)
                sp.wait_ge(shared_lo, 4)
                load_w1(0)
            elif half == 1 and more:
                sp.wait_ge(w1_hi, 3 * g + 3)
                sp.wait_ge(w1_lo, 3 * g + 3)
                load_w1(g + 1)
            sp.wait_ge(shared_ready, HS * h + HS)
            sp.dma_start(d["out"][bass.ds(GT * g + HT * half, HT), :].rearrange("(s p) e -> p s e", p=P), out_rows).then_inc(out_stored, 16)
            if more:
                load_h2(*after)

        def group(g, more):
            half_group(g, 0, True)
            half_group(g, 1, more)

        groups(sp, group)
        sp.wait_ge(dispatched, 16 * TOPK * NT)

        def load(s, par):
            sp.dma_start(x_slot[:, par, :], d["slot_rows"][bass.ds(P * s, P), :]).then_inc(x_slot_in[par], 16)

        load(0, 0)
        load(1, 1)
        with sp.Fori(0, (SLOTS - 1) // 2) as i:
            sp.wait_ge(x_turned, 2 * i + 1)
            sp.wait_ge(meta_ready, 2 * i + 1)
            load(2 * i + 2, 0)
            sp.wait_ge(x_turned, 2 * i + 2)
            sp.wait_ge(meta_ready, 2 * i + 2)
            load(2 * i + 3, 1)
        sp.wait_ge(out_stored, 16 * HALVES)

    @block.gpsimd
    def _(pool):
        for n, (tile, value) in enumerate(((ones[:], 1.0), (x3_in[TAIL:REST, 1, :], 0.0), (x3_in[TAIL:TAIL + 1, 1, :], 1.0),
                                           (x3_in[REST - 1:REST, 1, :], 1.0))):
            pool.memset(tile, value).then_inc(ones_ready, 1)
            pool.wait_ge(ones_ready, n + 1)
        pool.wait_ge(rows_ready, 1)
        for k in range(TOPK):
            if k > 0:
                pool.wait_ge(dispatched, 16 * NT)
            pool.wait_ge(gates_ready, 1)
            pool.tensor_copy(x3_all[:, :, EMB], gate[:, k, :]).then_inc(gate_set, 1)
            pool.wait_ge(gate_set, k + 1)
            for t in range(NT):
                pool.indirect_dma_start(out=d["slot_rows"], out_offset=bass.IndirectOffsetOnAxis(ap=rows[:, k, t:t + 1], axis=0),
                                        in_=x3_all[:, t, :], in_offset=None).then_inc(dispatched, 16)
        pool.wait_ge(dispatched, 16 * TOPK * NT)
        pool.wait_ge(shared_lo, 4)
        pool.dma_start(w2[:], d["w2"]).then_inc(w2_in, 16)
        pool.wait_ge(out_stored, 16 * HALVES)

        def take_meta(s, par, half):
            pool.wait_ge(x_slot_in[par], 16 * (half + 1))
            apart(pool, pool_passed)
            pool.tensor_copy(meta[:, bass.ds(s, 1), :].rearrange("p a w -> p (a w)"), x_slot[:, par, EMB:ROW]).then_inc(meta_ready, 1)

        def add_rows(s, par, half):
            take_meta(s + 1, 1 - par, half + par)
            pool.wait_ge(meta_ready, s + 1)
            least(pool, added, 16 * (s - 1))
            apart(pool, pool_passed)
            pool.tensor_copy(tokens[:, par:par + 1], meta[:, bass.ds(s, 1), 1]).then_inc(tokens_ready, 1)
            pool.wait_ge(tokens_ready, s + 1)
            pool.wait_ge(y_ready, s + 1)
            least(pool, added, 16 * s)
            apart(pool, pool_passed)
            pool.indirect_dma_start(out=d["out"], out_offset=bass.IndirectOffsetOnAxis(ap=tokens[:, par:par + 1], axis=0),
                                    in_=y_slot[:, par, 1, :], in_offset=None, compute_op=ALU.add).then_inc(added, 16)

        take_meta(0, 0, 0)
        add_rows(0, 0, 0)
        slots(pool, add_rows)
        pool.wait_ge(added, 16 * SLOTS)

    @block.scalar
    def _(act):
        def x_hi_out(h):
            act.wait_ge(x3t_in, 32 * (h + 1))
            least(act, hs_done, HK * h)
            act.activation(x3_t.hi[:], x3_in[:, 0, :], ACT.Copy).then_inc(x_hi, 1)
            for part in (x3_t.both[0:TAIL], x3_t.rest[0:TAIL]):
                act.activation(part, x3_in[0:TAIL, 1, :], ACT.Copy).then_inc(x_hi, 1)

        def hs_hi_out(h):
            least(act, ys_done, HS * h)
            for c in range(HK):
                act.wait_ge(hs_done, HK * h + c + 1)
                act.activation(hs_hi[:, c, :], psum[:, c % 3, 0:HT], ACT.Relu).then_inc(hs_hi_ready, 1)

        def w1_hi_out(e):
            act.wait_ge(w1_raw_in, 48 * (e + 1))
            for part, raw in ((w1.hi, w1_raw[0]), (w1.both, w1_raw[1]), (w1.rest, w1_raw[2][0:REST])):
                act.activation(expert_part(part, e), raw, ACT.Copy).then_inc(w1_hi, 1)

        def group(g, more):
            hs_hi_out(2 * g)
            x_hi_out(2 * g + 1)
            w1_hi_out(g)
            hs_hi_out(2 * g + 1)
            if more:
                x_hi_out(2 * g + 2)

        act.wait_ge(ones_ready, 4)
        act.activation(x3_t.rest[TAIL:REST], x3_in[TAIL:REST, 1, :], ACT.Copy).then_inc(rows_copied, 1)
        x_hi_out(0)
        act.wait_ge(shared_in, SHARED_LOADS)
        round_weights(act, ws1, ws1_raw, shared_hi)
        act.activation(ws2_hi[:], ws2_raw, ACT.Copy).then_inc(shared_hi, 1)
        act.wait_ge(gap_ready, 1)
        act.activation(gate[:, 2, :], gap[:], ACT.Exp).then_inc(gap_exp, 1)
        groups(act, group)

        def x_t_out(s, par):
            act.wait_ge(x_turned, s + 1)
            least(act, h_done, s - 1)
            t = slice(P * par, P * par + P)
            act.activation(x3_t.hi[:, t], psum[:, 0, 0:P], ACT.Copy).then_inc(x_t_hi, 1)
            for part in (x3_t.both[0:TAIL, t], x3_t.rest[0:TAIL, t]):
                act.activation(part, psum[0:TAIL, 0, P:2 * P], ACT.Copy).then_inc(x_t_hi, 1)

        def h_out(s, par):
            act.wait_ge(h_done, s + 1)
            least(act, h_turned, s - 1)
            act.activation(h_slot[:, par, 0:HALF], psum[:, 1, 0:HALF], ACT.Relu).then_inc(h_by_act, 1)

        def h_t_out(s, par):
            act.wait_ge(h_turned, s + 1)
            least(act, y_done, s - 1)
            act.activation(h_slot_t[:, par, 0:3, :].rearrange("p c t -> p (c t)"), psum[:, 3, 0:HALF], ACT.Copy).then_inc(h_t_by_act, 1)

        def y_out(s, par):
            act.wait_ge(y_plain_ready, s + 1)
            act.wait_ge(meta_ready, s + 1)
            least(act, added, 16 * (s - 1))
            act.activation(y_slot[:, par, 1, :], y_slot[:, par, 0, :], ACT.Copy, scale=meta[:, bass.ds(s, 1), 0]).then_inc(y_ready, 1)

        def step(s, par, half):
            h_out(s, par)
            x_t_out(s + 1, 1 - par)
            y_out(s - 1, 1 - par)
            h_t_out(s, par)

        act.wait_ge(out_stored, 16 * HALVES)
        act.wait_ge(w1_lo, 3 * NE)
        x_t_out(0, 0)
        h_out(0, 0)
        x_t_out(1, 1)
        h_t_out(0, 0)
        slots(act, step)
        y_out(SLOTS - 1, 0)

    @block.tensor
    def _(pe):
        def hs(h):
            pe.wait_ge(x_hi, 3 * h + 3)
            pe.wait_ge(x_lo, 2 * h + 2)
            for c in range(HK):
                least(pe, hs_lo_ready, HK * h + c - 2)
                product(pe, psum[:, c % 3, 0:HT], ws1.weights(slice(P * c, P * c + P)), x3_t.activations(slice(0, HT))).then_inc(hs_done, 1)

        def ys(h, half):
            for s in range(HS):
                least(pe, shared_ready, HS * h + s - 3)
                for c in range(HK):
                    if s == 0:
                        pe.wait_ge(hs_lo_ready, HK * h + c + 1)
                    for i, (h_part, w_part) in enumerate(((hs_hi, ws2_hi), (hs_hi, ws2_lo), (hs_lo, ws2_hi))):
                        m = pe.matmul(psum[:, 3 + HS * half + s, 0:EMB], h_part[:, c, P * s:P * s + P], w_part[:, c, :],
                                      start=(c == 0 and i == 0), stop=(c == HK - 1 and i == 2))
                m.then_inc(ys_done, 1)

        def group(g, more):
            hs(2 * g)
            if isinstance(g, int) and g == 0:
                pe.wait_ge(shared_hi, 4)
                pe.wait_ge(shared_lo, 4)
                pe.wait_ge(mask_ready, 1)
                flat = mask[:].rearrange("p t e -> p (t e)")
                pe.matmul(psum[:, 7, 0:NT * NE], tri, flat, start=True, stop=True)
                pe.matmul(psum[:, 7, NT * NE:2 * NT * NE], ones[:], flat, start=True, stop=True).then_inc(ranks_done, 1)
            ys(2 * g, 0)
            hs(2 * g + 1)
            ys(2 * g + 1, 1)

        pe.wait_ge(shared_hi, 3)
        pe.wait_ge(shared_lo, 3)
        pe.wait_ge(rows_copied, 1)
        pe.wait_ge(ones_ready, 4)
        groups(pe, group)

        def expert(s):
            return pe.value_load(slot_expert[0:1, bass.ds(s, 1)], min_val=0, max_val=NE - 1)

        def turn_x(s, par, half):
            pe.wait_ge(x_slot_in[par], 16 * (half + 1))
            least(pe, x_t_lo, 2 * s)
            pe.transpose(psum[:, 0, 0:P], x_slot[:, par, 0:P], ident)
            pe.transpose(psum[0:TAIL, 0, P:2 * P], x_slot[:, par, P:EMB], ident).then_inc(x_turned, 1)

        def h(s, par, e):
            pe.wait_ge(x_t_hi, 3 * s + 3)
            pe.wait_ge(x_t_lo, 2 * s + 2)
            least(pe, h_by_act, s)
            least(pe, h_by_dve, s)
            for n in range(2):
                m = product(pe, psum[:, 1 + n, 0:HALF], x3_t.activations(slice(P * par, P * par + P)),
                            w1.weights(bass.ds(HID * e + HALF * n, HALF)))
            m.then_inc(h_done, 1)

        def turn_h(s, par):
            pe.wait_ge(h_by_act, s + 1)
            pe.wait_ge(h_by_dve, s + 1)
            least(pe, h_t_by_act, s)
            least(pe, h_t_by_dve, s)
            for c in range(HK):
                m = pe.transpose(psum[:, 3 + c // 3, P * (c % 3):P * (c % 3) + P], h_slot[:, par, P * c:P * c + P], ident)
            m.then_inc(h_turned, 1)

        def y(s, par, e):
            pe.wait_ge(h_t_by_act, s + 1)
            pe.wait_ge(h_t_by_dve, s + 1)
            least(pe, y_plain_ready, s - 1)
            for c in range(HK):
                m = pe.matmul(psum[:, 5 + par, 0:EMB], h_slot_t[:, par, c, :],
                              w2[:, bass.ds(e, 1), c, :].rearrange("p a n -> p (a n)"), start=(c == 0), stop=(c == HK - 1))
            m.then_inc(y_done, 1)

        def step(s, par, half):
            before, now = expert(s - 1), expert(s)
            h(s, par, now)
            turn_x(s + 1, 1 - par, half + par)
            y(s - 1, 1 - par, before)
            turn_h(s, par)

        pe.wait_ge(w2_in, 16)
        pe.wait_ge(w1_hi, 3 * NE)
        pe.wait_ge(w1_lo, 3 * NE)
        pe.wait_ge(table_ready, 1)
        turn_x(0, 0, 0)
        h(0, 0, expert(0))
        turn_x(1, 1, 0)
        turn_h(0, 0)
        slots(pe, step)
        y(SLOTS - 1, 0, expert(SLOTS - 1))

    @block.vector
    def _(dve):
        steps = [0]

        def link(ins):
            steps[0] += 1
            ins.then_inc(route_step, 1)
            dve.wait_ge(route_step, steps[0])

        def by_token(x):
            return x.unsqueeze(1).broadcast_to([P, NT, NE])

        def by_expert(x):
            return x.unsqueeze(2).broadcast_to([P, NT, NE])

        def x_lo_out(h):
            dve.wait_ge(x_hi, 3 * h + 3)
            least(dve, hs_done, HK * h)
            dve.tensor_tensor(x3_t.lo[:], x3_in[:, 0, :], x3_t.hi[:].bitcast(F32), ALU.subtract).then_inc(x_lo, 1)
            dve.tensor_tensor(x3_t.both[TAIL:P], x3_in[0:TAIL, 1, :], x3_t.both[0:TAIL].bitcast(F32), ALU.subtract).then_inc(x_lo, 1)

        def hs_lo_out(h):
            least(dve, ys_done, HS * h)
            for c in range(HK):
                dve.wait_ge(hs_hi_ready, HK * h + c + 1)
                dve.scalar_tensor_tensor(hs_lo[:, c, :], psum[:, c % 3, 0:HT], 0.0, hs_hi[:, c, :].bitcast(F32), ALU.max, ALU.subtract)\
                   .then_inc(hs_lo_ready, 1)

        def ys_out(h, half):
            dve.wait_ge(h2_loaded, 16 * (h + 1))
            dve.tensor_tensor(h2_in, h2_in, bs2[:].unsqueeze(1).broadcast_to([P, HS, EMB]), ALU.add).then_inc(h2_plus, 1)
            dve.wait_ge(h2_plus, h + 1)
            least(dve, out_stored, 16 * h)
            for s in range(HS):
                dve.wait_ge(ys_done, HS * h + s + 1)
                dve.scalar_tensor_tensor(out_rows[:, s, :], psum[:, 3 + HS * half + s, 0:EMB], 0.1 * TOPK, h2_in[:, s, :], ALU.mult, ALU.add)\
                   .then_inc(shared_ready, 1)

        def w1_lo_out(e):
            dve.wait_ge(w1_hi, 3 * e + 3)
            lo, rest = expert_part(w1.lo, e), expert_part(w1.rest, e)
            dve.tensor_tensor(lo, w1_raw[0], expert_part(w1.hi, e).bitcast(F32), ALU.subtract).then_inc(w1_lo, 1)
            for rows_of in (slice(0, TAIL), slice(REST - 1, REST)):
                dve.tensor_tensor(rest[rows_of], w1_raw[2][rows_of], rest[rows_of].bitcast(F32), ALU.subtract).then_inc(w1_lo, 1)

        x_lo_out(0)
        for k in range(TOPK):
            link(dve.tensor_reduce(top[:, k, :], logits_all[:], AX.X, ALU.max))
            link(dve.tensor_tensor(place[:], logits_all[:], by_expert(top[:, k, :]), ALU.is_lt))
            link(dve.scalar_tensor_tensor(place[:], place[:], float(NE), by_token(experts_iota), ALU.mult, ALU.add))
            link(dve.tensor_reduce(at_expert[:], place[:], AX.X, ALU.min))
            link(dve.tensor_tensor(chosen[:, k], by_token(experts_iota), by_expert(at_expert[:]), ALU.is_equal))
            if k == 0:
                link(dve.scalar_tensor_tensor(logits_all[:], chosen[:, 0], -FAR, logits_all[:], ALU.mult, ALU.add))
        dve.tensor_tensor(gap[:], top[:, 1, :], top[:, 0, :], ALU.subtract).then_inc(gap_ready, 1)
        dve.tensor_tensor(mask[:], chosen[:, 0], chosen[:, 1], ALU.add).then_inc(mask_ready, 1)
        dve.wait_ge(gap_exp, 1)
        link(dve.tensor_scalar(gap[:], gate[:, 2, :], 1.0, None, ALU.add))
        link(dve.reciprocal(gate[:, 0, :], gap[:]))
        dve.tensor_tensor(gate[:, 1, :], gate[:, 2, :], gate[:, 0, :], ALU.mult).then_inc(gates_ready, 1)

        dve.wait_ge(shared_in, SHARED_LOADS)
        dve.tensor_scalar(bs2[:], bs2[:], 0.1 * TOPK, None, ALU.mult).then_inc(bias_scaled, 1)
        dve.wait_ge(shared_hi, 4)
        rest_of_weights(dve, ws1, ws1_raw, shared_lo)
        dve.tensor_tensor(ws2_lo[:], ws2_raw, ws2_hi[:].bitcast(F32), ALU.subtract).then_inc(shared_lo, 1)
        dve.wait_ge(bias_scaled, 1)
        hs_lo_out(0)
        x_lo_out(1)
        dve.wait_ge(ranks_done, 1)
        ranks = psum[:, 7, 0:NT * NE].rearrange("p (t e) -> p t e", e=NE)
        totals = psum[:, 7, NT * NE:2 * NT * NE].rearrange("p (t e) -> p t e", e=NE)
        link(dve.tensor_copy(running[:, 0], totals))
        at = 0
        for hop in (1, 2, 4, 8, 16):
            link(dve.tensor_tensor(running[:, 1 - at, hop:], running[:, at, hop:], running[:, at, :NT - hop], ALU.add))
            link(dve.tensor_copy(running[:, 1 - at, :hop], running[:, at, :hop]))
            at = 1 - at
        hs_lo_out(1)
        ys_out(0, 0)
        x_lo_out(2)
        link(dve.tensor_scalar(padded_i[:], running[:, at, NT - 1, :], float(P - 1), None, ALU.add))
        link(dve.tensor_single_scalar(padded_i[:], padded_i[:], -P, ALU.bitwise_and))
        link(dve.tensor_copy(padded[:], padded_i[:]))
        link(dve.tensor_copy(ends[:, 0], padded[:]))
        last = 0
        for hop in (1, 2, 4):
            link(dve.tensor_tensor(ends[:, 1 - last, hop:], ends[:, last, hop:], ends[:, last, :NE - hop], ALU.add))
            link(dve.tensor_copy(ends[:, 1 - last, :hop], ends[:, last, :hop]))
            last = 1 - last
        link(dve.tensor_tensor(starts[:], ends[:, last], padded[:], ALU.subtract))
        link(dve.tensor_tensor(place[:], running[:, at], totals, ALU.subtract))
        link(dve.tensor_tensor(place[:], place[:], ranks, ALU.add))
        link(dve.tensor_tensor(place[:], place[:], by_token(starts[:]), ALU.add))
        for k in range(TOPK):
            link(dve.tensor_tensor(running[:, 1 - at], chosen[:, k], place[:], ALU.mult))
            link(dve.tensor_reduce(rows_f[:, k, :], running[:, 1 - at], AX.X, ALU.add))
        dve.tensor_copy(rows[:], rows_f[:]).then_inc(rows_ready, 1)
        for part in (slice(0, (SLOTS + 1) // 2), slice((SLOTS + 1) // 2, SLOTS)):
            n = part.stop - part.start
            link(dve.tensor_tensor(past[:, 0:n], slot_starts[0:1, part].unsqueeze(2).broadcast_to([1, n, NE]),
                                   ends[0:1, last].unsqueeze(1).broadcast_to([1, n, NE]), ALU.is_ge))
            link(dve.tensor_reduce(slot_expert_f[:, part], past[:, 0:n], AX.X, ALU.add))
        dve.tensor_scalar(slot_expert[:], slot_expert_f[:], float(NE - 1), None, ALU.min).then_inc(table_ready, 1)

        def group(g, more):
            hs_lo_out(2 * g)
            x_lo_out(2 * g + 1)
            ys_out(2 * g, 0)
            w1_lo_out(g)
            hs_lo_out(2 * g + 1)
            if more:
                x_lo_out(2 * g + 2)
            ys_out(2 * g + 1, 1)

        w1_lo_out(0)
        ys_out(1, 1)
        with dve.Fori(1, G - 1) as g:
            group(g, True)
        group(G - 1, False)
        dve.wait_ge(out_stored, 16 * HALVES)

        def x_lo_of_slot(s, par):
            dve.wait_ge(x_t_hi, 3 * s + 3)
            least(dve, h_done, s - 1)
            t = slice(P * par, P * par + P)
            dve.tensor_tensor(x3_t.lo[:, t], psum[:, 0, 0:P], x3_t.hi[:, t].bitcast(F32), ALU.subtract).then_inc(x_t_lo, 1)
            dve.tensor_tensor(x3_t.both[TAIL:P, t], psum[0:TAIL, 0, P:2 * P], x3_t.both[0:TAIL, t].bitcast(F32), ALU.subtract).then_inc(x_t_lo, 1)

        def h_out(s, par):
            dve.wait_ge(h_done, s + 1)
            least(dve, h_turned, s - 1)
            dve.tensor_scalar(h_slot[:, par, HALF:], psum[:, 2, 0:HALF], 0.0, None, ALU.max).then_inc(h_by_dve, 1)

        def h_t_out(s, par):
            dve.wait_ge(h_turned, s + 1)
            least(dve, y_done, s - 1)
            dve.tensor_copy(h_slot_t[:, par, 3:6, :].rearrange("p c t -> p (c t)"), psum[:, 4, 0:HALF]).then_inc(h_t_by_dve, 1)

        def y_out(s, par):
            e = dve.value_load(slot_expert[0:1, bass.ds(s, 1)], min_val=0, max_val=NE - 1)
            dve.wait_ge(y_done, s + 1)
            least(dve, y_ready, s - 1)
            dve.tensor_tensor(y_slot[:, par, 0, :], psum[:, 5 + par, 0:EMB],
                              b2[:, bass.ds(e, 1), :].rearrange("p a n -> p (a n)"), ALU.add).then_inc(y_plain_ready, 1)

        def step(s, par, half):
            h_out(s, par)
            x_lo_of_slot(s + 1, 1 - par)
            y_out(s - 1, 1 - par)
            h_t_out(s, par)

        dve.wait_ge(table_ready, 1)
        dve.wait_ge(b2_in, 16)
        x_lo_of_slot(0, 0)
        h_out(0, 0)
        x_lo_of_slot(1, 1)
        h_t_out(0, 0)
        slots(dve, step)
        y_out(SLOTS - 1, 0)


def lay_out(x):
    import numpy as np
    a = {k: np.asarray(v) for k, v in x.items()}

    def halves(w, bias=None):
        n = w.shape[1]
        t = np.zeros((HC + 1, 2, n), w.dtype)
        t[:HC] = w.reshape(2, HC, n).transpose(1, 0, 2)
        if bias is not None:
            t[HC, 0] = bias
        return t

    def packed(w, bias):
        t = np.zeros((P, 3, w.shape[1]), w.dtype)
        t[:, 0] = w[:P]
        t[:TAIL, 1] = t[TAIL:, 1] = t[:TAIL, 2] = w[P:]
        t[TAIL, 2] = t[REST - 1, 2] = bias
        return t

    def columns(v):
        return np.stack([v[:P], np.concatenate([v[P:], v[P:]])], 1)

    side = IMG // PATCH
    patches = a["x"].reshape(G, B // G, CH, side, PATCH, side, PATCH).transpose(0, 2, 4, 6, 1, 3, 5)
    patches = patches.reshape(G, KP, P, GT).transpose(0, 2, 1, 3)
    w_conv = a["L0_tok_conv_w"].reshape(EMB, KP, P).transpose(2, 1, 0)
    wq, wk, wv, wo = (a[f"L0_tok_w{c}"].T for c in "qkvo")
    bq, bk, bv, bo = (a[f"L0_tok_b{c}"] for c in "qkvo")
    w_qkv = packed(np.concatenate([wq, wk[:, P:], wk[:, :P], wv], 1), np.concatenate([bq, bk[P:], bk[:P], bv]))
    w_o = halves(wo.reshape(PAIRS, 2, HD, EMB).transpose(1, 0, 2, 3).reshape(EMB, EMB), bo)
    uv, uvb = a["L0_attn_uv_W"], a["L0_attn_uv_b"]
    swap = (np.arange(S_GAU) + S_GAU // 2) % S_GAU
    base_cols = 2 * E_GAU + swap
    w_uv = packed(np.concatenate([uv, uv[:, base_cols]], 1), np.concatenate([uvb, uvb[base_cols]]))
    ln_gamma = np.ones((P, 3), np.float32)
    ln_gamma[:, 0:2] = columns(a["L0_attn_ln_gamma"])
    ln_gamma[:TAIL, 2] = a["L0_attn_ln_gamma"][P:]
    ln_beta = np.zeros((P, 2, REST), np.float32)
    ln_beta[:, 0, [TAIL, REST - 1]] = a["L0_attn_ln_beta"][:P, None]
    ln_beta[:TAIL, 1, [TAIL, REST - 1]] = a["L0_attn_ln_beta"][P:, None]
    w_route = np.zeros((P, 2, NE), np.float32)
    w_route[:, 0] = a["L0_ffn_Wr"].T[:P]
    w_route[:TAIL, 1] = a["L0_ffn_Wr"].T[P:]
    gq, bqk = a["L0_attn_gamma_qk"], a["L0_attn_beta_qk"]
    pair_up = lambda v: np.stack([v.T, v[:, swap].T], 2)
    half = S_GAU // 2
    inv_freq = np.power(np.float32(10000.0), -np.arange(half, dtype=np.float32) / half).astype(np.float32)
    angle = (np.arange(L, dtype=np.float32)[None, :] * inv_freq[:, None]).astype(np.float32)
    cos, sin = np.cos(angle), np.sin(angle)
    rope = np.stack([np.concatenate([cos, cos]), np.concatenate([-sin, sin])], 1)
    m, n = np.meshgrid(np.arange(P), np.arange(P), indexing="ij")
    inside = (m // L) == (n // L)
    rel = a["L0_attn_w_rel"][np.where(inside, m - n + L - 1, 0)]
    rel_bias = np.where(inside, rel, np.float32(-1e30))
    head_mask = np.zeros((P, 2), np.float32)
    for h in range(2):
        head_mask[(np.arange(P) // HD) % 2 == h, h] = HD ** -0.5
    consts = np.concatenate([
        np.eye(P), np.triu(np.ones((P, P)), 1), np.tile(np.arange(NE), (P, 1)), np.tile(P * np.arange(SLOTS), (P, 1)),
    ], 1)
    pad_rows = np.zeros((P, ROW), np.float32)
    pad_rows[:, EMB + 1] = T + np.arange(P)
    token_ids = (np.arange(NT)[None, :] * P + np.arange(P)[:, None]).astype(np.float32)
    w1 = np.stack([packed(a["L0_ffn_W1"][e].T, a["L0_ffn_b1"][e]) for e in range(NE)])
    w2 = a["L0_ffn_W2"].transpose(0, 2, 1).reshape(NE, HK, P, EMB).transpose(2, 0, 1, 3)
    w = dict(
        patches=patches, w_conv=w_conv, b_conv=columns(a["L0_tok_conv_b"]), w_qkv=w_qkv, head_mask=head_mask,
        w_o=w_o, w_uv=w_uv, ln_gamma=ln_gamma, ln_beta=ln_beta,
        qk_gain=pair_up(gq), qk_shift=pair_up(bqk), rope=rope, rel_bias=rel_bias,
        w_gau=a["L0_attn_o_W"].reshape(EC, P, EMB).transpose(1, 0, 2), b_gau=a["L0_attn_o_b"][None],
        w_route=w_route, w1=w1, w2=w2, b2=a["L0_ffn_b2"].reshape(1, -1),
        ws1=packed(a["L0_ffn_sW1"].T, a["L0_ffn_sb1"]), ws2=a["L0_ffn_sW2"].T.reshape(HK, P, EMB).transpose(1, 0, 2),
        bs2=a["L0_ffn_sb2"][None], consts=consts.astype(np.float32), pad_rows=pad_rows, token_ids=token_ids,
    )
    return {k: np.ascontiguousarray(v) for k, v in w.items()}


def kernel(**inputs):
    import concourse.bacc as bacc
    from concourse.bass_utils import run_bass_kernel_spmd

    nc = bacc.Bacc("TRN2", target_bir_lowering=False, num_devices=1)
    build_program(nc, declare(nc))
    result = run_bass_kernel_spmd(nc, [lay_out(inputs)], core_ids=[0])
    return result.results[0]["out"][:T].reshape(B, L, EMB)
```

```python
from contextlib import ExitStack

import concourse.bass as bass
from concourse import mybir

F32 = mybir.dt.float32
F32R = mybir.dt.float32r
I32 = mybir.dt.int32
U32 = mybir.dt.uint32
ALU = mybir.AluOpType
ACT = mybir.ActivationFunctionType
AX = mybir.AxisListType

P = 128
B, CH, IMG, PATCH = 64, 3, 128, 16
EMB, HEADS = 192, 12
L = (IMG // PATCH) ** 2
T = B * L
HD = EMB // HEADS
PAIRS = HEADS // 2
GT = 512
G = T // GT
SUB = GT // P
NT = T // P
KP = CH * PATCH * PATCH // P
RING = 3
HC = EMB // 2
TAIL = EMB - P
REST = 97
E_GAU, S_GAU = 384, 128
EC = E_GAU // P
NE, TOPK = 8, 2
HID = 4 * EMB
HK = HID // P
SLOT = 2 * P
SLOTS = (T * TOPK) // SLOT + NE - 1
ROW = EMB + 2
VH = HD + 1
EPS = 1e-5
FAR = 3e38
WUV = 2 * E_GAU + 2 * S_GAU
HT, HS = GT // 2, SUB // 2
QUARTERS = 4
QT = NT // QUARTERS


def declare(nc):
    shapes = dict(
        patches=[G, P, KP, GT], w_conv=[P, KP, EMB], b_conv=[P, 2], w_qkv=[P, 3, 3 * EMB],
        head_mask=[P, 2], w_o=[HC + 1, 2, EMB], w_uv=[P, 3, WUV], ln_gamma=[P, 3], ln_beta=[P, 2, REST],
        qk_gain=[P, 2, 2], qk_shift=[P, 2, 2], rope=[P, 2, L], rel_bias=[P, P], w_gau=[P, EC, EMB],
        b_gau=[1, EMB], w_route=[P, 2, NE], w1=[NE, P, 3, HID], w2=[P, NE, HK, EMB], b2=[1, NE * EMB],
        ws1=[P, 3, HID], ws2=[P, HK, EMB], bs2=[1, EMB], consts=[P, 2 * P + NE + SLOTS + 1],
    )
    d = {k: nc.dram_tensor(k, s, F32, kind="ExternalInput").ap() for k, s in shapes.items()}
    d["pad_rows"] = nc.dram_tensor("pad_rows", [SLOT, ROW], F32, kind="ExternalInput").ap()
    d["token_ids"] = nc.dram_tensor("token_ids", [P, NT], F32, kind="ExternalInput").ap()
    d["out"] = nc.dram_tensor("out", [T + SLOT, EMB], F32, kind="ExternalOutput").ap()
    d["x3t"] = nc.dram_tensor("x3t", [G, P, 2, GT], F32, kind="Internal").ap()
    d["h2"] = nc.dram_tensor("h2_of_groups", [G, P, SUB, EMB], F32, kind="Internal").ap()
    d["slot_rows"] = nc.dram_tensor("slot_rows", [(SLOTS + 1) * SLOT, ROW], F32, kind="Internal").ap()
    return d


def least(eng, sem, n):
    if not isinstance(n, int) or n > 0:
        eng.wait_ge(sem, n)


def apart(eng, passed):
    eng.sem_inc(passed, 1)


class Packed:

    def __init__(self, sb, name, cols):
        self.hi = sb(name + "_hi", [P, cols], F32R)
        self.lo = sb(name + "_lo", [P, cols], F32R)
        self.both = sb(name + "_both", [P, cols], F32R)
        self.rest = sb(name + "_rest", [REST, cols], F32R)

    def weights(self, cols):
        return [t[:, cols] for t in (self.hi, self.lo, self.hi, self.both, self.rest)]

    def activations(self, cols):
        return [t[:, cols] for t in (self.hi, self.hi, self.lo, self.both, self.rest)]


def product(pe, out, stationary, moving):
    for i in range(5):
        m = pe.matmul(out, stationary[i], moving[i], start=(i == 0), stop=(i == 4))
    return m


def round_weights(act, w, raw, done):
    act.activation(w.hi[:], raw[0], ACT.Copy).then_inc(done, 1)
    act.activation(w.both[:], raw[1], ACT.Copy).then_inc(done, 1)
    act.activation(w.rest[:], raw[2][0:REST], ACT.Copy).then_inc(done, 1)


def rest_of_weights(dve, w, raw, rounded, done):
    dve.wait_ge(rounded, 1)
    dve.tensor_tensor(w.lo[:], raw[0], w.hi[:].bitcast(F32), ALU.subtract).then_inc(done, 1)
    dve.wait_ge(rounded, 3)
    dve.tensor_tensor(w.rest[0:TAIL], raw[2][0:TAIL], w.rest[0:TAIL].bitcast(F32), ALU.subtract).then_inc(done, 1)
    dve.tensor_tensor(w.rest[REST - 1:REST], raw[2][REST - 1:REST], w.rest[REST - 1:REST].bitcast(F32), ALU.subtract).then_inc(done, 1)


def build_program(nc, d):
    with ExitStack() as whole:
        def keep(name, shape, dt=F32):
            return whole.enter_context(nc.sbuf_tensor(name, shape, dt))

        psum = whole.enter_context(nc.psum_tensor("psum", [P, 8, 512], F32))
        w2_flat = keep("w2_sb", [P, max(NE * HK * EMB, NT * ROW + KP * GT)])
        w2 = w2_flat[:, 0:NE * HK * EMB].rearrange("p (e c n) -> p e c n", c=HK, n=EMB)
        x3_all = w2_flat[:, 0:NT * ROW].rearrange("p (t w) -> p t w", w=ROW)
        patches = w2_flat[:, NT * ROW:NT * ROW + KP * GT].rearrange("p (c t) -> p c t", t=GT)
        ws1_raw = [w2_flat[:, NT * ROW + HID * i:NT * ROW + HID * i + HID] for i in range(3)]
        logits_all = keep("logits_all", [P, NT, NE])
        consts = keep("consts_sb", [P, 2 * P + NE + SLOTS + 1])
        ident = consts[:, 0:P]
        with ExitStack() as scope:
            front_and_back(nc, d, scope, psum, x3_all, patches, ws1_raw, logits_all, consts, ident)
        with ExitStack() as scope:
            experts(nc, d, scope, psum, w2, x3_all, ws1_raw, logits_all, consts, ident)


def front_and_back(nc, d, scope, psum, x3_all, patches, ws1_raw, logits_all, consts, ident):
    def sb(name, shape, dt=F32):
        return scope.enter_context(nc.sbuf_tensor(name, shape, dt))

    def sem(name):
        return scope.enter_context(nc.semaphore(name))

    w_conv_hi = sb("w_conv_hi", [P, KP, EMB], F32R)
    w_conv_lo = sb("w_conv_lo", [P, KP, EMB], F32R)
    b_conv = sb("b_conv_sb", [P, 2])
    w_qkv = Packed(sb, "w_qkv", 3 * EMB)
    head_mask = sb("head_mask_sb", [P, 2])
    w_o = sb("w_o_sb", [HC + 1, 2, EMB])
    w_uv = Packed(sb, "w_uv", WUV)
    gamma = sb("gamma_sb", [P, 3])
    qk_gain = sb("qk_gain_sb", [P, 2, 2])
    qk_shift = sb("qk_shift_sb", [P, 2, 2])
    rope = sb("rope_sb", [P, 2, L])
    rel_bias = sb("rel_bias_sb", [P, P])
    w_gau = sb("w_gau_sb", [P, EC, EMB])
    b_gau = sb("b_gau_sb", [P, EMB])
    w_route = sb("w_route_sb", [P, 2, NE])
    rope_tab = sb("rope_tab", [P, 3, 2, L])
    minus_half = sb("minus_half", [P, SUB])
    eps = sb("eps", [P, SUB])
    one = sb("one", [P, SUB])
    minus_one = sb("minus_one", [P, SUB])
    patch_hi = sb("patch_hi", [P, RING, GT], F32R)
    patch_lo = sb("patch_lo", [P, RING, GT], F32R)
    tok = Packed(sb, "tok", GT)
    q_a = sb("q_a", [P, GT // L, 2, L])
    q_b = sb("q_b", [P, GT // L, 2, L])
    k_a = sb("k_a", [P, 4, GT])
    k_b = sb("k_b", [P, 2, GT])
    v_ones = sb("v_ones", [P, SUB, PAIRS, 2, 2 * VH])
    row_max = sb("row_max", [P, 2, 2, PAIRS])
    probs = sb("probs", [P, 2, PAIRS, 2, L])
    probs_t = sb("probs_t", [P, 2, PAIRS, P])
    inv_sum = sb("inv_sum", [P, 2, PAIRS, 2])
    att = sb("att", [P, 2, 2, PAIRS, HD])
    att_t = sb("att_t", [HC + 1, 2, 2, P])
    h1 = sb("h1", [P, SUB, EMB])
    stats1 = sb("stats1", [P, SUB, 6])
    mean_var1 = sb("mean_var1", [P, SUB, 2])
    coef = sb("coef", [P, 8, SUB])
    h1_plus = sb("h1_plus", [P, SUB, EMB])
    beta = h1_plus[:].rearrange("p s e -> p (s e)")[:, 0:2 * REST].rearrange("p (j r) -> p j r", r=REST)
    xn = sb("xn", [P, SUB, EMB])
    xn_t = Packed(sb, "xn_t", GT)
    tanh = sb("tanh", [P, 3, 512])
    u_t = sb("u_t", [P, EC, GT])
    base = sb("base", [P, 2, GT])
    rope_1 = sb("rope_1", [P, 2, GT])
    rope_2 = sb("rope_2", [P, 2, GT])
    qk_t = sb("qk_t", [P, 2, GT])
    v_nat = sb("v_nat", [P, SUB, E_GAU])
    biased = sb("biased", [P, SUB, P])
    gated = sb("gated", [P, EC, GT])
    h2 = sb("h2", [P, SUB, EMB])
    stats2 = sb("stats2", [P, SUB, 6])
    mean_var2 = sb("mean_var2", [P, SUB, 2])
    coef2 = sb("coef2", [P, 3, SUB])
    x3 = sb("x3", [P, SUB, EMB])
    x3_t = gated[:, 0:2]

    weights_in, patch_weights_in, qkv_in = sem("weights_in"), sem("patch_weights_in"), sem("qkv_in")
    patches_in = sem("patches_in")
    first_patches_in = [sem(f"first_patches_in{i}") for i in range(KP // 2)]
    pads_in, shared_in = sem("pads_in"), sem("shared_in")
    w_conv_rounded, w_conv_split = sem("w_conv_rounded"), sem("w_conv_split")
    patches_rounded, patches_split = sem("patches_rounded"), sem("patches_split")
    chunk_done = sem("chunk_done")
    conv_done, qk_done, v_done = sem("conv_done"), sem("qk_done"), sem("v_done")
    scores_done, probs_turned, pv_done = sem("scores_done"), sem("probs_turned"), sem("pv_done")
    att_turned, proj_done = sem("att_turned"), sem("proj_done")
    xn_turned, uv_done, gqk_done, kv_done = sem("xn_turned"), sem("uv_done"), sem("gqk_done"), sem("kv_done")
    gau_done, x3_turned, route_done, fold_done = sem("gau_done"), sem("x3_turned"), sem("route_done"), sem("fold_done")
    const_ready, fold_ready = sem("const_ready"), sem("fold_ready")
    tok_hi, tok_lo, xn_hi, xn_lo = sem("tok_hi"), sem("tok_lo"), sem("xn_hi"), sem("xn_lo")
    qkv_hi, qkv_lo, uv_hi, uv_lo = sem("qkv_hi"), sem("qkv_lo"), sem("uv_hi"), sem("uv_lo")
    rows_set, rows_copied = sem("rows_set"), sem("rows_copied")
    qk_by_act, qk_by_dve = sem("qk_by_act"), sem("qk_by_dve")
    v_ready = sem("v_ready")
    max_ready, shifted, exp_done = sem("max_ready"), sem("shifted"), sem("exp_done")
    probs_t_act, probs_t_dve = sem("probs_t_act"), sem("probs_t_dve")
    inv_ready, att_ready, att_t_ready, h1_ready = sem("inv_ready"), sem("att_ready"), sem("att_t_ready"), sem("h1_ready")
    stat_step, var1_ready, coef_step, coef1_ready = sem("stat_step"), sem("var1_ready"), sem("coef_step"), sem("coef1_ready")
    xn_ready, h1_plus_act, h1_plus_ready = sem("xn_ready"), sem("h1_plus_act"), sem("h1_plus_ready")
    tanh_ready, silu_ready = sem("tanh_ready"), sem("silu_ready")
    rope_1_ready, rope_2_half, rope_2_ready, rope_ready = sem("rope_1_ready"), sem("rope_2_half"), sem("rope_2_ready"), sem("rope_ready")
    biased_ready, kern_ready, gated_ready = sem("biased_ready"), sem("kern_ready"), sem("gated_ready")
    h2_ready, var2_ready, coef2_ready, x3_ready, x3_t_ready = sem("h2_ready"), sem("var2_ready"), sem("coef2_ready"), sem("x3_ready"), sem("x3_t_ready")
    logits_read, coef2_step = sem("logits_read"), sem("coef2_step")
    dve_passed, pe_passed = sem("dve_passed"), sem("pe_passed")
    h2_kept, x3_kept, x3_t_kept = sem("h2_kept"), sem("x3_kept"), sem("x3_t_kept")

    qkv_raw = [v_nat[:].rearrange("p s e -> p (s e)")[:, 3 * EMB * i:3 * EMB * i + 3 * EMB] for i in range(2)]
    qkv_raw.append(u_t[:].rearrange("p c t -> p (c t)")[:, 0:3 * EMB])
    uv_raw = [t[:].rearrange("p q t -> p (q t)") for t in (base, rope_1, rope_2)]

    w_conv_raw = probs[:].rearrange("p s a h k -> p (s a h k)")[:, 0:KP * EMB].rearrange("p (c n) -> p c n", n=EMB)
    patch_weights = [(w_conv_raw, d["w_conv"]), (b_conv, d["b_conv"])]
    qkv_weights = [(t, d["w_qkv"][:, i]) for i, t in enumerate(qkv_raw)]
    weights = [(t, d["w_uv"][:, i]) for i, t in enumerate(uv_raw)]
    weights += [
        (head_mask, d["head_mask"]),
        (w_o, d["w_o"]), (gamma, d["ln_gamma"]), (beta, d["ln_beta"]),
        (qk_gain, d["qk_gain"]), (qk_shift, d["qk_shift"]), (rope, d["rope"]), (rel_bias, d["rel_bias"]),
        (w_gau, d["w_gau"]), (w_route, d["w_route"]), (consts, d["consts"]),
    ]
    N_WEIGHTS = len(weights) + 1
    ALL_WEIGHTS = 16 * N_WEIGHTS
    N_FOLDS = 13
    N_CONST = 11

    def peeled(eng, first, both, last):
        first(0)
        with eng.Fori(1, G - 1) as g:
            both(g, True)
        both(G - 1, False)
        last(G - 1)

    def cut(j):
        return slice(P, EMB) if j else slice(0, P)

    def images(t):
        return t.rearrange("p (i n) -> p i n", n=L)

    def by_image(t):
        return t[:].rearrange("p q (i n) -> p q i n", n=L)

    def of_base(t):
        return t.rearrange("p (i n) -> p i n", n=L).unsqueeze(1).broadcast_to([P, 2, GT // L, L])

    def table(i):
        return rope_tab[:, i, :, :].unsqueeze(2).broadcast_to([P, 2, GT // L, L])

    def v_dest(half, i):
        t = v_ones[64 * i:64 * i + 64, 2 * half:2 * half + 2, :, i, :]
        return t.rearrange("p s a (h e) -> p (s a) h e", e=VH)[:, :, :, 0:HD]

    def v_src(half, i):
        t = psum[64 * i:64 * i + 64, half, 0:2 * EMB]
        return t.rearrange("p (a h e) -> p a h e", h=2, e=HD)

    def score_banks(s):
        return 2 - 2 * (s % 2)

    block = scope.enter_context(nc.Block())

    @block.sync
    def _(sp):
        for tile, src in patch_weights:
            sp.dma_start(tile[:], src).then_inc(patch_weights_in, 16)
        for i, loaded in enumerate(first_patches_in):
            sp.dma_start(patches[:, 2 * i:2 * i + 2, :], d["patches"][0, :, 2 * i:2 * i + 2, :]).then_inc(loaded, 16)
        for tile, src in qkv_weights:
            sp.dma_start(tile, src).then_inc(qkv_in, 16)
        for tile, src in weights:
            sp.dma_start(tile[:], src).then_inc(weights_in, 16)
        sp.dma_start(b_gau[:], d["b_gau"].broadcast_to([P, EMB])).then_inc(weights_in, 16)
        def load_patches(g):
            sp.wait_ge(patches_split, KP * g)
            sp.dma_start(patches, d["patches"][bass.ds(g, 1)].rearrange("a p c t -> p (a c) t")).then_inc(patches_in, 16)

        def store_h2(g):
            sp.wait_ge(h2_ready, 2 * g + 2)
            sp.dma_start(d["h2"][bass.ds(g, 1)].rearrange("a p s e -> p (a s) e"), h2[:]).then_inc(h2_kept, 16)

        def store_x3(g):
            sp.wait_ge(x3_ready, SUB * g + SUB)
            sp.dma_start(x3_all[:, bass.ds(SUB * g, SUB), 0:EMB], x3[:]).then_inc(x3_kept, 16)
            sp.wait_ge(x3_t_ready, 2 * g + 2)
            for j, n in ((0, P), (1, TAIL)):
                sp.dma_start(d["x3t"][bass.ds(g, 1), 0:n, j, :].rearrange("a p t -> p (a t)"), x3_t[0:n, j, :]).then_inc(x3_t_kept, 16)

        load_patches(1)
        sp.dma_start(d["slot_rows"].rearrange("(s p) w -> s p w", p=SLOT),
                     d["pad_rows"].unsqueeze(0).broadcast_to([SLOTS + 1, SLOT, ROW])).then_inc(pads_in, 16)
        sp.dma_start(x3_all[:, :, EMB + 1:EMB + 2], d["token_ids"].unsqueeze(2),
                     allow_slow_non_contiguous=True).then_inc(pads_in, 16)
        load_patches(2)
        with sp.Fori(0, G - 3) as g:
            store_h2(g)
            load_patches(g + 3)
            store_x3(g)
        sp.wait_ge(patches_split, KP * G)
        for i, t in enumerate(ws1_raw):
            sp.dma_start(t, d["ws1"][:, i]).then_inc(shared_in, 16)
        with sp.Fori(G - 3, G) as g:
            store_h2(g)
            store_x3(g)
        sp.wait_ge(pads_in, 32)
        sp.wait_ge(shared_in, 48)
        sp.wait_ge(h2_kept, 16 * G)
        sp.wait_ge(x3_kept, 16 * G)
        sp.wait_ge(x3_t_kept, 32 * G)

    @block.gpsimd
    def _(pool):
        cleared = [q_b[:], k_a[:], k_b[:], v_ones[:]]
        ones = [att_t[HC:HC + 1, :, 0, :]]
        ones += [v_ones[64 * i:64 * i + 64, :, :, i, HD::VH] for i in range(2)]
        for n, tile in enumerate(cleared + ones):
            pool.memset(tile, 0.0 if n < len(cleared) else 1.0).then_inc(const_ready, 1)
            pool.wait_ge(const_ready, n + 1)
        for n, (tile, value) in enumerate(((minus_half, -0.5), (eps, EPS), (one, 1.0), (minus_one, -1.0))):
            pool.memset(tile[:], value).then_inc(const_ready, 1)
            pool.wait_ge(const_ready, len(cleared + ones) + n + 1)

        for n, (rows, value) in enumerate(((slice(TAIL, REST), 0.0), (slice(TAIL, TAIL + 1), 1.0), (slice(REST - 1, REST), 1.0))):
            pool.memset(biased[rows], value).then_inc(rows_set, 1)
            pool.wait_ge(rows_set, n + 1)

        def coef1(g):
            pool.wait_ge(var1_ready, g + 1)
            if not isinstance(g, int) or g > 0:
                pool.wait_ge(xn_ready, SUB * g)
                pool.wait_ge(h1_plus_act, SUB * g)
            n = 7 * g

            def step(ins):
                nonlocal n
                n = n + 1
                ins.then_inc(coef_step, 1)
                pool.wait_ge(coef_step, n)

            mean, var = mean_var1[:, :, 0], mean_var1[:, :, 1]
            step(pool.tensor_tensor(coef[:, 1, :], coef[:, 0, :], minus_half[:], ALU.pow))
            step(pool.tensor_tensor(coef[:, 2, :], coef[:, 1, :], coef[:, 1, :], ALU.mult))
            step(pool.tensor_tensor(coef[:, 2, :], coef[:, 2, :], var, ALU.mult))
            step(pool.tensor_tensor(coef[:, 2, :], coef[:, 2, :], eps[:], ALU.add))
            step(pool.tensor_tensor(coef[:, 3, :], coef[:, 2, :], minus_half[:], ALU.pow))
            step(pool.tensor_tensor(coef[:, 4, :], mean, coef[:, 1, :], ALU.mult))
            step(pool.tensor_tensor(coef[:, 5, :], coef[:, 4, :], minus_one[:], ALU.mult))
            pool.tensor_tensor(coef[:, 6, :], coef[:, 1, :], one[:], ALU.add).then_inc(coef1_ready, 1)
            pool.tensor_tensor(coef[:, 7, :], coef[:, 1, :], coef[:, 3, :], ALU.mult).then_inc(coef1_ready, 1)

        def add_b_gau(g):
            pool.wait_ge(h1_plus_act, SUB * g + SUB)
            pool.tensor_tensor(h1_plus[:], h1_plus[:], b_gau[:].unsqueeze(1).broadcast_to([P, SUB, EMB]), ALU.add)\
                .then_inc(h1_plus_ready, 1)

        def rope_second(g):
            pool.wait_ge(fold_ready, N_FOLDS)
            pool.wait_ge(silu_ready, 9 * g + 2)
            least(pool, rope_ready, g)
            pool.tensor_tensor(by_image(rope_2), of_base(base[:, 1, :]), table(1), ALU.mult).then_inc(rope_2_half, 1)
            pool.wait_ge(rope_2_half, g + 1)
            pool.tensor_tensor(by_image(rope_2), by_image(rope_2), table(2), ALU.add).then_inc(rope_2_ready, 1)

        def coef2_of(g):
            pool.wait_ge(var2_ready, g + 1)
            least(pool, x3_ready, SUB * g)
            pool.tensor_tensor(coef2[:, 1, :], coef2[:, 0, :], minus_half[:], ALU.pow).then_inc(coef2_step, 1)
            pool.wait_ge(coef2_step, 2 * g + 1)
            pool.tensor_tensor(coef2[:, 2, :], coef2[:, 1, :], mean_var2[:, :, 0], ALU.mult).then_inc(coef2_step, 1)
            pool.wait_ge(coef2_step, 2 * g + 2)
            pool.tensor_tensor(coef2[:, 2, :], coef2[:, 2, :], minus_one[:], ALU.mult).then_inc(coef2_ready, 1)

        def both(g, more):
            add_b_gau(g - 1)
            coef1(g)
            coef2_of(g - 1)
            rope_second(g)

        def front(g):
            coef1(g)
            rope_second(g)

        def back(g):
            add_b_gau(g)
            coef2_of(g)

        pool.wait_ge(weights_in, ALL_WEIGHTS)
        peeled(pool, front, both, back)

    @block.scalar
    def _(act):
        def round_patches(g, chunks=(0, KP)):
            least(act, patches_in, 16 * g)
            for c in range(*chunks):
                if isinstance(g, int) and g == 0:
                    act.wait_ge(first_patches_in[c // 2], 16)
                least(act, chunk_done, KP * g + c - RING + 1)
                act.activation(patch_hi[:, c % RING, :], patches[:, c, :], ACT.Copy).then_inc(patches_rounded, 1)

        def conv_out(g, j):
            if j == 0:
                act.wait_ge(conv_done, g + 1)
            else:
                act.wait_ge(chunk_done, KP * g + KP)
            least(act, v_done, 2 * g)
            for part in ([tok.hi[:]] if j == 0 else [tok.both[0:TAIL], tok.rest[0:TAIL]]):
                n = part.shape[0]
                act.activation(part, psum[0:n, j, :], ACT.Identity, bias=b_conv[0:n, j:j + 1]).then_inc(tok_hi, 1)

        def q_a_out(g):
            least(act, scores_done, SUB * g)
            act.wait_ge(qk_done, 3 * g + 1)
            for h in range(2):
                act.activation(q_a[:, :, h, :], images(psum[:, 2, :]), ACT.Copy, scale=head_mask[:, h:h + 1]).then_inc(qk_by_act, 1)

        def k_out(g):
            act.wait_ge(qk_done, 3 * g + 2)
            for a in range(2):
                act.activation(k_b[32 * a:32 * a + 32, a, :], psum[64 + 32 * a:96 + 32 * a, 3, :], ACT.Copy).then_inc(qk_by_act, 1)
            act.wait_ge(qk_done, 3 * g + 3)
            for a in range(2):
                act.activation(k_a[32 * a:32 * a + 32, a, :], psum[32 * a:32 * a + 32, 4, :], ACT.Copy).then_inc(qk_by_act, 1)

        def v_out(g, half):
            least(act, pv_done, SUB * g)
            act.wait_ge(v_done, 2 * g + half + 1)
            for i in range(2):
                act.activation(v_dest(half, i), v_src(half, i), ACT.Copy).then_inc(v_ready, 1)

        def exp(g, s):
            act.wait_ge(shifted, SUB * g + s + 1)
            x = probs[:, s % 2, :, :, :]
            act.activation(x, x, ACT.Exp).then_inc(exp_done, 1)

        def probs_t_out(g, s):
            act.wait_ge(probs_turned, SUB * g + s + 1)
            least(act, pv_done, SUB * g + s - 1)
            act.activation(probs_t[:, s % 2, 0:3, :], psum[:, score_banks(s), 0:384], ACT.Copy).then_inc(probs_t_act, 1)

        def att_t_out(g, s):
            act.wait_ge(att_turned, SUB * g + s + 1)
            least(act, proj_done, SUB * g + s - 1)
            act.activation(att_t[0:HC, s % 2, :, :].rearrange("p h (i q) -> p i h q", i=2),
                           psum[0:HC, 5, 0:2 * P].rearrange("p (i h q) -> p i h q", i=2, h=2), ACT.Copy)\
               .then_inc(att_t_ready, 1)

        def h1_out(g, s):
            act.wait_ge(proj_done, SUB * g + s + 1)
            least(act, xn_ready, SUB * g)
            least(act, h1_plus_act, SUB * g)
            act.activation(h1[:, s, :], psum[:, 5, 2 * P:2 * P + EMB], ACT.Copy).then_inc(h1_ready, 1)

        def residual(g):
            act.wait_ge(coef1_ready, 2 * g + 2)
            least(act, h2_ready, 2 * g)
            for s in range(SUB):
                act.activation(h1_plus[:, s, :], h1[:, s, :], ACT.Identity, scale=coef[:, 6, s:s + 1],
                               bias=coef[:, 5, s:s + 1]).then_inc(h1_plus_act, 1)

        def xn_t_out(g, j):
            act.wait_ge(xn_turned, 2 * g + j + 1)
            least(act, uv_done, 9 * g)
            for part in ([xn_t.hi[:]] if j == 0 else [xn_t.both[0:TAIL], xn_t.rest[0:TAIL]]):
                act.activation(part, psum[0:part.shape[0], 6 + j, :], ACT.Copy).then_inc(xn_hi, 1)

        def tanh_of(g, k):
            bank, cols = (6 + k % 2, 512) if k < 5 else (6 + k % 2, E_GAU)
            act.wait_ge(uv_done, 9 * g + k + 1)
            if k >= 3:
                act.wait_ge(silu_ready, 9 * g + k - 2)
            act.activation(tanh[:, k % 3, 0:cols], psum[:, bank, 0:cols], ACT.Tanh, scale=0.5).then_inc(tanh_ready, 1)

        def x3_t_out(g, j):
            act.wait_ge(x3_turned, 2 * g + j + 1)
            least(act, route_done, 2 * g)
            least(act, x3_t_kept, 32 * g)
            n = TAIL if j else P
            act.activation(x3_t[0:n, j, :], psum[0:n, 5, :], ACT.Copy).then_inc(x3_t_ready, 1)

        def x3_out(g):
            act.wait_ge(coef2_ready, g + 1)
            least(act, x3_kept, 16 * g)
            least(act, x3_turned, 2 * g)
            for s in range(SUB):
                act.activation(x3[:, s, :], h2[:, s, :], ACT.Identity, scale=coef2[:, 1, s:s + 1],
                               bias=coef2[:, 2, s:s + 1]).then_inc(x3_ready, 1)

        def front(g):
            round_patches(g + 1, (0, 3))
            exp(g, 2)
            att_t_out(g, 0)
            h1_out(g, 0)
            exp(g, 3)
            att_t_out(g, 1)
            probs_t_out(g, 2)
            h1_out(g, 1)
            probs_t_out(g, 3)
            att_t_out(g, 2)
            h1_out(g, 2)
            round_patches(g + 1, (3, 6))
            att_t_out(g, 3)
            h1_out(g, 3)
            conv_out(g + 1, 0)
            conv_out(g + 1, 1)
            act.wait_ge(fold_ready, N_FOLDS)
            round_weights(act, w_uv, uv_raw, uv_hi)
            q_a_out(g + 1)
            xn_t_out(g, 0)
            xn_t_out(g, 1)
            k_out(g + 1)
            v_out(g + 1, 0)
            v_out(g + 1, 1)
            tanh_of(g, 0)
            exp(g + 1, 0)
            tanh_of(g, 1)
            exp(g + 1, 1)
            tanh_of(g, 2)
            probs_t_out(g + 1, 0)
            tanh_of(g, 3)
            probs_t_out(g + 1, 1)
            tanh_of(g, 4)

        def both(g, more):
            b = g - 1
            residual(b)
            exp(g, 2)
            att_t_out(g, 0)
            tanh_of(b, 5)
            h1_out(g, 0)
            if more:
                round_patches(g + 1, (0, 2))
            att_t_out(g, 1)
            exp(g, 3)
            tanh_of(b, 6)
            h1_out(g, 1)
            probs_t_out(g, 2)
            tanh_of(b, 7)
            if more:
                round_patches(g + 1, (2, 3))
            probs_t_out(g, 3)
            tanh_of(b, 8)
            att_t_out(g, 2)
            if more:
                round_patches(g + 1, (3, 4))
            h1_out(g, 2)
            if more:
                round_patches(g + 1, (4, 6))
            att_t_out(g, 3)
            h1_out(g, 3)
            if more:
                conv_out(g + 1, 0)
                conv_out(g + 1, 1)
            xn_t_out(g, 0)
            xn_t_out(g, 1)
            if more:
                q_a_out(g + 1)
                k_out(g + 1)
                v_out(g + 1, 0)
                v_out(g + 1, 1)
            tanh_of(g, 0)
            x3_out(b)
            if more:
                exp(g + 1, 0)
            tanh_of(g, 1)
            x3_t_out(b, 0)
            if more:
                exp(g + 1, 1)
            tanh_of(g, 2)
            x3_t_out(b, 1)
            if more:
                probs_t_out(g + 1, 0)
            tanh_of(g, 3)
            if more:
                probs_t_out(g + 1, 1)
            tanh_of(g, 4)

        def back(g):
            residual(g)
            for k in range(5, 9):
                tanh_of(g, k)
            x3_out(g)
            x3_t_out(g, 0)
            x3_t_out(g, 1)

        act.wait_ge(patch_weights_in, 32)
        act.activation(w_conv_hi[:], w_conv_raw, ACT.Copy).then_inc(w_conv_rounded, 1)
        round_patches(0)
        act.wait_ge(const_ready, N_CONST)
        act.wait_ge(qkv_in, 48)
        round_weights(act, w_qkv, qkv_raw, qkv_hi)
        act.wait_ge(rows_set, 3)
        for t in (tok, xn_t):
            act.activation(t.rest[TAIL:REST], biased[TAIL:REST].rearrange("p s n -> p (s n)"), ACT.Copy).then_inc(rows_copied, 1)
        conv_out(0, 0)
        conv_out(0, 1)
        act.wait_ge(weights_in, ALL_WEIGHTS)
        q_a_out(0)
        k_out(0)
        v_out(0, 0)
        v_out(0, 1)
        exp(0, 0)
        exp(0, 1)
        probs_t_out(0, 0)
        probs_t_out(0, 1)
        peeled(act, front, both, back)

    @block.tensor
    def _(pe):
        def mm(out, lhs, rhs, start, stop):
            return pe.matmul(out, lhs, rhs, start=start, stop=stop)

        def conv(g, chunks=(0, KP)):
            if chunks[0] == 0:
                least(pe, probs_t_act, SUB * g)
                least(pe, probs_t_dve, SUB * g)
            for c in range(*chunks):
                pe.wait_ge(patches_split, KP * g + c + 1)
                for j in range(2):
                    w_hi, w_lo = w_conv_hi[:, c, cut(j)], w_conv_lo[:, c, cut(j)]
                    x_hi, x_lo = patch_hi[:, c % RING, :], patch_lo[:, c % RING, :]
                    for i, (w, x) in enumerate(((w_hi, x_hi), (w_lo, x_hi), (w_hi, x_lo))):
                        m = mm(psum[0:(TAIL if j else P), j, :], w, x, c == 0 and i == 0, c == KP - 1 and i == 2)
                    if j == 0 and c == KP - 1:
                        m.then_inc(conv_done, 1)
                m.then_inc(chunk_done, 1)

        def two(out, lhs, rhs):
            mm(out, lhs(HC + 1, 0), rhs(HC + 1, 0), True, False)
            return mm(out, lhs(HC, 1), rhs(HC, 1), False, True)

        def qk(g, m):
            pe.wait_ge(tok_hi, 3 * g + 3)
            pe.wait_ge(tok_lo, 2 * g + 2)
            if m < 2:
                least(pe, probs_t_act, SUB * g - 1)
                least(pe, probs_t_dve, SUB * g - 1)
            else:
                least(pe, att_ready, 2 * SUB * g)
            product(pe, psum[:, 2 + m, :], w_qkv.weights(slice(P * m, P * m + P)), tok.activations(slice(0, GT))).then_inc(qk_done, 1)

        def v(g, half):
            for s in range(2):
                t = P * (2 * half + s)
                m = product(pe, psum[:, half, EMB * s:EMB * s + EMB], tok.activations(slice(t, t + P)),
                            w_qkv.weights(slice(2 * EMB, 3 * EMB)))
            m.then_inc(v_done, 1)

        def scores(g, s):
            pe.wait_ge(qk_by_act, 6 * g + 6)
            pe.wait_ge(qk_by_dve, 4 * g + 4)
            if s == 1:
                pe.wait_ge(v_ready, 4 * g + 4)
            if s >= 2:
                pe.wait_ge(probs_t_act, SUB * g + s - 1)
                pe.wait_ge(probs_t_dve, SUB * g + s - 1)
            for i in range(2):
                t = slice(P * s + L * i, P * s + L * i + L)
                out = psum[:, score_banks(s) + i, :]
                mm(out[:, 0:4 * L], q_a[:, 2 * s + i].rearrange("p h q -> p (h q)"), k_a[:, :, t], True, True)
                m = mm(out[:, 4 * L:6 * L], q_b[:, 2 * s + i].rearrange("p h q -> p (h q)"), k_b[:, :, t], True, True)
            m.then_inc(scores_done, 1)

        def turn_probs(g, s):
            pe.wait_ge(exp_done, SUB * g + s + 1)
            for a in range(PAIRS):
                out = psum[:, score_banks(s) + a // 3, P * (a % 3):P * (a % 3) + P]
                m = pe.transpose(out, probs[:, s % 2, a].rearrange("p i k -> p (i k)"), ident)
            m.then_inc(probs_turned, 1)

        def pv(g, s):
            pe.wait_ge(probs_t_act, SUB * g + s + 1)
            pe.wait_ge(probs_t_dve, SUB * g + s + 1)
            if s > 0:
                pe.wait_ge(att_ready, 2 * (SUB * g + s))
            for a in range(PAIRS):
                m = mm(psum[:, 4, 4 * VH * a:4 * VH * a + 4 * VH], probs_t[:, s % 2, a, :],
                       v_ones[:, s, a, :, :].rearrange("p i e -> p (i e)"), True, True)
            m.then_inc(pv_done, 1)

        def turn_att(g, s):
            pe.wait_ge(att_ready, 2 * (SUB * g + s + 1))
            least(pe, h1_ready, SUB * g + s)
            if s == 0:
                least(pe, logits_read, g - 1)
            for i in range(2):
                m = pe.transpose(psum[0:HC, 5, P * i:P * i + P], att[:, s % 2, i, :, :].rearrange("p a e -> p (a e)"), ident)
            m.then_inc(att_turned, 1)

        def proj(g, s):
            pe.wait_ge(att_t_ready, SUB * g + s + 1)
            two(psum[:, 5, 2 * P:2 * P + EMB], lambda k, j: att_t[0:k, s % 2, j, :], lambda k, j: w_o[0:k, j, :]).then_inc(proj_done, 1)

        def turn_xn(g, j):
            pe.wait_ge(xn_ready, SUB * g + SUB)
            if j == 0:
                least(pe, gated_ready, EC * g)
            else:
                least(pe, h2_ready, 2 * g - 1)
            if j:
                apart(pe, pe_passed)
            for s in range(SUB):
                m = pe.transpose(psum[0:(TAIL if j else P), 6 + j, P * s:P * s + P], xn[:, s, cut(j)], ident)
            m.then_inc(xn_turned, 1)

        def uv(g, k):
            pe.wait_ge(xn_hi, 3 * g + 3)
            pe.wait_ge(xn_lo, 2 * g + 2)
            if k < 2:
                least(pe, h2_ready, 2 * g)
            if k == 7:
                pe.wait_ge(biased_ready, g + 1)
            elif k >= 2:
                pe.wait_ge(silu_ready, 9 * g + k - 1)
            if k < 5:
                col = 2 * E_GAU + P * k if k < 2 else P * (k - 2)
                m = product(pe, psum[:, 6 + k % 2, :], w_uv.weights(slice(col, col + P)), xn_t.activations(slice(0, GT)))
            else:
                t = P * (k - 5)
                m = product(pe, psum[:, 6 + k % 2, 0:E_GAU], xn_t.activations(slice(t, t + P)), w_uv.weights(slice(E_GAU, 2 * E_GAU)))
            m.then_inc(uv_done, 1)

        def gqk(g):
            pe.wait_ge(rope_ready, g + 1)
            pe.wait_ge(silu_ready, 9 * g + 6)
            for s in range(SUB):
                t = slice(P * s, P * s + P)
                m = mm(psum[:, 7, t], qk_t[:, 1, t], qk_t[:, 0, t], True, True)
            m.then_inc(gqk_done, 1)

        def kv(g, c):
            pe.wait_ge(kern_ready, g + 1)
            pe.wait_ge(silu_ready, 9 * g + 9)
            if c == 2:
                pe.wait_ge(gated_ready, EC * g + 1)
            for s in range(SUB):
                t = slice(P * s, P * s + P)
                m = mm(psum[:, 6 + c % 2, t], v_nat[:, s, P * c:P * c + P], biased[:, s, :], True, True)
            m.then_inc(kv_done, 1)

        def gau(g, half, xn_count):
            pe.wait_ge(gated_ready, EC * g + EC)
            least(pe, xn_hi, xn_count[0])
            least(pe, xn_lo, xn_count[1])
            for s in (2 * half, 2 * half + 1):
                for c in range(EC):
                    m = mm(psum[:, 7 - half, EMB * (s % 2):EMB * (s % 2) + EMB], gated[:, c, P * s:P * s + P],
                           w_gau[:, c, :], c == 0, c == EC - 1)
            m.then_inc(gau_done, 1)

        def turn_x3(g, j, h1_count):
            pe.wait_ge(x3_ready, SUB * g + SUB)
            if j == 0:
                pe.wait_ge(h1_ready, h1_count)
            else:
                pe.wait_ge(x3_t_ready, 2 * g + 1)
            if j:
                apart(pe, pe_passed)
            for s in range(SUB):
                t = slice(P * s, P * s + P)
                m = pe.transpose(psum[0:(TAIL if j else P), 5, t], x3[:, s, cut(j)], ident)
            m.then_inc(x3_turned, 1)

        def route(g, subtiles):
            pe.wait_ge(x3_t_ready, 2 * g + 2)
            for s in subtiles:
                for j in range(2):
                    k = TAIL if j else P
                    m = mm(psum[:, 5, NE * s:NE * s + NE], x3_t[0:k, j, P * s:P * s + P], w_route[0:k, j, :], j == 0, j == 1)
            m.then_inc(route_done, 1)

        def front(g):
            turn_att(g, 0)
            scores(g, 3)
            proj(g, 0)
            turn_att(g, 1)
            turn_probs(g, 2)
            proj(g, 1)
            pv(g, 2)
            turn_probs(g, 3)
            turn_att(g, 2)
            conv(g + 1, (0, 2))
            pv(g, 3)
            proj(g, 2)
            conv(g + 1, (2, 3))
            turn_att(g, 3)
            conv(g + 1, (3, 5))
            proj(g, 3)
            conv(g + 1, (5, 6))
            qk(g + 1, 0)
            qk(g + 1, 1)
            turn_xn(g, 0)
            turn_xn(g, 1)
            qk(g + 1, 2)
            v(g + 1, 0)
            v(g + 1, 1)
            pe.wait_ge(uv_hi, 3)
            pe.wait_ge(uv_lo, 3)
            uv(g, 0)
            scores(g + 1, 0)
            uv(g, 1)
            scores(g + 1, 1)
            uv(g, 2)
            turn_probs(g + 1, 0)
            uv(g, 3)
            turn_probs(g + 1, 1)
            pv(g + 1, 0)
            uv(g, 4)
            scores(g + 1, 2)
            pv(g + 1, 1)

        def both(g, more):
            b = g - 1
            turn_att(g, 0)
            uv(b, 5)
            scores(g, 3)
            proj(g, 0)
            gqk(b)
            turn_att(g, 1)
            uv(b, 6)
            proj(g, 1)
            turn_probs(g, 2)
            uv(b, 7)
            pv(g, 2)
            turn_probs(g, 3)
            uv(b, 8)
            turn_att(g, 2)
            if more:
                conv(g + 1, (0, 1))
            kv(b, 0)
            pv(g, 3)
            proj(g, 2)
            if more:
                conv(g + 1, (1, 3))
            kv(b, 1)
            turn_att(g, 3)
            kv(b, 2)
            if more:
                conv(g + 1, (3, 4))
            proj(g, 3)
            if more:
                conv(g + 1, (4, 6))
            gau(b, 0, (0, 0))
            if more:
                qk(g + 1, 0)
                qk(g + 1, 1)
            turn_xn(g, 0)
            turn_xn(g, 1)
            if more:
                qk(g + 1, 2)
            if more:
                v(g + 1, 0)
            gau(b, 1, (3 * g + 1, 2 * g + 1))
            if more:
                v(g + 1, 1)
            uv(g, 0)
            if more:
                scores(g + 1, 0)
            uv(g, 1)
            if more:
                scores(g + 1, 1)
            turn_x3(b, 0, SUB * g + SUB)
            uv(g, 2)
            if more:
                turn_probs(g + 1, 0)
            turn_x3(b, 1, 0)
            uv(g, 3)
            if more:
                turn_probs(g + 1, 1)
            uv(g, 4)
            if more:
                pv(g + 1, 0)
            route(b, (0, 1))
            if more:
                scores(g + 1, 2)
            route(b, (2, 3))
            if more:
                pv(g + 1, 1)

        def back(g):
            uv(g, 5)
            gqk(g)
            for k in range(6, 9):
                uv(g, k)
            for c in range(EC):
                kv(g, c)
            gau(g, 0, (0, 0))
            gau(g, 1, (0, 0))
            turn_x3(g, 0, SUB * g + SUB)
            turn_x3(g, 1, 0)
            route(g, (0, 1))
            route(g, (2, 3))

        pe.wait_ge(w_conv_split, 1)
        conv(0)
        pe.wait_ge(qkv_hi, 3)
        pe.wait_ge(qkv_lo, 3)
        pe.wait_ge(rows_copied, 2)
        for m in range(3):
            qk(0, m)
        v(0, 0)
        v(0, 1)
        scores(0, 0)
        scores(0, 1)
        pe.wait_ge(weights_in, ALL_WEIGHTS)
        pe.wait_ge(const_ready, N_CONST)
        for n in range(2):
            for j in range(2):
                k = TAIL if j else P
                m = mm(psum[0:REST, 6 + n, :], beta[0:k, j, :], uv_raw[j][0:k, 512 * n:512 * n + 512], j == 0, j == 1)
        m.then_inc(fold_done, 1)
        turn_probs(0, 0)
        turn_probs(0, 1)
        pv(0, 0)
        scores(0, 2)
        pv(0, 1)
        peeled(pe, front, both, back)

    @block.vector
    def _(dve):
        def fold(ins, n):
            ins.then_inc(fold_ready, 1)
            dve.wait_ge(fold_ready, n)

        def rotary_tables():
            dve.wait_ge(rows_copied, 2)
            for q in range(2):
                fold(dve.tensor_scalar(rope_tab[:, 0, q, :], rope[:, 0, :], qk_gain[:, q, 0:1], 0.5, ALU.mult, ALU.mult), 5 * q + 1)
                fold(dve.tensor_scalar(rope_tab[:, 1, q, :], rope[:, 1, :], qk_gain[:, q, 1:2], 0.5, ALU.mult, ALU.mult), 5 * q + 2)
                fold(dve.tensor_scalar(rope_tab[:, 2, q, :], rope[:, 0, :], qk_shift[:, q, 0:1], None, ALU.mult), 5 * q + 3)
                fold(dve.tensor_scalar(biased[:, q, 0:L], rope[:, 1, :], qk_shift[:, q, 1:2], None, ALU.mult), 5 * q + 4)
                fold(dve.tensor_tensor(rope_tab[:, 2, q, :], rope_tab[:, 2, q, :], biased[:, q, 0:L], ALU.add), 5 * q + 5)

        def fold_norm():
            dve.wait_ge(fold_done, 1)
            fold(dve.tensor_scalar(uv_raw[0], uv_raw[0], gamma[:, 0:1], None, ALU.mult), 11)
            fold(dve.tensor_scalar(uv_raw[1], uv_raw[1], gamma[:, 1:2], None, ALU.mult), 12)
            raw = uv_raw[2][0:REST].rearrange("p (a b) -> p a b", a=2)
            fold(dve.scalar_tensor_tensor(raw, raw, gamma[0:REST, 2:3], psum[0:REST, 6:8, :], ALU.mult, ALU.add), N_FOLDS)

        def split_patches(g, chunks=(0, KP)):
            for c in range(*chunks):
                dve.wait_ge(patches_rounded, KP * g + c + 1)
                dve.tensor_tensor(patch_lo[:, c % RING, :], patches[:, c, :], patch_hi[:, c % RING, :].bitcast(F32), ALU.subtract).then_inc(patches_split, 1)

        def tok_lo_out(g, j):
            dve.wait_ge(tok_hi, 3 * g + (3 if j else 1))
            least(dve, v_done, 2 * g)
            hi, lo = (tok.both[0:TAIL], tok.both[TAIL:P]) if j else (tok.hi[:], tok.lo[:])
            n = hi.shape[0]
            dve.scalar_tensor_tensor(lo, psum[0:n, j, :], b_conv[0:n, j:j + 1], hi.bitcast(F32), ALU.add, ALU.subtract).then_inc(tok_lo, 1)

        def xn_lo_out(g, j):
            dve.wait_ge(xn_hi, 3 * g + (3 if j else 1))
            least(dve, uv_done, 9 * g)
            hi, lo = (xn_t.both[0:TAIL], xn_t.both[TAIL:P]) if j else (xn_t.hi[:], xn_t.lo[:])
            dve.tensor_tensor(lo, psum[0:hi.shape[0], 6 + j, :], hi.bitcast(F32), ALU.subtract).then_inc(xn_lo, 1)

        def qk_out(g):
            least(dve, scores_done, SUB * g)
            dve.wait_ge(qk_done, 3 * g + 2)
            for h in range(2):
                dve.tensor_scalar(q_b[0:64, :, h, :], images(psum[0:64, 3, :]), head_mask[0:64, h:h + 1], None, ALU.mult).then_inc(qk_by_dve, 1)
            dve.wait_ge(qk_done, 3 * g + 3)
            for a in range(2, 4):
                dve.tensor_copy(k_a[32 * a:32 * a + 32, a, :], psum[32 * a:32 * a + 32, 4, :]).then_inc(qk_by_dve, 1)

        def shift(g, s):
            dve.wait_ge(scores_done, SUB * g + s + 1)
            x = psum[:, score_banks(s):score_banks(s) + 2, 0:PAIRS * L].rearrange("p i (a k) -> p i a k", k=L)
            top = row_max[:, s % 2, :, :]
            dve.tensor_reduce(top, x, AX.X, ALU.max).then_inc(max_ready, 1)
            dve.wait_ge(max_ready, SUB * g + s + 1)
            least(dve, probs_turned, SUB * g + s - 1)
            dve.tensor_tensor(probs[:, s % 2].rearrange("p a i k -> p i a k"), x, top.unsqueeze(3).broadcast_to([P, 2, PAIRS, L]), ALU.subtract)\
                .then_inc(shifted, 1)

        def probs_t_out(g, s):
            dve.wait_ge(probs_turned, SUB * g + s + 1)
            least(dve, pv_done, SUB * g + s - 1)
            dve.tensor_copy(probs_t[:, s % 2, 3:6, :].rearrange("p a q -> p (a q)"), psum[:, score_banks(s) + 1, 0:384]).then_inc(probs_t_dve, 1)

        def normalise(g, s):
            dve.wait_ge(pv_done, SUB * g + s + 1)
            least(dve, att_turned, SUB * g + s - 1)
            o = psum[:, 4, 0:PAIRS * 4 * VH].rearrange("p (a i e) -> p a i e", i=2, e=2 * VH)
            for h in range(2):
                r = slice(64 * h, 64 * h + 64)
                dve.reciprocal(inv_sum[r, s % 2, :, :], o[r, :, :, VH * h + HD]).then_inc(inv_ready, 1)
            dve.wait_ge(inv_ready, 2 * (SUB * g + s + 1))
            for h in range(2):
                r = slice(64 * h, 64 * h + 64)
                dve.tensor_tensor(att[r, s % 2, :, :, :].rearrange("p i a e -> p a i e"), o[r, :, :, VH * h:VH * h + HD],
                                  inv_sum[r, s % 2, :, :].unsqueeze(3).broadcast_to([64, PAIRS, 2, HD]), ALU.mult)\
                   .then_inc(att_ready, 1)

        def moments1(g, s):
            dve.wait_ge(h1_ready, SUB * g + s + 1)
            if s == 0 and (not isinstance(g, int) or g > 0):
                dve.wait_ge(coef1_ready, 2 * g)
            dve.bn_stats(stats1[:, s, :], h1[:, s, :]).then_inc(stat_step, 1)

        def moments1_end(g, stat_base):
            dve.wait_ge(stat_step, stat_base + 4)
            apart(dve, dve_passed)
            for s in range(SUB):
                ins = dve.bn_aggr(mean_var1[:, s, :], stats1[:, s, :]).then_inc(stat_step, 1)
            dve.wait_ge(stat_step, stat_base + 8)
            dve.tensor_scalar(coef[:, 0, :], mean_var1[:, :, 1], EPS, None, ALU.add).then_inc(var1_ready, 1)

        def xn_out(g):
            dve.wait_ge(coef1_ready, 2 * g + 2)
            least(dve, xn_turned, 2 * g)
            for s in range(SUB):
                dve.tensor_scalar(xn[:, s, :], h1[:, s, :], mean_var1[:, s, 0:1], coef[:, 7, s:s + 1],
                                  ALU.subtract, ALU.mult).then_inc(xn_ready, 1)

        def silu(g, k):
            bank, cols = (6 + k % 2, 512) if k < 5 else (6 + k % 2, E_GAU)
            dve.wait_ge(tanh_ready, 9 * g + k + 1)
            if k == 1:
                least(dve, rope_2_half, g)
            if k == 5:
                least(dve, kv_done, EC * g)
            dest = base[:, k, :] if k < 2 else u_t[:, k - 2, :] if k < 5 else v_nat[:, k - 5, :]
            dve.scalar_tensor_tensor(dest, tanh[:, k % 3, 0:cols], 1.0, psum[:, bank, 0:cols], ALU.add, ALU.mult)\
               .then_inc(silu_ready, 1)

        def rope_first(g):
            dve.wait_ge(silu_ready, 9 * g + 1)
            dve.tensor_tensor(by_image(rope_1), of_base(base[:, 0, :]), table(0), ALU.mult).then_inc(rope_1_ready, 1)

        def rope_out(g):
            dve.wait_ge(rope_1_ready, g + 1)
            dve.wait_ge(rope_2_ready, g + 1)
            least(dve, gqk_done, g)
            dve.tensor_tensor(qk_t[:], rope_1[:], rope_2[:], ALU.add).then_inc(rope_ready, 1)

        def kern_out(g):
            dve.wait_ge(gqk_done, g + 1)
            least(dve, kv_done, EC * g)
            dve.scalar_tensor_tensor(biased[:], psum[:, 7, :].rearrange("p (s n) -> p s n", n=P), 1.0 / L,
                                     rel_bias[:].unsqueeze(1).broadcast_to([P, SUB, P]), ALU.mult, ALU.add).then_inc(biased_ready, 1)
            dve.wait_ge(biased_ready, g + 1)
            dve.scalar_tensor_tensor(biased[:], biased[:], 0.0, biased[:], ALU.max, ALU.mult).then_inc(kern_ready, 1)

        def gate_out(g, c):
            dve.wait_ge(kv_done, EC * g + c + 1)
            least(dve, gau_done, 2 * g)
            if c == 0:
                least(dve, route_done, 2 * g)
                least(dve, x3_t_kept, 32 * g)
            dve.scalar_tensor_tensor(gated[:, c, :], u_t[:, c, :], 0.25, psum[:, 6 + c % 2, :], ALU.mult, ALU.mult)\
               .then_inc(gated_ready, 1)

        def h2_out(g, half):
            dve.wait_ge(gau_done, 2 * g + half + 1)
            dve.wait_ge(h1_plus_ready, g + 1)
            least(dve, h2_kept, 16 * g)
            s = slice(2 * half, 2 * half + 2)
            dve.tensor_tensor(h2[:, s, :], psum[:, 7 - half, 0:2 * EMB].rearrange("p (s e) -> p s e", e=EMB),
                              h1_plus[:, s, :], ALU.add).then_inc(h2_ready, 1)

        def moments2(g, stat_base):
            dve.wait_ge(h2_ready, 2 * g + 2)
            least(dve, coef2_ready, g)
            for s in range(SUB):
                dve.bn_stats(stats2[:, s, :], h2[:, s, :]).then_inc(stat_step, 1)
            dve.wait_ge(stat_step, stat_base + 4)
            apart(dve, dve_passed)
            for s in range(SUB):
                dve.bn_aggr(mean_var2[:, s, :], stats2[:, s, :]).then_inc(stat_step, 1)
            dve.wait_ge(stat_step, stat_base + 8)
            dve.tensor_scalar(coef2[:, 0, :], mean_var2[:, :, 1], EPS, None, ALU.add).then_inc(var2_ready, 1)

        def logits_out(g):
            dve.wait_ge(route_done, 2 * g + 2)
            dve.tensor_copy(logits_all[:, bass.ds(SUB * g, SUB), :], psum[:, 5, 0:SUB * NE].rearrange("p (s e) -> p s e", e=NE)).then_inc(logits_read, 1)

        def front(g):
            normalise(g, 1)
            shift(g, 3)
            probs_t_out(g, 2)
            split_patches(g + 1, (0, 3))
            normalise(g, 2)
            probs_t_out(g, 3)
            fold_norm()
            normalise(g, 3)
            split_patches(g + 1, (3, 6))
            for s in range(SUB):
                moments1(g, s)
            moments1_end(g, 0)
            tok_lo_out(g + 1, 0)
            tok_lo_out(g + 1, 1)
            xn_out(g)
            rest_of_weights(dve, w_uv, uv_raw, uv_hi, uv_lo)
            xn_lo_out(g, 0)
            xn_lo_out(g, 1)
            qk_out(g + 1)
            silu(g, 0)
            shift(g + 1, 0)
            silu(g, 1)
            shift(g + 1, 1)
            silu(g, 2)
            probs_t_out(g + 1, 0)
            silu(g, 3)
            probs_t_out(g + 1, 1)
            normalise(g + 1, 0)
            rope_first(g)
            silu(g, 4)
            shift(g + 1, 2)

        def both(g, more):
            b = g - 1
            normalise(g, 1)
            rope_out(b)
            silu(b, 5)
            shift(g, 3)
            kern_out(b)
            silu(b, 6)
            probs_t_out(g, 2)
            if more:
                split_patches(g + 1, (0, 2))
            silu(b, 7)
            normalise(g, 2)
            probs_t_out(g, 3)
            silu(b, 8)
            if more:
                split_patches(g + 1, (2, 4))
            gate_out(b, 0)
            normalise(g, 3)
            if more:
                split_patches(g + 1, (4, 6))
            gate_out(b, 1)
            gate_out(b, 2)
            for s in range(SUB):
                moments1(g, s)
            moments1_end(g, 16 * g - 8)
            if more:
                tok_lo_out(g + 1, 0)
            if more:
                tok_lo_out(g + 1, 1)
            xn_out(g)
            h2_out(b, 0)
            xn_lo_out(g, 0)
            xn_lo_out(g, 1)
            if more:
                qk_out(g + 1)
            h2_out(b, 1)
            moments2(b, 16 * g)
            silu(g, 0)
            if more:
                shift(g + 1, 0)
            silu(g, 1)
            if more:
                shift(g + 1, 1)
            silu(g, 2)
            if more:
                probs_t_out(g + 1, 0)
            silu(g, 3)
            if more:
                probs_t_out(g + 1, 1)
                normalise(g + 1, 0)
            rope_first(g)
            silu(g, 4)
            logits_out(b)
            if more:
                shift(g + 1, 2)

        def back(g):
            rope_out(g)
            silu(g, 5)
            kern_out(g)
            for k in range(6, 9):
                silu(g, k)
            for c in range(EC):
                gate_out(g, c)
            h2_out(g, 0)
            h2_out(g, 1)
            moments2(g, 16 * g + 8)
            logits_out(g)

        dve.wait_ge(w_conv_rounded, 1)
        dve.tensor_tensor(w_conv_lo[:], w_conv_raw, w_conv_hi[:].bitcast(F32), ALU.subtract).then_inc(w_conv_split, 1)
        split_patches(0)
        dve.wait_ge(const_ready, N_CONST)
        rest_of_weights(dve, w_qkv, qkv_raw, qkv_hi, qkv_lo)
        tok_lo_out(0, 0)
        tok_lo_out(0, 1)
        dve.wait_ge(weights_in, ALL_WEIGHTS)
        rotary_tables()
        qk_out(0)
        shift(0, 0)
        shift(0, 1)
        probs_t_out(0, 0)
        probs_t_out(0, 1)
        normalise(0, 0)
        shift(0, 2)
        peeled(dve, front, both, back)
        dve.wait_ge(logits_read, G)


def experts(nc, d, scope, psum, w2, x3_all, ws1_raw, logits_all, consts, ident):
    def sb(name, shape, dt=F32):
        return scope.enter_context(nc.sbuf_tensor(name, shape, dt))

    def sem(name):
        return scope.enter_context(nc.semaphore(name))

    tri = consts[:, P:2 * P]
    experts_iota = consts[:, 2 * P:2 * P + NE]
    slot_starts = consts[:, 2 * P + NE:2 * P + NE + SLOTS + 1]
    w1 = Packed(sb, "w1", NE * HID)
    b2 = sb("b2_sb", [P, NE, EMB])
    ws1 = Packed(sb, "ws1", HID)
    ws2_hi = sb("ws2_hi", [P, HK, EMB], F32R)
    ws2_lo = sb("ws2_lo", [P, HK, EMB], F32R)
    h_t = sb("h_t", [P, 2, HK, SLOT])
    h_t_flat = h_t[:].rearrange("p q c t -> p (q c t)")
    ws2_raw = h_t_flat[:, 0:HK * EMB].rearrange("p (c n) -> p c n", n=EMB)
    w1_raw = [h_t_flat[:, HID * i:HID * i + HID] for i in range(3)]
    h2_in, out_rows = (h_t_flat[:, 3 * HID + HS * EMB * i:3 * HID + HS * EMB * (i + 1)].rearrange("p (s e) -> p s e", e=EMB)
                       for i in range(2))
    bs2 = sb("bs2_sb", [P, EMB])
    x3_in = sb("x3_in", [P, 2, HT])
    x3_t = Packed(sb, "x3_t", HT)
    hs_hi = sb("hs_hi", [P, HK, HT], F32R)
    hs_lo = sb("hs_lo", [P, HK, HT], F32R)
    ones = sb("ones", [P, P])
    routing = sb("routing", [P, 2 * TOPK, NT, NE])
    chosen, running = routing[:, 0:TOPK], routing[:, TOPK:2 * TOPK]
    x_slot = routing[:].rearrange("p q t e -> p (q t e)")[:, 0:4 * ROW].rearrange("p (q j w) -> p q j w", q=2, w=ROW)
    mask = sb("mask", [P, NT, NE])
    place = sb("place", [P, NT, NE])
    rows_f = sb("rows_f", [P, TOPK, NT])
    rows = sb("rows", [P, TOPK, NT], U32)
    top = sb("top", [P, TOPK, NT])
    at_expert = sb("at_expert", [P, NT])
    gap = sb("gap", [P, NT])
    gate = sb("gate", [P, 3, NT])
    padded_i = sb("padded_i", [P, NE], I32)
    padded = sb("padded", [P, NE])
    ends = sb("ends", [P, 2, NE])
    starts = sb("starts", [P, NE])
    past = sb("past", [1, SLOTS + 1, NE])
    slot_expert_f = sb("slot_expert_f", [1, SLOTS + 1])
    slot_expert = sb("slot_expert", [1, SLOTS + 1], I32)
    meta = sb("meta", [P, SLOTS + 1, 2, 2])
    y_slot = sb("y_slot", [P, 2, 2, EMB])
    tokens = sb("tokens", [P, 2], U32)

    x3t_in, shared_in, b2_in, w2_in, h2_loaded = sem("x3t_in"), sem("shared_in"), sem("b2_in"), sem("w2_in"), sem("h2_loaded")
    shared_hi, shared_lo, rows_copied, bias_scaled = sem("shared_hi"), sem("shared_lo"), sem("rows_copied"), sem("bias_scaled")
    x_hi, x_lo, hs_done, hs_hi_ready, hs_lo_ready = sem("x_hi"), sem("x_lo"), sem("hs_done"), sem("hs_hi_ready"), sem("hs_lo_ready")
    ys_done, h2_plus, shared_ready, out_stored = sem("ys_done"), sem("h2_plus"), sem("shared_ready"), sem("out_stored")
    ones_ready, mask_ready, ranks_done, route_step = sem("ones_ready"), sem("mask_ready"), sem("ranks_done"), sem("route_step")
    ranks_read = sem("ranks_read")
    gates_ready = sem("gates_ready")
    gap_ready, gap_exp, table_ready = sem("gap_ready"), sem("gap_exp"), sem("table_ready")
    rows_ready, gate_set = sem("rows_ready"), sem("gate_set")
    dispatched = [sem(f"dispatched{q}") for q in range(QUARTERS)]
    meta_ready = sem("meta_ready")
    x_slot_in = [sem("x_slot_in0"), sem("x_slot_in1")]
    x_turned, x_t_hi, x_t_lo = sem("x_turned"), sem("x_t_hi"), sem("x_t_lo")
    w1_main_in, w1_tail_in, w1_hi, w1_lo = sem("w1_main_in"), sem("w1_tail_in"), sem("w1_hi"), sem("w1_lo")
    w1_by_act, w1_by_dve = sem("w1_by_act"), sem("w1_by_dve")
    h_done, h_by_act, h_by_dve = sem("h_done"), sem("h_by_act"), sem("h_by_dve")
    y_done, y_plain_ready, y_ready = sem("y_done"), sem("y_plain_ready"), sem("y_ready")
    tokens_ready, added, pool_passed = sem("tokens_ready"), sem("added"), sem("pool_passed")
    SHARED_LOADS = 16 * 2
    HALVES = 2 * G
    RANKS = 6
    HS_BANKS = (0, 1, 2, 7)

    def hs_bank(half, c):
        return HS_BANKS[(HK * half + c) % len(HS_BANKS)]

    def expert_part(tile, e):
        return tile[:, HID * e:HID * e + HID] if isinstance(e, int) else tile[:, bass.ds(HID * e, HID)]

    def groups(eng, body):
        body(0, True)
        with eng.Fori(1, G - 1) as g:
            body(g, True)
        body(G - 1, False)

    def h_pair(b):
        return psum[:, 1 + b, :]

    def slots(eng, step):
        assert (SLOTS - 3) % 4 == 0
        step(1, 1, 0)
        step(2, 0, 1)
        with eng.Fori(0, (SLOTS - 3) // 4) as i:
            step(4 * i + 3, 1, 2 * i + 1)
            step(4 * i + 4, 0, 2 * i + 2)
            step(4 * i + 5, 1, 2 * i + 2)
            step(4 * i + 6, 0, 2 * i + 3)

    block = scope.enter_context(nc.Block())

    @block.sync
    def _(sp):
        def load_x3(g, half):
            t = slice(HT * half, HT * half + HT)
            for j, n in ((0, P), (1, TAIL)):
                sp.dma_start(x3_in[0:n, j, :], d["x3t"][bass.ds(g, 1), 0:n, j, t].rearrange("a p t -> p (a t)")).then_inc(x3t_in, 16)

        def load_h2(g, half):
            sp.dma_start(h2_in, d["h2"][bass.ds(g, 1), :, HS * half:HS * half + HS, :].rearrange("a p s e -> p (a s) e")).then_inc(h2_loaded, 16)

        def load_w1_main(e):
            sp.dma_start(w1_raw[0], d["w1"][bass.ds(e, 1), :, 0, :].rearrange("a p n -> p (a n)")).then_inc(w1_main_in, 16)

        def load_w1_tail(e):
            for i in (1, 2):
                sp.dma_start(w1_raw[i], d["w1"][bass.ds(e, 1), :, i, :].rearrange("a p n -> p (a n)")).then_inc(w1_tail_in, 16)

        def load(s, par):
            sp.dma_start(x_slot[:, par], d["slot_rows"][bass.ds(SLOT * s, SLOT), :].rearrange("(j p) w -> p j w", p=P)).then_inc(x_slot_in[par], 16)

        load_x3(0, 0)
        sp.dma_start(ws2_raw, d["ws2"]).then_inc(shared_in, 16)
        sp.dma_start(bs2[:], d["bs2"].broadcast_to([P, EMB])).then_inc(shared_in, 16)
        load_h2(0, 0)
        sp.dma_start(b2[:].rearrange("p e n -> p (e n)"), d["b2"].broadcast_to([P, NE * EMB])).then_inc(b2_in, 16)

        def store(h):
            sp.wait_ge(shared_ready, HS * h + HS)
            sp.dma_start(d["out"][bass.ds(HT * h, HT), :].rearrange("(s p) e -> p s e", p=P), out_rows).then_inc(out_stored, 16)

        def half_group(g, half, first, more):
            h = 2 * g + half
            if more:
                sp.wait_ge(x_hi, 3 * h + 3)
                sp.wait_ge(x_lo, 2 * h + 2)
                load_x3(g + half, 1 - half)
            if half == 1 or not first:
                store(h - 1)
                load_h2(g, half)
            if half == 0:
                if first:
                    sp.wait_ge(shared_hi, 4)
                    sp.wait_ge(shared_lo, 4)
                else:
                    sp.wait_ge(w1_hi, 3 * g - 2)
                    sp.wait_ge(w1_lo, 3 * g - 2)
                load_w1_main(g)
            else:
                if not first:
                    sp.wait_ge(w1_hi, 3 * g)
                    sp.wait_ge(w1_lo, 3 * g)
                load_w1_tail(g)

        def group(g, more):
            first = isinstance(g, int) and g == 0
            half_group(g, 0, first, True)
            half_group(g, 1, first, more)

        groups(sp, group)
        for q in range(QUARTERS):
            sp.wait_ge(dispatched[q], 16 * TOPK * QT)
        load(0, 0)
        load(1, 1)
        store(HALVES - 1)
        with sp.Fori(0, (SLOTS - 1) // 2) as i:
            sp.wait_ge(x_turned, 2 * i + 1)
            sp.wait_ge(meta_ready, 2 * i + 1)
            load(2 * i + 2, 0)
            sp.wait_ge(x_turned, 2 * i + 2)
            sp.wait_ge(meta_ready, 2 * i + 2)
            load(2 * i + 3, 1)
        sp.wait_ge(out_stored, 16 * HALVES)

    @block.gpsimd
    def _(pool):
        for n, (tile, value) in enumerate(((ones[:], 1.0), (x3_in[TAIL:REST, 1, :], 0.0), (x3_in[TAIL:TAIL + 1, 1, :], 1.0),
                                           (x3_in[REST - 1:REST, 1, :], 1.0))):
            pool.memset(tile, value).then_inc(ones_ready, 1)
            pool.wait_ge(ones_ready, n + 1)
        def load_w2(experts):
            for e in experts:
                pool.dma_start(w2[:, e], d["w2"][:, e]).then_inc(w2_in, 16)

        def dispatch(k, q):
            for t in range(QT * q, QT * q + QT):
                pool.indirect_dma_start(out=d["slot_rows"], out_offset=bass.IndirectOffsetOnAxis(ap=rows[:, k, t:t + 1], axis=0),
                                        in_=x3_all[:, t, :], in_offset=None).then_inc(dispatched[q], 16)

        behind = -(-NT * ROW // (HK * EMB))
        freed = [min(QT * q * ROW // (HK * EMB), behind) for q in range(QUARTERS)] + [behind]
        pool.wait_ge(shared_hi, 3)
        pool.wait_ge(shared_lo, 3)
        load_w2(range(behind, NE))
        pool.wait_ge(rows_ready, 1)
        pool.wait_ge(gates_ready, 1)
        pool.tensor_copy(x3_all[:, :, EMB], gate[:, 0, :]).then_inc(gate_set, 1)
        pool.wait_ge(gate_set, 1)
        for q in range(QUARTERS + 2):
            if q < QUARTERS:
                dispatch(0, q)
            if 0 <= q - 1 < QUARTERS:
                pool.wait_ge(dispatched[q - 1], 16 * QT)
                pool.tensor_copy(x3_all[:, QT * (q - 1):QT * q, EMB], gate[:, 1, QT * (q - 1):QT * q]).then_inc(gate_set, 1)
                pool.wait_ge(gate_set, q + 1)
                dispatch(1, q - 1)
            if q >= 2:
                pool.wait_ge(dispatched[q - 2], 16 * TOPK * QT)
                load_w2(range(freed[q - 2], freed[q - 1]))
        pool.wait_ge(out_stored, 16 * HALVES)

        def take_meta(s, par, half):
            pool.wait_ge(x_slot_in[par], 16 * (half + 1))
            apart(pool, pool_passed)
            pool.tensor_copy(meta[:, bass.ds(s, 1)].rearrange("p a j w -> p (a j) w"), x_slot[:, par, :, EMB:ROW]).then_inc(meta_ready, 1)

        def add_rows(s, par, half):
            take_meta(s + 1, 1 - par, half + par)
            pool.wait_ge(meta_ready, s + 1)
            least(pool, added, 32 * s)
            for j in range(2):
                apart(pool, pool_passed)
                pool.tensor_copy(tokens[:, j:j + 1], meta[:, bass.ds(s, 1), j, 1]).then_inc(tokens_ready, 1)
                pool.wait_ge(tokens_ready, 2 * s + j + 1)
                pool.wait_ge(y_ready, 2 * s + j + 1)
                apart(pool, pool_passed)
                pool.indirect_dma_start(out=d["out"], out_offset=bass.IndirectOffsetOnAxis(ap=tokens[:, j:j + 1], axis=0),
                                        in_=y_slot[:, j, 1, :], in_offset=None, compute_op=ALU.add).then_inc(added, 16)

        take_meta(0, 0, 0)
        add_rows(0, 0, 0)
        slots(pool, add_rows)
        pool.wait_ge(added, 32 * SLOTS)

    @block.scalar
    def _(act):
        def x_hi_out(h):
            act.wait_ge(x3t_in, 32 * (h + 1))
            least(act, hs_done, HK * h)
            act.activation(x3_t.hi[:], x3_in[:, 0, :], ACT.Copy).then_inc(x_hi, 1)
            for part in (x3_t.both[0:TAIL], x3_t.rest[0:TAIL]):
                act.activation(part, x3_in[0:TAIL, 1, :], ACT.Copy).then_inc(x_hi, 1)

        def hs_hi_out(h, half):
            least(act, ys_done, HS * h)
            for c in range(HK):
                act.wait_ge(hs_done, HK * h + c + 1)
                act.activation(hs_hi[:, c, :], psum[:, hs_bank(half, c), 0:HT], ACT.Relu).then_inc(hs_hi_ready, 1)

        def w1_main_hi(e):
            act.wait_ge(w1_main_in, 16 * (e + 1))
            act.activation(expert_part(w1.hi, e), w1_raw[0], ACT.Copy).then_inc(w1_hi, 1)

        def w1_tail_hi(e):
            act.wait_ge(w1_tail_in, 32 * (e + 1))
            act.activation(expert_part(w1.rest, e), w1_raw[2][0:REST], ACT.Copy).then_inc(w1_hi, 1)
            act.activation(expert_part(w1.both, e), w1_raw[1], ACT.Copy).then_inc(w1_hi, 1)

        def group(g, more):
            hs_hi_out(2 * g, 0)
            x_hi_out(2 * g + 1)
            if isinstance(g, int) and g == 0:
                hs_hi_out(2 * g + 1, 1)
                act.wait_ge(gap_ready, 1)
                act.activation(gate[:, 2, :], gap[:], ACT.Exp).then_inc(gap_exp, 1)
            else:
                w1_tail_hi(g - 1)
                hs_hi_out(2 * g + 1, 1)
            if more:
                x_hi_out(2 * g + 2)
            w1_main_hi(g)

        round_weights(act, ws1, ws1_raw, shared_hi)
        act.wait_ge(ones_ready, 4)
        act.activation(x3_t.rest[TAIL:REST], x3_in[TAIL:REST, 1, :], ACT.Copy).then_inc(rows_copied, 1)
        x_hi_out(0)
        act.wait_ge(shared_in, SHARED_LOADS)
        act.activation(ws2_hi[:], ws2_raw, ACT.Copy).then_inc(shared_hi, 1)
        groups(act, group)
        w1_tail_hi(NE - 1)

        def x_t_out(s):
            act.wait_ge(x_turned, s + 1)
            least(act, h_done, HK // 2 * s)
            act.activation(x3_t.hi[:], psum[:, 0, 0:SLOT], ACT.Copy).then_inc(x_t_hi, 1)
            for part in (x3_t.both[0:TAIL], x3_t.rest[0:TAIL]):
                act.activation(part, psum[0:TAIL, 0, SLOT:2 * SLOT], ACT.Copy).then_inc(x_t_hi, 1)

        def h_out(s, par, b):
            least(act, y_done, 2 * s - 2)
            act.wait_ge(h_done, HK // 2 * s + b + 1)
            act.activation(h_t[:, par, 2 * b:2 * b + 2, :].rearrange("p c t -> p (c t)"), h_pair(b), ACT.Relu).then_inc(h_by_act, 1)

        def y_out(s):
            act.wait_ge(meta_ready, s + 1)
            least(act, added, 32 * s)
            for j in range(2):
                act.wait_ge(y_plain_ready, 2 * s + j + 1)
                act.activation(y_slot[:, j, 1, :], y_slot[:, j, 0, :], ACT.Copy, scale=meta[:, bass.ds(s, 1), j, 0]).then_inc(y_ready, 1)

        def w1_out(s):
            e = act.value_load(slot_expert[0:1, bass.ds(s, 1)], min_val=0, max_val=NE - 1)
            least(act, h_done, HK // 2 * s)
            for now, w in ((ws1.hi, w1.hi), (ws1.both, w1.both)):
                act.activation(now[:], w[:, bass.ds(HID * e, HID)], ACT.Copy).then_inc(w1_by_act, 1)

        def step(s, par, half):
            h_out(s, par, 0)
            w1_out(s + 1)
            x_t_out(s + 1)
            h_out(s, par, 2)
            y_out(s - 1)

        x_t_out(0)
        act.wait_ge(table_ready, 1)
        act.wait_ge(hs_done, HK * HALVES)
        w1_out(0)
        act.wait_ge(w1_lo, 3 * NE)
        h_out(0, 0, 0)
        w1_out(1)
        x_t_out(1)
        h_out(0, 0, 2)
        act.wait_ge(out_stored, 16 * HALVES)
        slots(act, step)
        y_out(SLOTS - 1)

    @block.tensor
    def _(pe):
        def hs(h, half):
            pe.wait_ge(x_hi, 3 * h + 3)
            pe.wait_ge(x_lo, 2 * h + 2)
            for c in range(HK):
                least(pe, hs_lo_ready, HK * h + c - 3)
                product(pe, psum[:, hs_bank(half, c), 0:HT], ws1.weights(slice(P * c, P * c + P)), x3_t.activations(slice(0, HT))).then_inc(hs_done, 1)

        def ys(h, half):
            for s in range(HS):
                least(pe, shared_ready, HS * h + s - 3)
                if 3 + HS * half + s == RANKS and isinstance(h, int) and h == 1:
                    pe.wait_ge(ranks_read, 1)
                for c in range(HK):
                    if s == 0:
                        pe.wait_ge(hs_lo_ready, HK * h + c + 1)
                    for i, (h_part, w_part) in enumerate(((hs_hi, ws2_hi), (hs_hi, ws2_lo), (hs_lo, ws2_hi))):
                        m = pe.matmul(psum[:, 3 + HS * half + s, 0:EMB], h_part[:, c, P * s:P * s + P], w_part[:, c, :],
                                      start=(c == 0 and i == 0), stop=(c == HK - 1 and i == 2))
                m.then_inc(ys_done, 1)

        def group(g, more):
            first = isinstance(g, int) and g == 0
            hs(2 * g, 0)
            if first:
                pe.wait_ge(shared_hi, 4)
                pe.wait_ge(shared_lo, 4)
            ys(2 * g, 0)
            hs(2 * g + 1, 1)
            if first:
                pe.wait_ge(mask_ready, 1)
                flat = mask[:].rearrange("p t e -> p (t e)")
                pe.matmul(psum[:, RANKS, 0:NT * NE], tri, flat, start=True, stop=True)
                pe.matmul(psum[:, RANKS, NT * NE:2 * NT * NE], ones[:], flat, start=True, stop=True).then_inc(ranks_done, 1)
            ys(2 * g + 1, 1)

        pe.wait_ge(shared_hi, 3)
        pe.wait_ge(shared_lo, 3)
        pe.wait_ge(rows_copied, 1)
        pe.wait_ge(ones_ready, 4)
        groups(pe, group)

        def expert(s):
            return pe.value_load(slot_expert[0:1, bass.ds(s, 1)], min_val=0, max_val=NE - 1)

        def turn_x(s, par, half):
            pe.wait_ge(x_slot_in[par], 16 * (half + 1))
            least(pe, x_t_lo, 2 * s)
            for j in range(2):
                pe.transpose(psum[:, 0, P * j:P * j + P], x_slot[:, par, j, 0:P], ident)
                m = pe.transpose(psum[0:TAIL, 0, SLOT + P * j:SLOT + P * j + P], x_slot[:, par, j, P:EMB], ident)
            m.then_inc(x_turned, 1)

        def h(s):
            pe.wait_ge(w1_by_act, 2 * s + 2)
            pe.wait_ge(w1_by_dve, 2 * s + 2)
            pe.wait_ge(x_t_hi, 3 * s + 3)
            pe.wait_ge(x_t_lo, 2 * s + 2)
            for b in range(HK // 2):
                least(pe, *((h_by_dve, s) if b == 1 else (h_by_act, 2 * s - 1 + b // 2)))
                for i in range(2):
                    c = 2 * b + i
                    m = product(pe, h_pair(b)[:, SLOT * i:SLOT * i + SLOT], ws1.weights(slice(P * c, P * c + P)), x3_t.activations(slice(0, SLOT)))
                m.then_inc(h_done, 1)

        def y(s, par, e):
            pe.wait_ge(h_by_act, 2 * s + 2)
            pe.wait_ge(h_by_dve, s + 1)
            for j in range(2):
                least(pe, y_plain_ready, 2 * s + j - 1)
                for c in range(HK):
                    m = pe.matmul(psum[:, 5 + j, 0:EMB], h_t[:, par, c, P * j:P * j + P],
                                  w2[:, bass.ds(e, 1), c, :].rearrange("p a n -> p (a n)"), start=(c == 0), stop=(c == HK - 1))
                m.then_inc(y_done, 1)

        def step(s, par, half):
            before = expert(s - 1)
            h(s)
            turn_x(s + 1, 1 - par, half + par)
            y(s - 1, 1 - par, before)

        turn_x(0, 0, 0)
        h(0)
        turn_x(1, 1, 0)
        pe.wait_ge(w2_in, 16 * NE)
        pe.wait_ge(table_ready, 1)
        slots(pe, step)
        y(SLOTS - 1, 0, expert(SLOTS - 1))

    @block.vector
    def _(dve):
        steps = [0]

        def link(ins):
            steps[0] += 1
            ins.then_inc(route_step, 1)
            dve.wait_ge(route_step, steps[0])

        def by_token(x):
            return x.unsqueeze(1).broadcast_to([P, NT, NE])

        def by_expert(x):
            return x.unsqueeze(2).broadcast_to([P, NT, NE])

        def x_lo_out(h):
            dve.wait_ge(x_hi, 3 * h + 3)
            least(dve, hs_done, HK * h)
            dve.tensor_tensor(x3_t.lo[:], x3_in[:, 0, :], x3_t.hi[:].bitcast(F32), ALU.subtract).then_inc(x_lo, 1)
            dve.tensor_tensor(x3_t.both[TAIL:P], x3_in[0:TAIL, 1, :], x3_t.both[0:TAIL].bitcast(F32), ALU.subtract).then_inc(x_lo, 1)

        def hs_lo_out(h, half):
            least(dve, ys_done, HS * h)
            for c in range(HK):
                dve.wait_ge(hs_hi_ready, HK * h + c + 1)
                dve.scalar_tensor_tensor(hs_lo[:, c, :], psum[:, hs_bank(half, c), 0:HT], 0.0, hs_hi[:, c, :].bitcast(F32), ALU.max, ALU.subtract)\
                   .then_inc(hs_lo_ready, 1)

        def ys_out(h, half):
            dve.wait_ge(h2_loaded, 16 * (h + 1))
            dve.tensor_tensor(h2_in, h2_in, bs2[:].unsqueeze(1).broadcast_to([P, HS, EMB]), ALU.add).then_inc(h2_plus, 1)
            dve.wait_ge(h2_plus, h + 1)
            least(dve, out_stored, 16 * h)
            for s in range(HS):
                dve.wait_ge(ys_done, HS * h + s + 1)
                dve.scalar_tensor_tensor(out_rows[:, s, :], psum[:, 3 + HS * half + s, 0:EMB], 0.1 * TOPK, h2_in[:, s, :], ALU.mult, ALU.add)\
                   .then_inc(shared_ready, 1)

        def w1_main_lo(e):
            dve.wait_ge(w1_hi, 3 * e + 1)
            dve.tensor_tensor(expert_part(w1.lo, e), w1_raw[0], expert_part(w1.hi, e).bitcast(F32), ALU.subtract).then_inc(w1_lo, 1)

        def w1_tail_lo(e):
            dve.wait_ge(w1_hi, 3 * e + 2)
            rest = expert_part(w1.rest, e)
            for rows_of in (slice(0, TAIL), slice(REST - 1, REST)):
                dve.tensor_tensor(rest[rows_of], w1_raw[2][rows_of], rest[rows_of].bitcast(F32), ALU.subtract).then_inc(w1_lo, 1)

        rest_of_weights(dve, ws1, ws1_raw, shared_hi, shared_lo)
        x_lo_out(0)
        dve.wait_ge(shared_in, SHARED_LOADS)
        dve.tensor_scalar(bs2[:], bs2[:], 0.1 * TOPK, None, ALU.mult).then_inc(bias_scaled, 1)
        dve.wait_ge(shared_hi, 4)
        dve.tensor_tensor(ws2_lo[:], ws2_raw, ws2_hi[:].bitcast(F32), ALU.subtract).then_inc(shared_lo, 1)
        hs_lo_out(0, 0)
        x_lo_out(1)
        for k in range(TOPK):
            link(dve.tensor_reduce(top[:, k, :], logits_all[:], AX.X, ALU.max))
            link(dve.tensor_tensor(place[:], logits_all[:], by_expert(top[:, k, :]), ALU.is_lt))
            link(dve.scalar_tensor_tensor(place[:], place[:], float(NE), by_token(experts_iota), ALU.mult, ALU.add))
            link(dve.tensor_reduce(at_expert[:], place[:], AX.X, ALU.min))
            link(dve.tensor_tensor(chosen[:, k], by_token(experts_iota), by_expert(at_expert[:]), ALU.is_equal))
            if k == 0:
                link(dve.scalar_tensor_tensor(logits_all[:], chosen[:, 0], -FAR, logits_all[:], ALU.mult, ALU.add))
        dve.tensor_tensor(gap[:], top[:, 1, :], top[:, 0, :], ALU.subtract).then_inc(gap_ready, 1)
        dve.tensor_tensor(mask[:], chosen[:, 0], chosen[:, 1], ALU.add).then_inc(mask_ready, 1)
        hs_lo_out(1, 1)
        dve.wait_ge(ranks_done, 1)
        ranks = psum[:, RANKS, 0:NT * NE].rearrange("p (t e) -> p t e", e=NE)
        totals = psum[:, RANKS, NT * NE:2 * NT * NE].rearrange("p (t e) -> p t e", e=NE)
        link(dve.tensor_copy(running[:, 0], totals))
        dve.tensor_tensor(place[:], ranks, running[:, 0], ALU.subtract).then_inc(ranks_read, 1)
        dve.wait_ge(bias_scaled, 1)
        ys_out(0, 0)
        x_lo_out(2)
        dve.wait_ge(gap_exp, 1)
        link(dve.tensor_scalar(gap[:], gate[:, 2, :], 1.0, None, ALU.add))
        link(dve.reciprocal(gate[:, 0, :], gap[:]))
        dve.tensor_tensor(gate[:, 1, :], gate[:, 2, :], gate[:, 0, :], ALU.mult).then_inc(gates_ready, 1)
        at = 0
        for hop in (1, 2, 4, 8, 16):
            link(dve.tensor_tensor(running[:, 1 - at, hop:], running[:, at, hop:], running[:, at, :NT - hop], ALU.add))
            link(dve.tensor_copy(running[:, 1 - at, :hop], running[:, at, :hop]))
            at = 1 - at
        ys_out(1, 1)
        w1_main_lo(0)
        hs_lo_out(2, 0)
        x_lo_out(3)
        link(dve.tensor_scalar(padded_i[:], running[:, at, NT - 1, :], float(SLOT - 1), None, ALU.add))
        link(dve.tensor_single_scalar(padded_i[:], padded_i[:], -SLOT, ALU.bitwise_and))
        link(dve.tensor_copy(padded[:], padded_i[:]))
        link(dve.tensor_copy(ends[:, 0], padded[:]))
        last = 0
        for hop in (1, 2, 4):
            link(dve.tensor_tensor(ends[:, 1 - last, hop:], ends[:, last, hop:], ends[:, last, :NE - hop], ALU.add))
            link(dve.tensor_copy(ends[:, 1 - last, :hop], ends[:, last, :hop]))
            last = 1 - last
        link(dve.tensor_tensor(starts[:], ends[:, last], padded[:], ALU.subtract))
        link(dve.tensor_tensor(place[:], place[:], running[:, at], ALU.add))
        link(dve.tensor_tensor(place[:], place[:], by_token(starts[:]), ALU.add))
        for k in range(TOPK):
            link(dve.tensor_tensor(running[:, 1 - at], chosen[:, k], place[:], ALU.mult))
            link(dve.tensor_reduce(rows_f[:, k, :], running[:, 1 - at], AX.X, ALU.add))
        dve.tensor_copy(rows[:], rows_f[:]).then_inc(rows_ready, 1)
        hs_lo_out(3, 1)
        ys_out(2, 0)
        x_lo_out(4)
        w1_tail_lo(0)
        w1_main_lo(1)
        ys_out(3, 1)

        def group(g, more):
            hs_lo_out(2 * g, 0)
            x_lo_out(2 * g + 1)
            w1_tail_lo(g - 1)
            ys_out(2 * g, 0)
            if not more:
                slot_experts()
            hs_lo_out(2 * g + 1, 1)
            if more:
                x_lo_out(2 * g + 2)
            w1_main_lo(g)
            if not more:
                w1_tail_lo(g)
            ys_out(2 * g + 1, 1)

        def slot_experts():
            link(dve.tensor_tensor(past[:], slot_starts[0:1].unsqueeze(2).broadcast_to([1, SLOTS + 1, NE]),
                                   ends[0:1, last].unsqueeze(1).broadcast_to([1, SLOTS + 1, NE]), ALU.is_ge))
            link(dve.tensor_reduce(slot_expert_f[:], past[:], AX.X, ALU.add))
            dve.tensor_scalar(slot_expert[:], slot_expert_f[:], float(NE - 1), None, ALU.min).then_inc(table_ready, 1)

        with dve.Fori(2, G - 1) as g:
            group(g, True)
        group(G - 1, False)

        def x_lo_of_slot(s):
            dve.wait_ge(x_t_hi, 3 * s + 3)
            least(dve, h_done, HK // 2 * s)
            dve.tensor_tensor(x3_t.lo[:], psum[:, 0, 0:SLOT], x3_t.hi[:].bitcast(F32), ALU.subtract).then_inc(x_t_lo, 1)
            dve.tensor_tensor(x3_t.both[TAIL:P], psum[0:TAIL, 0, SLOT:2 * SLOT], x3_t.both[0:TAIL].bitcast(F32), ALU.subtract).then_inc(x_t_lo, 1)

        def h_out(s, par):
            least(dve, y_done, 2 * s - 2)
            dve.wait_ge(h_done, HK // 2 * s + 2)
            dve.tensor_scalar(h_t[:, par, 2:4, :].rearrange("p c t -> p (c t)"), h_pair(1), 0.0, None, ALU.max).then_inc(h_by_dve, 1)

        def y_out(s):
            e = dve.value_load(slot_expert[0:1, bass.ds(s, 1)], min_val=0, max_val=NE - 1)
            for j in range(2):
                dve.wait_ge(y_done, 2 * s + j + 1)
                least(dve, y_ready, 2 * s + j - 1)
                dve.tensor_tensor(y_slot[:, j, 0, :], psum[:, 5 + j, 0:EMB],
                                  b2[:, bass.ds(e, 1), :].rearrange("p a n -> p (a n)"), ALU.add).then_inc(y_plain_ready, 1)

        def w1_out(s):
            e = dve.value_load(slot_expert[0:1, bass.ds(s, 1)], min_val=0, max_val=NE - 1)
            least(dve, h_done, HK // 2 * s)
            for now, w in ((ws1.lo, w1.lo), (ws1.rest, w1.rest)):
                dve.tensor_copy(now[:], w[:, bass.ds(HID * e, HID)]).then_inc(w1_by_dve, 1)

        def step(s, par, half):
            h_out(s, par)
            w1_out(s + 1)
            x_lo_of_slot(s + 1)
            y_out(s - 1)

        dve.wait_ge(table_ready, 1)
        dve.wait_ge(b2_in, 16)
        x_lo_of_slot(0)
        dve.wait_ge(hs_done, HK * HALVES)
        dve.wait_ge(w1_lo, 3 * NE)
        w1_out(0)
        dve.wait_ge(w1_hi, 3 * NE)
        h_out(0, 0)
        w1_out(1)
        x_lo_of_slot(1)
        dve.wait_ge(out_stored, 16 * HALVES)
        slots(dve, step)
        y_out(SLOTS - 1)


def lay_out(x):
    import numpy as np
    a = {k: np.asarray(v) for k, v in x.items()}

    def halves(w, bias=None):
        n = w.shape[1]
        t = np.zeros((HC + 1, 2, n), w.dtype)
        t[:HC] = w.reshape(2, HC, n).transpose(1, 0, 2)
        if bias is not None:
            t[HC, 0] = bias
        return t

    def packed(w, bias):
        t = np.zeros((P, 3, w.shape[1]), w.dtype)
        t[:, 0] = w[:P]
        t[:TAIL, 1] = t[TAIL:, 1] = t[:TAIL, 2] = w[P:]
        t[TAIL, 2] = t[REST - 1, 2] = bias
        return t

    def columns(v):
        return np.stack([v[:P], np.concatenate([v[P:], v[P:]])], 1)

    side = IMG // PATCH
    patches = a["x"].reshape(G, B // G, CH, side, PATCH, side, PATCH).transpose(0, 2, 4, 6, 1, 3, 5)
    patches = patches.reshape(G, KP, P, GT).transpose(0, 2, 1, 3)
    w_conv = a["L0_tok_conv_w"].reshape(EMB, KP, P).transpose(2, 1, 0)
    wq, wk, wv, wo = (a[f"L0_tok_w{c}"].T for c in "qkvo")
    bq, bk, bv, bo = (a[f"L0_tok_b{c}"] for c in "qkvo")
    w_qkv = packed(np.concatenate([wq, wk[:, P:], wk[:, :P], wv], 1), np.concatenate([bq, bk[P:], bk[:P], bv]))
    w_o = halves(wo.reshape(PAIRS, 2, HD, EMB).transpose(1, 0, 2, 3).reshape(EMB, EMB), bo)
    uv, uvb = a["L0_attn_uv_W"], a["L0_attn_uv_b"]
    swap = (np.arange(S_GAU) + S_GAU // 2) % S_GAU
    base_cols = 2 * E_GAU + swap
    w_uv = packed(np.concatenate([uv, uv[:, base_cols]], 1), np.concatenate([uvb, uvb[base_cols]]))
    ln_gamma = np.ones((P, 3), np.float32)
    ln_gamma[:, 0:2] = columns(a["L0_attn_ln_gamma"])
    ln_gamma[:TAIL, 2] = a["L0_attn_ln_gamma"][P:]
    ln_beta = np.zeros((P, 2, REST), np.float32)
    ln_beta[:, 0, [TAIL, REST - 1]] = a["L0_attn_ln_beta"][:P, None]
    ln_beta[:TAIL, 1, [TAIL, REST - 1]] = a["L0_attn_ln_beta"][P:, None]
    w_route = np.zeros((P, 2, NE), np.float32)
    w_route[:, 0] = a["L0_ffn_Wr"].T[:P]
    w_route[:TAIL, 1] = a["L0_ffn_Wr"].T[P:]
    gq, bqk = a["L0_attn_gamma_qk"], a["L0_attn_beta_qk"]
    pair_up = lambda v: np.stack([v.T, v[:, swap].T], 2)
    half = S_GAU // 2
    inv_freq = np.power(np.float32(10000.0), -np.arange(half, dtype=np.float32) / half).astype(np.float32)
    angle = (np.arange(L, dtype=np.float32)[None, :] * inv_freq[:, None]).astype(np.float32)
    cos, sin = np.cos(angle), np.sin(angle)
    rope = np.stack([np.concatenate([cos, cos]), np.concatenate([-sin, sin])], 1)
    m, n = np.meshgrid(np.arange(P), np.arange(P), indexing="ij")
    inside = (m // L) == (n // L)
    rel = a["L0_attn_w_rel"][np.where(inside, m - n + L - 1, 0)]
    rel_bias = np.where(inside, rel, np.float32(-1e30))
    head_mask = np.zeros((P, 2), np.float32)
    for h in range(2):
        head_mask[(np.arange(P) // HD) % 2 == h, h] = HD ** -0.5
    consts = np.concatenate([
        np.eye(P), np.triu(np.ones((P, P)), 1), np.tile(np.arange(NE), (P, 1)), np.tile(SLOT * np.arange(SLOTS + 1), (P, 1)),
    ], 1)
    pad_rows = np.zeros((SLOT, ROW), np.float32)
    pad_rows[:, EMB + 1] = T + np.arange(SLOT)
    token_ids = (np.arange(NT)[None, :] * P + np.arange(P)[:, None]).astype(np.float32)
    w1 = np.stack([packed(a["L0_ffn_W1"][e].T, a["L0_ffn_b1"][e]) for e in range(NE)])
    w2 = a["L0_ffn_W2"].transpose(0, 2, 1).reshape(NE, HK, P, EMB).transpose(2, 0, 1, 3)
    w = dict(
        patches=patches, w_conv=w_conv, b_conv=columns(a["L0_tok_conv_b"]), w_qkv=w_qkv, head_mask=head_mask,
        w_o=w_o, w_uv=w_uv, ln_gamma=ln_gamma, ln_beta=ln_beta,
        qk_gain=pair_up(gq), qk_shift=pair_up(bqk), rope=rope, rel_bias=rel_bias,
        w_gau=a["L0_attn_o_W"].reshape(EC, P, EMB).transpose(1, 0, 2), b_gau=a["L0_attn_o_b"][None],
        w_route=w_route, w1=w1, w2=w2, b2=a["L0_ffn_b2"].reshape(1, -1),
        ws1=packed(a["L0_ffn_sW1"].T, a["L0_ffn_sb1"]), ws2=a["L0_ffn_sW2"].T.reshape(HK, P, EMB).transpose(1, 0, 2),
        bs2=a["L0_ffn_sb2"][None], consts=consts.astype(np.float32), pad_rows=pad_rows, token_ids=token_ids,
    )
    return {k: np.ascontiguousarray(v) for k, v in w.items()}


def kernel(**inputs):
    import concourse.bacc as bacc
    from concourse.bass_utils import run_bass_kernel_spmd

    nc = bacc.Bacc("TRN2", target_bir_lowering=False, num_devices=1)
    build_program(nc, declare(nc))
    result = run_bass_kernel_spmd(nc, [lay_out(inputs)], core_ids=[0])
    return result.results[0]["out"][:T].reshape(B, L, EMB)
```
